# Optimizing a Trainium2 kernel written in Bass

```python
import numpy as np
import jax
import jax.numpy as jnp

def _softmax(x, axis=-1):
    return jax.nn.softmax(x, axis=axis)

def _gelu(x):
    return jax.nn.gelu(x, approximate=True)

def _silu(x):
    return jax.nn.silu(x)

def _sigmoid(x):
    return jax.nn.sigmoid(x)

def _layernorm(x, axis=-1, eps=1e-05):
    m = jnp.mean(x, axis=axis, keepdims=True)
    v = jnp.var(x, axis=axis, keepdims=True)
    return (x - m) / jnp.sqrt(v + eps)

def _scatter_add(tgt, idx, src, axis=0):
    return tgt.at[idx].add(src)

def _segment_sum(src, seg, n):
    return jax.ops.segment_sum(src, seg, n)
kernel_name = 'mk_gnn_ffn_d2_gnn_r8_93b615'

def setup_inputs(seed: int=0):
    np.random.seed(seed)
    _w = jnp.asarray

    def _rec_inputs():
        import jax
        import jax.numpy as jnp
        _gk = jax.random.key(seed)
        x = -0.0003713 + 1 * jax.random.normal(jax.random.fold_in(_gk, 1), (12500, 256), jnp.float32)
        _s = jax.random.randint(jax.random.fold_in(_gk, 2), (100000,), 0, 12500, jnp.int32)
        _d = jax.random.randint(jax.random.fold_in(_gk, 3), (100000,), 0, 12500, jnp.int32)
        _loop = jnp.arange(12500, dtype=jnp.int32)
        src = jnp.concatenate([_s, _d, _loop])
        dst = jnp.concatenate([_d, _s, _loop])
        _o = jnp.argsort(dst, stable=True)
        src = src[_o]
        dst = dst[_o]
        edge_attr3_1x1 = jax.random.uniform(jax.random.fold_in(_gk, 12), (212500, 1, 1), jnp.float32, 0.0, 0.999998)
        return (x, src, dst, edge_attr3_1x1)
    x, src, dst, edge_attr3_1x1 = _rec_inputs()

    def _L0_gnn_setup():
        import jax, jax.numpy as jnp
        import numpy as np
        N = 6250
        E = 100000
        HID = 256
        HEADS = 8
        HEAD_DIM = HID // HEADS
        EPS = 1e-05
        key = jax.random.key(seed)
        ks = jax.random.split(key, 8)
        scale = 1.0 / np.sqrt(HID)
        return {'x': jax.random.normal(ks[0], (N, HID), dtype=jnp.float32), 'WQ': jax.random.normal(ks[1], (HID, HID), dtype=jnp.float32) * scale, 'WK': jax.random.normal(ks[2], (HID, HID), dtype=jnp.float32) * scale, 'WV': jax.random.normal(ks[3], (HID, HID), dtype=jnp.float32) * scale, 'W_out': jax.random.normal(ks[4], (HID, HID), dtype=jnp.float32) * scale, 'b_out': jnp.zeros((HID,), dtype=jnp.float32), 'gn_weight': jnp.ones((HID,), dtype=jnp.float32), 'gn_bias': jnp.zeros((HID,), dtype=jnp.float32), 'gn_mean_scale': jnp.ones((HID,), dtype=jnp.float32), 'edge_index': jax.random.randint(ks[5], (2, E), 0, N, dtype=jnp.int32)}
    _L0_gnn_all = _L0_gnn_setup()
    _L0_gnn_in = {k: v for k, v in _L0_gnn_all.items() if k in ('WQ', 'WK', 'WV', 'W_out', 'b_out', 'gn_weight', 'gn_bias', 'gn_mean_scale')}
    del _L0_gnn_all

    def _L0_ffn_setup():
        import jax, jax.numpy as jnp
        import numpy as np
        NUM_EXPERTS = 8
        TOP_K = 2
        B, S, D = (8, 1024, 256)

        def _moe(tokens, router_w, w1, b1, w2, b2):
            N = tokens.shape[0]
            E = router_w.shape[0]
            logits = tokens.astype(jnp.float32) @ router_w.astype(jnp.float32).T
            probs = jax.nn.softmax(logits, axis=-1)
            rw, re = jax.lax.top_k(probs, TOP_K)
            if TOP_K > 1:
                rw = rw / jnp.maximum(rw.sum(-1, keepdims=True), 1e-12)
            rw = rw.astype(tokens.dtype)
            combine = jnp.zeros((N, E), tokens.dtype).at[jnp.arange(N)[:, None], re].set(rw)
            out = tokens
            for e in range(E):
                h = jax.nn.gelu(tokens @ w1[e] + b1[e], approximate=False)
                y = h @ w2[e] + b2[e]
                out = out + combine[:, e:e + 1] * y
            return out
        key = jax.random.key(seed)
        ks = jax.random.split(key, 4)
        scale = 1.0 / np.sqrt(D).astype(np.float32)
        return {'input_embeddings': jax.random.normal(ks[0], (B, S, D), jnp.float32), 'router_w': jax.random.normal(ks[1], (NUM_EXPERTS, D), jnp.float32) * scale, 'w1': jax.random.normal(ks[2], (NUM_EXPERTS, D, D), jnp.float32) * scale, 'b1': jnp.zeros((NUM_EXPERTS, D), jnp.float32), 'w2': jax.random.normal(ks[3], (NUM_EXPERTS, D, D), jnp.float32) * scale, 'b2': jnp.zeros((NUM_EXPERTS, D), jnp.float32)}
    _L0_ffn_all = _L0_ffn_setup()
    _L0_ffn_in = {k: v for k, v in _L0_ffn_all.items() if k in ('router_w', 'w1', 'b1', 'w2', 'b2')}
    del _L0_ffn_all

    def _L1_gnn_setup():
        import jax, jax.numpy as jnp
        import numpy as np
        N, F_IN, H, OUT, E = (4000, 256, 4, 64, 64000)
        NEG_SLOPE = 0.2
        key = jax.random.key(seed)
        ks = jax.random.split(key, 7)
        return {'feat': jax.random.normal(ks[0], (N, F_IN), dtype=jnp.float32), 'dist': jax.random.uniform(ks[1], (E, 1, 1), dtype=jnp.float32), 'W': jax.random.normal(ks[2], (F_IN, H * OUT), dtype=jnp.float32) * (1.0 / np.sqrt(F_IN)), 'w_att_src': jax.random.normal(ks[3], (1, H, OUT), dtype=jnp.float32) * 0.1, 'w_att_dst': jax.random.normal(ks[4], (1, H, OUT), dtype=jnp.float32) * 0.1, 'src': jax.random.randint(ks[5], (E,), 0, N, dtype=jnp.int32), 'dst': jax.random.randint(ks[6], (E,), 0, N, dtype=jnp.int32)}
    _L1_gnn_all = _L1_gnn_setup()
    _L1_gnn_in = {k: v for k, v in _L1_gnn_all.items() if k in ('W', 'w_att_src', 'w_att_dst')}
    del _L1_gnn_all

    def _L1_ffn_setup():
        import math
        import jax, jax.numpy as jnp
        import numpy as np
        CAPACITY_FACTOR = 1.25
        key = jax.random.key(seed)
        ks = jax.random.split(key, 5)
        B, L, D, F, E = (8, 1024, 256, 1024, 8)
        h = jax.random.normal(ks[0], (B, L, D), dtype=jnp.float32)
        gate_w = jax.random.normal(ks[1], (D, E), dtype=jnp.float32) * 0.02
        gate_b = jnp.zeros((E,), dtype=jnp.float32)
        w1 = jax.random.normal(ks[2], (E, D, F), dtype=jnp.float32) * (1.0 / math.sqrt(D))
        b1 = jnp.zeros((E, F), dtype=jnp.float32)
        w2 = jax.random.normal(ks[3], (E, F, D), dtype=jnp.float32) * (1.0 / math.sqrt(F))
        b2 = jnp.zeros((E, D), dtype=jnp.float32)
        return {'h': h, 'gate_w': gate_w, 'gate_b': gate_b, 'w1': w1, 'b1': b1, 'w2': w2, 'b2': b2}
    _L1_ffn_all = _L1_ffn_setup()
    _L1_ffn_in = {k: v for k, v in _L1_ffn_all.items() if k in ('gate_w', 'gate_b', 'w1', 'b1', 'w2', 'b2')}
    del _L1_ffn_all
    return {'x': x, 'src': src, 'dst': dst, 'edge_attr3_1x1': edge_attr3_1x1, 'L0_gnn_WQ': _L0_gnn_in['WQ'], 'L0_gnn_WK': _L0_gnn_in['WK'], 'L0_gnn_WV': _L0_gnn_in['WV'], 'L0_gnn_W_out': _L0_gnn_in['W_out'], 'L0_gnn_b_out': _L0_gnn_in['b_out'], 'L0_gnn_gn_weight': _L0_gnn_in['gn_weight'], 'L0_gnn_gn_bias': _L0_gnn_in['gn_bias'], 'L0_gnn_gn_mean_scale': _L0_gnn_in['gn_mean_scale'], 'L0_ffn_router_w': _L0_ffn_in['router_w'], 'L0_ffn_w1': _L0_ffn_in['w1'], 'L0_ffn_b1': _L0_ffn_in['b1'], 'L0_ffn_w2': _L0_ffn_in['w2'], 'L0_ffn_b2': _L0_ffn_in['b2'], 'L1_gnn_W': _L1_gnn_in['W'], 'L1_gnn_w_att_src': _L1_gnn_in['w_att_src'], 'L1_gnn_w_att_dst': _L1_gnn_in['w_att_dst'], 'L1_ffn_gate_w': _L1_ffn_in['gate_w'], 'L1_ffn_gate_b': _L1_ffn_in['gate_b'], 'L1_ffn_w1': _L1_ffn_in['w1'], 'L1_ffn_b1': _L1_ffn_in['b1'], 'L1_ffn_w2': _L1_ffn_in['w2'], 'L1_ffn_b2': _L1_ffn_in['b2']}

def reference(x, src, dst, edge_attr3_1x1, L0_gnn_WQ, L0_gnn_WK, L0_gnn_WV, L0_gnn_W_out, L0_gnn_b_out, L0_gnn_gn_weight, L0_gnn_gn_bias, L0_gnn_gn_mean_scale, L0_ffn_router_w, L0_ffn_w1, L0_ffn_b1, L0_ffn_w2, L0_ffn_b2, L1_gnn_W, L1_gnn_w_att_src, L1_gnn_w_att_dst, L1_ffn_gate_w, L1_ffn_gate_b, L1_ffn_w1, L1_ffn_b1, L1_ffn_w2, L1_ffn_b2):
    import jax
    import jax.numpy as jnp

    def _L0_gnn_ref(x, WQ, WK, WV, W_out, b_out, gn_weight, gn_bias, gn_mean_scale, edge_index):
        import jax, jax.numpy as jnp
        import numpy as np
        N = 6250
        E = 100000
        HID = 256
        HEADS = 8
        HEAD_DIM = HID // HEADS
        EPS = 1e-05
        n = x.shape[0]
        src = edge_index[0]
        dst = edge_index[1]
        q = (x @ WQ).reshape(n, HEADS, HEAD_DIM)
        k = (x @ WK).reshape(n, HEADS, HEAD_DIM)
        v = (x @ WV).reshape(n, HEADS, HEAD_DIM)
        score = jnp.einsum('ehd,ehd->eh', q[dst], k[src]) / jnp.sqrt(jnp.asarray(HEAD_DIM, x.dtype))
        m = jax.ops.segment_max(score, dst, num_segments=n)
        ex = jnp.exp(score - m[dst])
        denom = jax.ops.segment_sum(ex, dst, num_segments=n)
        alpha = ex / denom[dst]
        msg = alpha[..., None] * v[src]
        out = jax.ops.segment_sum(msg, dst, num_segments=n).reshape(n, HID)
        out = out @ W_out + b_out
        h = out + x
        mean = h.mean(axis=0)
        o = h - gn_mean_scale * mean
        var = (o * o).mean(axis=0)
        o = o / jnp.sqrt(var + EPS) * gn_weight + gn_bias
        return jax.nn.gelu(o, approximate=False)

    def _L0_ffn_ref(input_embeddings, router_w, w1, b1, w2, b2):
        import jax, jax.numpy as jnp
        import numpy as np
        NUM_EXPERTS = 8
        TOP_K = 2
        B, S, D = (8, 1024, 256)

        def _moe(tokens, router_w, w1, b1, w2, b2):
            N = tokens.shape[0]
            E = router_w.shape[0]
            logits = tokens.astype(jnp.float32) @ router_w.astype(jnp.float32).T
            probs = jax.nn.softmax(logits, axis=-1)
            rw, re = jax.lax.top_k(probs, TOP_K)
            if TOP_K > 1:
                rw = rw / jnp.maximum(rw.sum(-1, keepdims=True), 1e-12)
            rw = rw.astype(tokens.dtype)
            combine = jnp.zeros((N, E), tokens.dtype).at[jnp.arange(N)[:, None], re].set(rw)
            out = tokens
            for e in range(E):
                h = jax.nn.gelu(tokens @ w1[e] + b1[e], approximate=False)
                y = h @ w2[e] + b2[e]
                out = out + combine[:, e:e + 1] * y
            return out
        b, s, d = input_embeddings.shape
        tokens = input_embeddings.reshape(b * s, d)
        return _moe(tokens, router_w, w1, b1, w2, b2).reshape(b, s, d)

    def _L1_gnn_ref(feat, dist, W, w_att_src, w_att_dst, src, dst):
        import jax, jax.numpy as jnp
        import numpy as np
        N, F_IN, H, OUT, E = (4000, 256, 4, 64, 64000)
        NEG_SLOPE = 0.2
        n = feat.shape[0]
        ft = (feat @ W).reshape(n, H, OUT)
        e_src = jnp.sum(ft * w_att_src, axis=-1, keepdims=True)
        e_dst = jnp.sum(ft * w_att_dst, axis=-1, keepdims=True)
        e = e_src[src] + e_dst[dst]
        e = jnp.where(e >= 0, e, NEG_SLOPE * e)
        emax = jax.ops.segment_max(e, dst, num_segments=n)
        ex = jnp.exp(e - emax[dst])
        denom = jax.ops.segment_sum(ex, dst, num_segments=n)
        a = ex / denom[dst] * dist
        m = ft[src] * a
        out = jax.ops.segment_sum(m, dst, num_segments=n)
        return out.reshape(n, H * OUT)

    def _L1_ffn_ref(h, gate_w, gate_b, w1, b1, w2, b2):
        import math
        import jax, jax.numpy as jnp
        import numpy as np
        CAPACITY_FACTOR = 1.25
        B, L, D = h.shape
        E = gate_w.shape[1]
        T = B * L
        C = max(1, math.ceil(CAPACITY_FACTOR * T / E))
        x = h.reshape(T, D)
        logits = x @ gate_w + gate_b
        probs = jax.nn.softmax(logits, axis=-1)
        idx = jnp.argmax(probs, axis=-1)
        prb = jnp.take_along_axis(probs, idx[:, None], axis=1)[:, 0]
        one_hot = jax.nn.one_hot(idx, E, dtype=jnp.float32)
        pos = (jnp.cumsum(one_hot, axis=0) * one_hot).sum(-1).astype(jnp.int32) - 1
        kept = pos < C
        pos_safe = jnp.where(kept, pos, C)
        buf = jnp.zeros((E, C, D), dtype=h.dtype).at[idx, pos_safe].set(x, mode='drop')
        hmid = jax.nn.relu(jnp.einsum('ecd,edf->ecf', buf, w1) + b1[:, None, :])
        ybuf = jnp.einsum('ecf,efd->ecd', hmid, w2) + b2[:, None, :]
        pos_g = jnp.minimum(pos, C - 1)
        y_tok = ybuf[idx, pos_g] * (prb * kept)[:, None]
        y = y_tok.reshape(B, L, D)
        y = jnp.nan_to_num(y, nan=0.0, posinf=10000.0, neginf=-10000.0)
        return y
    edge_index = jnp.stack([src, dst])
    x = x + _L0_gnn_ref(_layernorm(x, axis=-1), L0_gnn_WQ, L0_gnn_WK, L0_gnn_WV, L0_gnn_W_out, L0_gnn_b_out, L0_gnn_gn_weight, L0_gnn_gn_bias, L0_gnn_gn_mean_scale, edge_index)
    x = x + _L0_ffn_ref(_layernorm(x, axis=-1)[None], L0_ffn_router_w, L0_ffn_w1, L0_ffn_b1, L0_ffn_w2, L0_ffn_b2)[0]
    x = x + _L1_gnn_ref(_layernorm(x, axis=-1), edge_attr3_1x1, L1_gnn_W, L1_gnn_w_att_src, L1_gnn_w_att_dst, src, dst)
    x = x + _L1_ffn_ref(_layernorm(x, axis=-1)[None], L1_ffn_gate_w, L1_ffn_gate_b, L1_ffn_w1, L1_ffn_b1, L1_ffn_w2, L1_ffn_b2)[0]
    return x

_drawn_inputs = setup_inputs


def setup_inputs(seed=0):
    import zlib

    import numpy as np

    out = dict(_drawn_inputs(seed))
    spreads = {'L0_gnn_b_out': (0.0, 0.476),
     'L0_gnn_gn_weight': (1.0, 0.2),
     'L0_gnn_gn_bias': (0.0, 0.1),
     'L0_gnn_gn_mean_scale': (1.0, 0.6),
     'L0_ffn_b1': (0.0, 0.378),
     'L0_ffn_b2': (0.0, 0.1),
     'L1_ffn_gate_b': (0.0, 0.283),
     'L1_ffn_b1': (0.0, 0.8),
     'L1_ffn_b2': (0.0, 0.8)}
    factors = {'L1_gnn_w_att_dst': 4.538}
    for name, (base, spread) in spreads.items():
        noise = np.random.default_rng([zlib.crc32(name.encode()), seed]).standard_normal(out[name].shape)
        drawn = base * np.exp(spread * noise) if base else spread * noise
        out[name] = jnp.asarray(drawn.astype(out[name].dtype))
    for name, factor in factors.items():
        out[name] = (out[name] * factor).astype(out[name].dtype)
    return out
```

```python
from contextlib import ExitStack

import numpy as np
import concourse.bass as bass
from concourse import mybir
from concourse.bass import IndirectOffsetOnAxis

ALU = mybir.AluOpType
ACT = mybir.ActivationFunctionType
AX = mybir.AxisListType
F32 = mybir.dt.float32
I32 = mybir.dt.int32
U32 = mybir.dt.uint32
BF16 = mybir.dt.bfloat16
SP_ENG, ACT_ENG, DVE_ENG = mybir.EngineType.SP, mybir.EngineType.Activation, mybir.EngineType.DVE

P = 128
N = 12500
D = 256
E = 212500
EPS = 1e-5
NB = 100
NR = NB * P
G = 16
NG = 105
NT = NG * G
NE = NT * P
TB = 120
MW = 132
BIG = 1e30
assert NT % TB == 0 and NE > E and NR >= N + P and E > (NT - 8) * P - 8 * P * G


class Step:

    def __init__(self, eng, sem, base=0):
        self.eng, self.sem, self.base, self.n = eng, sem, base, 0

    def __call__(self, ins):
        ins.then_inc(self.sem, 1)
        self.n += 1
        self.eng.wait_ge(self.sem, self.base + self.n)


class Scope(ExitStack):

    def __init__(self, nc, tag):
        super().__init__()
        self.nc, self.tag = nc, tag

    def sb(self, name, shape, dt=F32):
        return self.enter_context(self.nc.sbuf_tensor(f"{self.tag}_{name}", shape, dt))

    def ps(self, name, shape, dt=F32):
        return self.enter_context(self.nc.psum_tensor(f"{self.tag}_{name}", shape, dt))


def sems(nc, tag, *names):
    return [nc.alloc_semaphore(name=f"{tag}_{n}") for n in names]



def prepare_edges(nc, ident, x, src, dst, dist, dr):
    s_fill, s_pad, s_nat, s_free, s_dve, s_turn, s_out, s_st = sems(
        nc, "prep", "filled", "padded", "loaded", "read", "dve", "turned", "copied", "stored")
    NP_ = NE - E
    with Scope(nc, "prep") as m:
        zero = m.sb("zero", [P, (NR - N) * D // 100])
        tail = m.sb("tail", [1, 3, NP_], I32)
        ftail = m.sb("ftail", [1, NP_])
        spare = m.sb("spare", [P, G], I32)
        nat = m.sb("nat", [P, 3, P], I32)
        natd = m.sb("natd", [P, P])
        f = m.sb("f", [P, 3, P])
        rel = m.sb("rel", [P, P])
        cont = m.sb("cont", [P, P])
        mask = m.sb("mask", [P, MW])
        tsrc = m.sb("tsrc", [P, P], I32)
        trel = m.sb("trel", [P, P])
        tdist = m.sb("tdist", [P, P])
        pt = m.ps("pt", [P, 3, P])
        with nc.Block() as block:

            @block.sync
            def _(sp):
                sp.dma_start(dr["x"][0:N, :], x).then_inc(s_pad, 16)
                sp.dma_start(dr["src"][0:1, 0:E], src.rearrange("(a e) -> a e", a=1)).then_inc(s_pad, 16)
                sp.dma_start(dr["dst"][0:1, 1:E + 1], dst.rearrange("(a e) -> a e", a=1)).then_inc(s_pad, 16)
                sp.dma_start(dr["dist"][0:1, 0:E], dist.rearrange("e a b -> (a b) e")).then_inc(s_pad, 16)
                sp.wait_ge(s_fill, 7)
                sp.dma_start(dr["x"][N:NR, :].rearrange("(p r) d -> p (r d)", p=100),
                             zero[0:100, :]).then_inc(s_pad, 16)
                sp.dma_start(dr["src"][0:1, E:NE], tail[:, 0, :]).then_inc(s_pad, 16)
                sp.dma_start(dr["dst"][0:1, E + 1:NE + 1], tail[:, 1, :]).then_inc(s_pad, 16)
                sp.dma_start(dr["dst"][0:1, 0:1], tail[:, 2, 0:1]).then_inc(s_pad, 16)
                sp.dma_start(dr["dist"][0:1, E:NE], ftail[:, :]).then_inc(s_pad, 16)
                sp.dma_start(dr["srcT"][:, NT:NT + G], spare[:, :]).then_inc(s_pad, 16)
                sp.dma_start(dr["relT"][:, NT:NT + G], zero[:, 0:G]).then_inc(s_pad, 16)
                sp.wait_ge(s_pad, 11 * 16)
                with sp.Fori(0, NT // TB) as b:
                    sp.wait_ge(s_free, b + 1)
                    e0 = b * (TB * P)
                    for i, (name, off) in enumerate((("src", 0), ("dst", 1), ("dst", 0))):
                        sp.dma_start(nat[0:TB, i, :], dr[name][0:1, bass.ds(e0 + off, TB * P)].rearrange(
                            "a (t e) -> (a t) e", e=P)).then_inc(s_nat, 16)
                    sp.dma_start(natd[0:TB, :], dr["dist"][0:1, bass.ds(e0, TB * P)].rearrange(
                        "a (t e) -> (a t) e", e=P)).then_inc(s_nat, 16)
                    sp.wait_ge(s_out, b + 1)
                    c = bass.ds(b * TB, TB)
                    sp.dma_start(dr["mask"][c, :], mask[0:TB, :]).then_inc(s_st, 16)
                    sp.dma_start(dr["d0"][c, :], nat[0:TB, 1, 0:1]).then_inc(s_st, 16)
                    sp.dma_start(dr["srcT"][:, c], tsrc[:, 0:TB]).then_inc(s_st, 16)
                    sp.dma_start(dr["relT"][:, c], trel[:, 0:TB]).then_inc(s_st, 16)
                    sp.dma_start(dr["distT"][:, c], tdist[:, 0:TB]).then_inc(s_st, 16)

            @block.vector
            def _(v):
                v.memset(zero[:, :], 0.0).then_inc(s_fill, 1)
                v.memset(tail[:, 0, :], 0).then_inc(s_fill, 1)
                v.memset(tail[:, 1, :], N).then_inc(s_fill, 1)
                v.memset(tail[:, 2, :], -1).then_inc(s_fill, 1)
                v.memset(ftail[:, :], 0.0).then_inc(s_fill, 1)
                v.memset(spare[:, :], 0).then_inc(s_fill, 1)
                v.memset(mask[:, :], 1.0).then_inc(s_fill, 1)
                v.wait_ge(s_fill, 7)
                v.sem_inc(s_free, 1)
                with v.Fori(0, NT // TB) as b:
                    own = Step(v, s_dve, b * 5)
                    v.wait_ge(s_nat, b * 64 + 64)
                    own(v.tensor_copy(f[0:TB, :, :], nat[0:TB, :, :]))
                    own(v.tensor_scalar(rel[0:TB, :], f[0:TB, 1, :], f[0:TB, 1, 0:1], None, ALU.subtract))
                    own(v.tensor_tensor(cont[0:TB, :], f[0:TB, 1, :], f[0:TB, 2, :], ALU.is_equal))
                    v.wait_ge(s_st, b * 80 + 16)
                    own(v.tensor_copy(mask[0:TB, 1:P], cont[0:TB, 1:P]))
                    v.tensor_copy(mask[0:TB, 129:130], cont[0:TB, 0:1])
                    own(v.scalar_tensor_tensor(mask[0:TB, 130:131], rel[0:TB, 127:128], 0.0, cont[0:TB, 0:1],
                                               ALU.is_equal, ALU.mult))
                    v.wait_ge(s_turn, b + 1)
                    v.tensor_copy(tsrc[:, 0:TB], pt[:, 0, 0:TB])
                    v.tensor_copy(trel[:, 0:TB], pt[:, 1, 0:TB])
                    v.tensor_copy(tdist[:, 0:TB], pt[:, 2, 0:TB]).then_inc(s_out, 1)
                    v.wait_ge(s_st, b * 80 + 96)
                    v.sem_inc(s_free, 1)

            @block.scalar
            def _(act):
                act.wait_ge(s_fill, 7)
                act.sem_inc(s_st, 16)

            @block.tensor
            def _(pe):
                with pe.Fori(0, NT // TB) as b:
                    pe.wait_ge(s_dve, b * 5 + 2)
                    pe.transpose(pt[:, 0, 0:TB], f[0:TB, 0, :], ident[0:TB, 0:TB])
                    pe.transpose(pt[:, 1, 0:TB], rel[0:TB, :], ident[0:TB, 0:TB])
                    pe.transpose(pt[:, 2, 0:TB], natd[0:TB, :], ident[0:TB, 0:TB]).then_inc(s_turn, 1)


def node_tables(nc, ident, tag, src_rows, weights, NC, outs, xT_out=None, attention=None, ln_out=None):
    (s_w, s_c, s_x0, s_x1, s_bn, s_sd, s_ln, s_tp, s_xt, s_mm, s_evd, s_eva, s_st0, s_st1, s_own, s_att, s_go) = sems(
        nc, tag, "weights", "consts", "rows0", "rows1", "stats", "std", "normed", "turned", "xT", "product",
        "copied_dve", "copied_act", "stored0", "stored1", "dve", "att", "go")
    s_x, s_st = (s_x0, s_x1), (s_st0, s_st1)
    nst = len(outs) + (xT_out is not None) + (ln_out is not None)
    split = 384 if NC > 512 else NC // 2
    with Scope(nc, tag) as m:
        w = m.sb("w", [P, 2, NC])
        xin = m.sb("xin", [P, 2, D])
        st = m.sb("st", [P, 2, 6])
        mv = m.sb("mv", [P, 2, 2])
        sd = m.sb("sd", [P, 2, 2])
        eps = m.sb("eps", [P, 1])
        xln = m.sb("xln", [P, 2, D])
        xT = m.sb("xT", [P, 2, 2, P])
        row = m.sb("row", [P, 2, NC])
        att = m.sb("att", [P, 2, D])
        prod = m.sb("prod", [P, 2, D])
        pT = m.ps("pT", [P, 2, 512])
        pq = m.ps("pq", [P, 2, 1024])
        halves = [(0, min(512, NC))] + ([(512, NC)] if NC > 512 else [])
        with nc.Block() as block:

            @block.sync
            def _(sp):
                for i, (c0, ap) in enumerate(weights):
                    sp.dma_start(w[:, :, c0:c0 + ap.shape[1]], ap.rearrange("(c p) n -> p c n", p=P)).then_inc(s_w, 16)
                if attention:
                    for i in range(2):
                        sp.dma_start(att[:, i, :], attention[i].rearrange("a h o -> a (h o)").to_broadcast(
                            [P, D])).then_inc(s_w, 16)

                def store(b, s):
                    rows = bass.ds(b * P, P)
                    if xT_out is not None:
                        sp.wait_ge(s_xt, b + 1)
                    sp.wait_ge(s_evd, b + 1)
                    sp.wait_ge(s_eva, b + 1)
                    for ap, o0, c0, n in outs:
                        sp.dma_start(ap[rows, o0:o0 + n], row[:, s, c0:c0 + n]).then_inc(s_st[s], 16)
                    if xT_out is not None:
                        sp.dma_start(xT_out[:, :, rows], xT[:, s, :, :]).then_inc(s_st[s], 16)
                    if ln_out is not None:
                        sp.dma_start(ln_out[rows, :], xln[:, s, :]).then_inc(s_st[s], 16)

                for s in range(2):
                    sp.dma_start(xin[:, s, :], src_rows[s * P:s * P + P, :]).then_inc(s_x[s], 16)
                with sp.Fori(0, NB // 2 - 1) as i:
                    for s in range(2):
                        b = 2 * i + s
                        sp.wait_ge(s_ln, b + 1)
                        sp.dma_start(xin[:, s, :], src_rows[bass.ds(b * P + 2 * P, P), :]).then_inc(s_x[s], 16)
                        store(b, s)
                for s in range(2):
                    store(NB - 2 + s, s)
                for s in range(2):
                    sp.wait_ge(s_st[s], NB // 2 * nst * 16)

            @block.vector
            def _(v):
                v.memset(eps[:, :], EPS).then_inc(s_c, 1)
                if attention:
                    H = attention[0].shape[1]
                    v.wait_ge(s_w, 16 * (len(weights) + 2))
                    for a in range(2):
                        for c in range(2):
                            if a + c:
                                v.wait_ge(s_att, 2 * (2 * a + c))
                            v.tensor_tensor(prod[:, c, :], w[:, c, 0:D], att[:, a, :], ALU.mult).then_inc(s_att, 1)
                            v.wait_ge(s_att, 2 * (2 * a + c) + 1)
                            v.tensor_reduce(w[:, c, D + a * H:D + a * H + H],
                                            prod[:, c, :].rearrange("p (h o) -> p h o", h=H),
                                            AX.X, ALU.add).then_inc(s_att, 1)

                def body(i, s, first=False):
                    b = 2 * i + s
                    own = Step(v, s_own, b * 2)
                    v.wait_ge(s_x[s], i * 16 + 16)
                    own(v.bn_stats(st[:, s, :], xin[:, s, :]))
                    v.sem_inc(s_go, 1)
                    v.bn_aggr(mv[:, s, :], st[:, s, :]).then_inc(s_bn, 1)
                    if not first:
                        evac(b - 1, 1 - s, i - 1 + s)
                    v.wait_ge(s_sd, b + 1)
                    own(v.reciprocal(sd[:, s, 1:2], sd[:, s, 0:1]))
                    if ln_out is not None and not isinstance(i, int):
                        v.wait_ge(s_st[s], i * (nst * 16))
                    v.tensor_scalar(xln[:, s, :], xin[:, s, :], mv[:, s, 0:1], sd[:, s, 1:2],
                                    ALU.subtract, ALU.mult).then_inc(s_ln, 1)

                def evac(b, s, k):
                    v.wait_ge(s_mm, b + 1)
                    if not isinstance(k, int) or k > 0:
                        v.wait_ge(s_st[s], k * (nst * 16))
                    v.tensor_copy(row[:, s, 0:split], pq[:, s, 0:split]).then_inc(s_evd, 1)

                for s in range(2):
                    body(0, s, first=(s == 0))
                with v.Fori(1, NB // 2) as i:
                    for s in range(2):
                        body(i, s)
                evac(NB - 1, 1, NB // 2 - 1)

            @block.scalar
            def _(act):
                act.wait_ge(s_c, 1)

                def body(i, s):
                    b = 2 * i + s
                    act.wait_ge(s_bn, b + 1)
                    act.activation(sd[:, s, 0:1], mv[:, s, 1:2], ACT.Sqrt, bias=eps[:, 0:1]).then_inc(s_sd, 1)
                    act.wait_ge(s_tp, b + 1)
                    if not isinstance(i, int):
                        if xT_out is not None:
                            act.wait_ge(s_st[s], i * (nst * 16))
                        act.wait_ge(s_mm, b - 1)
                    act.copy(xT[:, s, :, :], pT[:, s, 0:D]).then_inc(s_xt, 1)
                    act.wait_ge(s_evd, b + 1)
                    if not isinstance(i, int):
                        act.wait_ge(s_st[s], i * (nst * 16))
                    act.copy(row[:, s, split:NC], pq[:, s, split:NC]).then_inc(s_eva, 1)

                for s in range(2):
                    body(0, s)
                with act.Fori(1, NB // 2) as i:
                    for s in range(2):
                        body(i, s)

            @block.tensor
            def _(pe):
                pe.wait_ge(s_w, 16 * (len(weights) + (2 if attention else 0)))
                if attention:
                    pe.wait_ge(s_att, 8)

                def body(i, s):
                    b = 2 * i + s
                    pe.wait_ge(s_ln, b + 1)
                    if not isinstance(i, int):
                        pe.wait_ge(s_xt, b - 1)
                    for c in range(2):
                        t = pe.transpose(pT[:, s, c * P:c * P + P], xln[:, s, c * P:c * P + P], ident[:, :])
                    t.then_inc(s_tp, 1)
                    pe.wait_ge(s_xt, b + 1)
                    if not isinstance(i, int):
                        pe.wait_ge(s_eva, b - 1)
                    for h0, h1 in halves:
                        for c in range(2):
                            t = pe.matmul(pq[:, s, h0:h1], xT[:, s, c, :], w[:, c, h0:h1],
                                          start=(c == 0), stop=(c == 1))
                    t.then_inc(s_mm, 1)

                for s in range(2):
                    body(0, s)
                with pe.Fori(1, NB // 2) as i:
                    for s in range(2):
                        body(i, s)


def edge_phase(nc, tag, c, dr, acc, H, scale, rows_t, dst_t, dist_t):
    gat = dist_t is not None
    RW, DW = rows_t.shape[1], dst_t.shape[1]
    Dh, HT, VW = D // H, H * G, (RW if gat else D)
    R, Q = 8, 4
    (s_d0, s_fl0, s_fl1, s_cl0, s_cl1, s_init, s_go) = sems(
        nc, tag, "firsts", "lists0", "lists1", "masks0", "masks1", "init", "go")
    s_fl, s_cl = (s_fl0, s_fl1), (s_cl0, s_cl1)
    s_g = sems(nc, tag, *[f"gathered{r}" for r in range(R)])
    s_q = sems(nc, tag, *[f"window{r}" for r in range(Q)])
    (s_S, s_turn, s_ST, s_qd, s_front, s_score, s_v, s_msg, s_agg, s_add, s_own, s_cp, s_ca, s_cd, s_cn, s_pgo) = sems(
        nc, tag, "onehot", "turned", "onehotT", "expanded", "front", "scores", "values", "messages",
        "summed", "added", "dve", "chain_pe", "chain_act", "chain_dve", "chain_own", "pe_go")
    CD, CN = (8, 15) if gat else (7, 14)
    NL = 2
    NC_ = 2 if gat else 1
    with Scope(nc, tag) as m:
        idx = m.sb("idx", [P, 2, G], I32)
        rel = m.sb("rel", [P, 2, G])
        mrow = m.sb("mrow", [G, 2, MW])
        dist = m.sb("dist", [P, 2, G]) if gat else None
        d0 = m.sb("d0", [1, NT], I32)
        S = m.sb("S", [P, 2, G, P])
        ST = m.sb("ST", [P, 2, P])
        vst = m.sb("vst", [P, 2, G, VW])
        kv = None if gat else m.sb("kv", [P, R, RW])
        win = m.sb("win", [P, Q, DW])
        prod = None if gat else m.sb("prod", [P, 2, D])
        score = m.sb("score", [P, 2, H, G])
        msg = m.sb("msg", [P, 2, D])
        alpha = m.sb("alpha", [P, 2, H, G])
        fac = m.sb("fac", [P, 2, 2, G])
        X = m.sb("X", [HT, P])
        X0 = m.sb("X0", [HT, P]) if gat else X
        M = m.sb("M", [HT, 131])
        NBm = m.sb("NB", [HT, 129])
        F = m.sb("F", [HT, P])
        B = m.sb("B", [HT, P])
        Y = m.sb("Y", [HT, 129])
        EX = m.sb("EX", [HT, 129])
        AL = m.sb("AL", [HT, P])
        Df = m.sb("Df", [HT, G])
        col = m.sb("col", [HT, 2])
        r3 = m.sb("r3", [1, 3, H, G])
        r2 = m.sb("r2", [1, 2, H, G])
        wn = m.sb("wn", [1, H, G + 1])
        Lx = m.sb("Lx", [1, H, G + 1])
        Rm = m.sb("Rm", [1, H, G + 1])
        wg = m.sb("wg", [1, H, G + 1])
        Ls = m.sb("Ls", [1, H, G + 1])
        Rs = m.sb("Rs", [1, H, G + 1])
        cn = m.sb("cn", [1, H, G])
        back_row = m.sb("brow", [1, H, G])
        pST = [m.ps(f"pST{i}", [P, 512]) for i in range(2)]
        pqd = [m.ps(f"pqd{i}", [P, 512]) for i in range(2)]
        pag = [m.ps(f"pag{i}", [P, 512]) for i in range(2)]
        cA = m.ps("cA", [P, 512])
        cB = m.ps("cB", [P, 512])
        flat = lambda t: t[:, :, :].rearrange("a h g -> a (h g)")

        def wait(eng, sem, value):
            if not isinstance(value, int) or value > 0:
                eng.wait_ge(sem, value)

        def run(eng, step):
            step(0, 0, 0, 0, True)
            with eng.Fori(0, (NG - 1) // 2) as it:
                step(2 * it + 1, 1, it, it, True)
                step(2 * it + 2, 0, it + 1, it, True)
            step(NG, NG % 2, 0, (NG - 1) // 2, False)

        with nc.Block() as block:

            @block.sync
            def _(sp):
                sp.dma_start(d0[:, :], dr["d0"].rearrange("t a -> a t")).then_inc(s_d0, 16)

                def lists(g, p):
                    t = bass.ds(g * G, G)
                    sp.dma_start(idx[:, p, :], dr["srcT"][:, t]).then_inc(s_fl[p], 16)
                    sp.dma_start(rel[:, p, :], dr["relT"][:, t]).then_inc(s_fl[p], 16)

                def masks(g, p):
                    t = bass.ds(g * G, G)
                    sp.dma_start(mrow[:, p, :], dr["mask"][t, :]).then_inc(s_cl[p], 16)
                    if gat:
                        sp.dma_start(dist[:, p, :], dist_t[:, t]).then_inc(s_cl[p], 16)

                lists(0, 0)
                sp.wait_ge(s_d0, 16)

                def step(g, k, u, ub, front):
                    if not front:
                        return
                    wait(sp, s_front, g * G)
                    lists(g + 1, 1 - k)
                    masks(g, k)
                    for q in range(0, G, 4):
                        _, first = nc.values_load_multi_w_load_instructions(
                            d0[0:1, bass.ds(g * G + q, 4)], engines=[SP_ENG], min_val=0, max_val=N)
                        for i in range(q, q + 4):
                            wait(sp, s_qd, g * G + i - Q + 1)
                            sp.dma_start(win[:, i % Q, :], dst_t[bass.ds(first[i - q], P), :]).then_inc(s_q[i % Q], 16)

                run(sp, step)
                sp.wait_ge(s_fl[1], 16 * NL * ((NG + 1) // 2))

            @block.gpsimd
            def _(pool):
                def step(g, k, u, ub, front):
                    if not front:
                        return
                    pool.wait_ge(s_fl[k], (u + 1) * (16 * NL))
                    for i in range(G):
                        wait(pool, s_front, g * G + i - R + 1)
                        if gat:
                            pool.wait_ge(s_msg, g * G + i + 1)
                            row = vst[:, k, i, :]
                        else:
                            wait(pool, s_v, g * G + i - R + 1)
                            row = kv[:, i % R, :]
                        pool.sem_inc(s_go, 1)
                        pool.indirect_dma_start(row, None, rows_t, IndirectOffsetOnAxis(
                            ap=idx[:, k, i:i + 1], axis=0)).then_inc(s_g[i % R], 16)

                run(pool, step)

            @block.tensor
            def _(pe):
                pe.wait_ge(s_init, 12)
                pe.sem_inc(s_agg, 2 * G)

                def step(g, k, u, ub, front):
                    b, h = 1 - k, g - 1
                    back = not isinstance(g, int) or g > 0

                    def chain(n):
                        if n == 0:
                            pe.wait_ge(s_score, h * G + G)
                            pe.wait_ge(s_cl[b], (ub + 1) * (16 * NC_))
                            pe.sem_inc(s_pgo, 1)
                            pe.transpose(cA[0:HT, 0:P], score[:, b, :, :].rearrange("p h g -> p (h g)"), c.ident[:, :])
                            pe.matmul(cA[0:HT, P:P + 131], c.rep[:, 0:HT], mrow[:, b, 0:131],
                                      start=True, stop=True).then_inc(s_cp, 1)
                        elif n == 1:
                            pe.wait_ge(s_cd, h * CD + 2)
                            pe.sem_inc(s_pgo, 1)
                            pe.matmul(cB[0:1, 0:HT], F[:, 127:128], c.ident[0:HT, 0:HT], start=True, stop=True)
                            for j in range(2):
                                t = pe.matmul(cB[0:1, HT + j * HT:2 * HT + j * HT], M[:, 129 + j:130 + j],
                                              c.ident[0:HT, 0:HT], start=True, stop=True)
                            t.then_inc(s_cp, 1)
                        elif n in (2, 4):
                            pe.wait_ge(s_cd, h * CD + (3 if n == 2 else 6))
                            pe.sem_inc(s_pgo, 1)
                            pe.matmul(cB[0:HT, 400:401], flat(back_row), c.one[0:1, 0:1],
                                      start=True, stop=True).then_inc(s_cp, 1)
                        elif n == 3:
                            pe.wait_ge(s_cd, h * CD + 5)
                            pe.sem_inc(s_pgo, 1)
                            pe.matmul(cB[0:1, 0:HT], F[:, 127:128], c.ident[0:HT, 0:HT], start=True, stop=True)
                            pe.matmul(cB[0:1, HT:2 * HT], EX[:, 128:129], c.ident[0:HT, 0:HT],
                                      start=True, stop=True).then_inc(s_cp, 1)
                        else:
                            pe.wait_ge(s_cd, h * CD + 7)
                            pe.sem_inc(s_pgo, 1)
                            pe.transpose(cA[:, 0:HT], AL[:, :], c.ident[0:HT, 0:HT])
                            for j in range(2):
                                t = pe.matmul(cA[:, P + j * G:P + j * G + G], c.heads[H][:, j, :], Df[:, :],
                                              start=True, stop=True)
                            t.then_inc(s_cp, 1)

                    def aggregate(i):
                        T = h * G + i
                        pe.wait_ge(s_msg, T + 2 * G + 1)
                        pe.wait_ge(s_add, T + 1)
                        for j in range(2):
                            t = pe.matmul(pag[i % 2][:, j * P:j * P + P], msg[:, i % 2, j * P:j * P + P],
                                          S[:, b, i, :], start=True, stop=True)
                        t.then_inc(s_agg, 1)

                    at = {0: 0, 1: 1, 2: 2, 4: 3, 6: 4, 7: 5}
                    for i in range(G):
                        if back and i in at:
                            chain(at[i])
                        if front:
                            T = g * G + i
                            pe.wait_ge(s_S, T + 1)
                            wait(pe, s_ST, T - 1)
                            pe.transpose(pST[i % 2][:, 0:P], S[:, k, i, :], c.ident[:, :]).then_inc(s_turn, 1)
                            pe.wait_ge(s_ST, T + 1)
                            pe.wait_ge(s_q[i % Q], (g * 4 + (i // Q + 1)) * 16)
                            wait(pe, s_front, T - 1)
                            pe.matmul(pqd[i % 2][:, 0:DW], ST[:, i % 2, :], win[:, i % Q, :],
                                      start=True, stop=True).then_inc(s_qd, 1)
                        if back and i >= 8:
                            aggregate(2 * (i - 8))
                            aggregate(2 * (i - 8) + 1)

                run(pe, step)

            @block.scalar
            def _(act):
                def step(g, k, u, ub, front):
                    b, h = 1 - k, g - 1
                    back = not isinstance(g, int) or g > 0

                    def chain(n):
                        if n == 0:
                            act.wait_ge(s_cp, h * 6 + 1)
                            act.activation(X0[:, :], cA[0:HT, 0:P], ACT.Copy, scale=scale).then_inc(s_ca, 1)
                        elif n == 1:
                            act.wait_ge(s_cd, h * CD + 4)
                            act.activation(EX[:, :], Y[:, :], ACT.Exp).then_inc(s_ca, 1)
                        else:
                            act.wait_ge(s_cp, h * 6 + 6)
                            if not gat:
                                act.copy(alpha[:, b, :, :].rearrange("p h g -> p (h g)"), cA[:, 0:HT])
                            act.copy(fac[:, b, :, :].rearrange("p c g -> p (c g)"),
                                     cA[:, P:P + 2 * G]).then_inc(s_ca, 1)

                    at = {0: 0, 3: 1, 7: 2}
                    for i in range(G):
                        if back and i in at:
                            chain(at[i])
                        if front:
                            T = g * G + i
                            act.wait_ge(s_turn, T + 1)
                            wait(act, s_qd, T - 1)
                            act.copy(ST[:, i % 2, :], pST[i % 2][:, 0:P]).then_inc(s_ST, 1)
                            if not gat:
                                act.wait_ge(s_g[i % R], (g * 2 + (i // R + 1)) * 16)
                                act.wait_ge(s_msg, T + 1)
                                act.copy(vst[:, k, i, :], kv[:, i % R, D:2 * D]).then_inc(s_v, 1)

                run(act, step)

            @block.vector
            def _(v):
                ini = Step(v, s_init)
                ini(v.memset(acc[:, :, :], 0.0))
                for t, value in ((wn, -BIG), (Rm, -BIG), (Lx, -BIG), (wg, 0.0), (Rs, 0.0), (Ls, 0.0)):
                    ini(v.memset(t[:, :, :], value))
                for t in (r3, r2):
                    ini(v.memset(t[:, :, :, :], 0.0))
                ini(v.memset(cn[:, :, :], 0.0))
                ini(v.memset(back_row[:, :, :], 0.0))
                ini(v.memset(col[:, :], 0.0))
                v.wait_ge(s_d0, 16)
                v.sem_inc(s_msg, 2 * G)
                v.sem_inc(s_add, 2)

                def step(g, k, u, ub, front):
                    b, h = 1 - k, g - 1
                    back = not isinstance(g, int) or g > 0
                    own = Step(v, s_cn, h * CN)

                    def chain(n):
                        if n == 0:
                            v.wait_ge(s_ca, h * 3 + 1)
                            v.tensor_copy(M[:, :], cA[0:HT, P:P + 131]).then_inc(s_cd, 1)
                            own(v.tensor_scalar(NBm[:, :], cA[0:HT, P:P + 129], 1.0, BIG, ALU.subtract, ALU.mult))
                            if gat:
                                own(v.scalar_tensor_tensor(X[:, :], X0[:, :], 0.2, X0[:, :], ALU.mult, ALU.max))
                            v.tensor_tensor_scan(F[:, :], NBm[:, 0:P], X[:, :], -BIG, ALU.add, ALU.max).then_inc(s_cd, 1)
                        elif n == 1:
                            v.wait_ge(s_cp, h * 6 + 2)
                            v.tensor_copy(Lx[:, :, 0:1], Rm[:, :, G:G + 1])
                            own(v.tensor_copy(r3[:, :, :, :].rearrange("a c h g -> a (c h g)"), cB[0:1, 0:3 * HT]))
                            v.tensor_scalar(wn[:, :, 1:G + 1], r3[:, 2, :, :], 1.0, BIG, ALU.subtract, ALU.mult)
                            v.tensor_scalar(cn[:, :, :], r3[:, 1, :, :], 1.0, BIG, ALU.subtract, ALU.mult)
                            own(v.tensor_copy(Lx[:, :, 1:G + 1], r3[:, 0, :, :]))
                            own(v.tensor_tensor_scan(flat(Rm), flat(wn), flat(Lx), -BIG, ALU.add, ALU.max))
                            v.tensor_tensor(back_row[:, :, :], Rm[:, :, 0:G], cn[:, :, :], ALU.add).then_inc(s_cd, 1)
                        elif n == 2:
                            v.wait_ge(s_cp, h * 6 + 3)
                            own(v.tensor_copy(col[:, 0:1], cB[0:HT, 400:401]))
                            own(v.tensor_tensor_scan(F[:, :], NBm[:, 0:P], X[:, :], col[:, 0:1], ALU.add, ALU.max))
                            own(v.tensor_tensor_scan(B[:, ::-1], NBm[:, 128:0:-1], F[:, ::-1], -BIG, ALU.add, ALU.max))
                            v.tensor_tensor(Y[:, 128:129], col[:, 0:1], B[:, 0:1], ALU.subtract)
                            v.tensor_tensor(Y[:, 0:P], X[:, :], B[:, :], ALU.subtract).then_inc(s_cd, 1)
                        elif n == 3:
                            v.wait_ge(s_ca, h * 3 + 2)
                            v.tensor_tensor_scan(F[:, :], M[:, 0:P], EX[:, 0:P], 0.0, ALU.mult, ALU.add).then_inc(s_cd, 1)
                        elif n == 4:
                            v.wait_ge(s_cp, h * 6 + 4)
                            v.tensor_copy(Ls[:, :, 0:1], Rs[:, :, G:G + 1])
                            own(v.tensor_copy(r2[:, :, :, :].rearrange("a c h g -> a (c h g)"), cB[0:1, 0:2 * HT]))
                            v.tensor_tensor(wg[:, :, 1:G + 1], r3[:, 2, :, :], r2[:, 1, :, :], ALU.mult)
                            own(v.tensor_copy(Ls[:, :, 1:G + 1], r2[:, 0, :, :]))
                            own(v.tensor_tensor_scan(flat(Rs), flat(wg), flat(Ls), 0.0, ALU.mult, ALU.add))
                            v.tensor_tensor(back_row[:, :, :], Rs[:, :, 0:G], r2[:, 1, :, :], ALU.mult).then_inc(s_cd, 1)
                        elif n == 5:
                            v.wait_ge(s_cp, h * 6 + 5)
                            own(v.tensor_copy(col[:, 1:2], cB[0:HT, 400:401]))
                            own(v.tensor_tensor_scan(F[:, :], M[:, 0:P], EX[:, 0:P], col[:, 1:2], ALU.mult, ALU.add))
                            v.tensor_tensor_scan(B[:, ::-1], M[:, 128:0:-1], F[:, ::-1], 0.0,
                                                 ALU.mult, ALU.max).then_inc(s_cn, 1)
                            own.n += 1
                            v.wait_ge(s_cn, own.base + own.n)
                            v.reciprocal(Y[:, 0:P], B[:, :]).then_inc(s_cn, 1)
                            v.wait_ge(s_cn, own.base + own.n + 1)
                            own.n += 1
                            v.tensor_scalar(Df[:, :], c.same[0:HT, :], col[:, 1:2], Y[:, 0:1], ALU.mult, ALU.mult)
                            v.tensor_tensor(AL[:, :], EX[:, 0:P], Y[:, 0:P], ALU.mult).then_inc(s_cd, 1)
                        elif n == 6:
                            v.wait_ge(s_ca, h * 3 + 3)
                            if gat:
                                v.tensor_tensor(alpha[:, b, :, :], cA[:, 0:HT].rearrange("p (h g) -> p h g", h=H),
                                                dist[:, b, :].unsqueeze(1).to_broadcast([P, H, G]),
                                                ALU.mult).then_inc(s_cd, 1)
                                v.wait_ge(s_cd, h * CD + CD)

                    def onehot(i):
                        if i == 0:
                            v.wait_ge(s_fl[k], (u + 1) * (16 * NL))
                        v.wait_ge(s_agg, g * G + i + 1)
                        v.tensor_scalar(S[:, k, i, :], c.iota[:, :], rel[:, k, i:i + 1], None,
                                        ALU.is_equal).then_inc(s_S, 1)

                    def scores(i):
                        T = g * G + i
                        v.wait_ge(s_g[i % R], (g * 2 + (i // R + 1)) * 16)
                        v.wait_ge(s_qd, T + 1)
                        if gat:
                            v.tensor_tensor(score[:, k, :, i], vst[:, k, i, D:D + H], pqd[i % 2][:, 0:H],
                                            ALU.add).then_inc(s_front, 1)
                        else:
                            wait(v, s_score, T - 1)
                            v.tensor_tensor(prod[:, i % 2, :], kv[:, i % R, 0:D], pqd[i % 2][:, 0:D],
                                            ALU.mult).then_inc(s_front, 1)

                    def reduce(i):
                        if gat:
                            v.wait_ge(s_front, g * G + i + 1)
                            v.sem_inc(s_score, 1)
                        else:
                            v.wait_ge(s_front, g * G + i + 1)
                            v.tensor_reduce(score[:, k, :, i], prod[:, i % 2, :].rearrange("p (h o) -> p h o", h=H),
                                            AX.X, ALU.add).then_inc(s_score, 1)

                    def message(i):
                        T = h * G + i
                        if not gat:
                            v.wait_ge(s_v, T + 1)
                        v.wait_ge(s_agg, T + 2 * G - 1)
                        v.tensor_tensor(msg[:, i % 2, :].rearrange("p (h o) -> p h o", h=H),
                                        vst[:, b, i, 0:D].rearrange("p (h o) -> p h o", h=H),
                                        alpha[:, b, :, i:i + 1].to_broadcast([P, H, Dh]), ALU.mult).then_inc(s_msg, 1)

                    first = {}

                    def add(i):
                        T = h * G + i
                        if i % 4 == 0:
                            _, first[0] = nc.values_load_multi_w_load_instructions(
                                d0[0:1, bass.ds(T, 4)], engines=[DVE_ENG], min_val=0, max_val=N)
                        n0 = first[0][i % 4]
                        v.wait_ge(s_agg, T + 2 * G + 1)
                        v.wait_ge(s_add, T + 2)
                        for j in range(2):
                            v.scalar_tensor_tensor(acc[:, j, bass.ds(n0, 1)], acc[:, j, bass.ds(n0, 1)],
                                                   fac[:, b, j, i:i + 1], pag[i % 2][:, j * P:j * P + 1],
                                                   ALU.mult, ALU.add)
                        v.tensor_tensor(acc[:, :, bass.ds(n0 + 1, P - 1)], acc[:, :, bass.ds(n0 + 1, P - 1)],
                                        pag[i % 2][:, 0:2 * P].rearrange("p (j r) -> p j r", j=2)[:, :, 1:P],
                                        ALU.add).then_inc(s_add, 1)

                    early, late = {0: 0, 4: 3}, {1: 1, 2: 2, 5: 4, 6: 5, 7: 6}
                    for i in range(G):
                        if front and i == 0:
                            onehot(0)
                            onehot(1)
                        if back and i in early:
                            chain(early[i])
                        if front:
                            if i + 2 < G:
                                onehot(i + 2)
                            scores(i)
                            if i:
                                reduce(i - 1)
                        if back and i in late:
                            chain(late[i])
                        if back and i >= 8:
                            j = 2 * (i - 8)
                            message(j)
                            if j:
                                add(j - 2)
                            message(j + 1)
                            if j:
                                add(j - 1)
                    if front:
                        reduce(G - 1)
                    if back:
                        add(G - 2)
                        add(G - 1)

                run(v, step)


class Constants:

    def __init__(self, nc, m):
        s_c, s_p, s_o = sems(nc, "const", "dve", "pool", "own")
        self.ident = m.sb("ident", [P, P])
        self.iota = m.sb("iota", [P, P])
        self.one = m.sb("one", [P, 2])
        self.rep = m.sb("rep", [G, 8 * G])
        self.same = m.sb("same", [P, G])
        self.heads = {H: m.sb(f"heads{H}", [H * G, 2, P]) for H in (8, 4)}
        ints = m.sb("ints", [P, P], I32)
        with nc.Block() as block:

            @block.vector
            def _(v):
                own = Step(v, s_o)
                v.memset(self.one[:, :], 1.0)
                v.memset(self.ident[:, :], 1.0)
                for H in (8, 4):
                    v.memset(self.heads[H][:, :, :], 1.0)
                v.engine_nop().then_inc(s_c, 1)
                v.wait_ge(s_p, 6)
                v.tensor_copy(self.iota[:, :], ints[:, :])
                for h in range(8):
                    v.tensor_copy(self.rep[:, h * G:h * G + G], self.ident[0:G, 0:G])
                own(v.tensor_reduce(self.same[:, :], self.ident[:, :].rearrange("p (h t) -> p t h", t=G),
                                    AX.X, ALU.add))

            @block.gpsimd
            def _(pool):
                pool.wait_ge(s_c, 1)
                own = Step(pool, s_p)
                own(pool.affine_select(out=self.ident[:, :], in_=self.ident[:, :], compare_op=ALU.is_equal,
                                       fill=0.0, base=0, pattern=[[-1, P]], channel_multiplier=1))
                own(pool.iota(ints[:, :], [[1, P]], base=0, channel_multiplier=0))
                for H in (8, 4):
                    HH, Dh = H // 2, D // H
                    t = self.heads[H][:, :, :].rearrange("p j (a o) -> p j a o", a=HH)
                    own(pool.affine_select(out=t, in_=t, compare_op=ALU.is_ge, fill=0.0, base=0,
                                           pattern=[[-G * HH, 2], [-G, HH], [0, Dh]], channel_multiplier=1))
                    own(pool.affine_select(out=t, in_=t, compare_op=ALU.is_ge, fill=0.0, base=G - 1,
                                           pattern=[[G * HH, 2], [G, HH], [0, Dh]], channel_multiplier=-1))


def graph_norm(nc, c, dr, acc, w_out, b_out, gw, gb, gms):
    CH, SQ = 500, 2500
    NCH, NSQ, NBK = N // CH, N // SQ, 98
    (s_w, s_x0, s_x1, s_mm, s_h, s_own, s_mean, s_sq, s_std, s_sc, s_g, s_t, s_r0, s_r1, s_add, s_st0, s_st1) = sems(
        nc, "gn", "weights", "xT0", "xT1", "product", "h", "dve", "mean", "squares", "std", "scale",
        "gelu", "turned", "rows0", "rows1", "added", "stored0", "stored1")
    s_x, s_r, s_st = (s_x0, s_x1), (s_r0, s_r1), (s_st0, s_st1)
    with Scope(nc, "gn") as m:
        wo = m.sb("wo", [P, 2, D])
        vec = m.sb("vec", [P, 4, 2])
        xT = m.sb("xT", [P, 2, 2, CH])
        sums = m.sb("sums", [P, 2, NCH])
        squares = m.sb("squares", [P, 2, NSQ])
        junk = m.sb("junk", [P, SQ])
        st = m.sb("st", [P, 6, 2])
        eps = m.sb("eps", [P, 1])
        g = m.sb("g", [P, 2, 2, P])
        row = m.sb("row", [P, 2, D])
        ph = [m.ps(f"ph{i}", [P, 512]) for i in range(4)]
        pt = [m.ps(f"pt{i}", [P, 512]) for i in range(2)]
        with nc.Block() as block:

            @block.sync
            def _(sp):
                sp.dma_start(wo[:, :, :], w_out.rearrange("(c p) n -> p c n", p=P)).then_inc(s_w, 16)
                for j, a in enumerate((b_out, gw, gb, gms)):
                    sp.dma_start(vec[:, j, :], a.rearrange("(c p) -> p c", p=P),
                                 allow_slow_non_contiguous=True).then_inc(s_w, 16)
                for s in range(2):
                    sp.dma_start(xT[:, s, :, :], dr["xT"][:, :, s * CH:s * CH + CH]).then_inc(s_x[s], 16)
                with sp.Fori(0, (NCH - 3) // 2) as i:
                    for s in range(2):
                        b = 2 * i + s
                        sp.wait_ge(s_h, 2 * b + 4)
                        sp.dma_start(xT[:, s, :, :], dr["xT"][:, :, bass.ds((b + 2) * CH, CH)]).then_inc(s_x[s], 16)
                sp.wait_ge(s_h, 2 * NCH - 2)
                sp.dma_start(xT[:, 0, :, :], dr["xT"][:, :, (NCH - 1) * CH:NCH * CH]).then_inc(s_x[0], 16)
                for s in range(2):
                    sp.dma_start(row[:, s, :], dr["x"][s * P:s * P + P, :]).then_inc(s_r[s], 16)
                with sp.Fori(0, NBK // 2 - 1) as i:
                    for s in range(2):
                        b = 2 * i + s
                        sp.wait_ge(s_add, b + 3)
                        sp.dma_start(dr["x"][bass.ds(b * P, P), :], row[:, s, :]).then_inc(s_st[s], 16)
                        sp.wait_ge(s_st[s], i * 16 + 16)
                        sp.dma_start(row[:, s, :], dr["x"][bass.ds((b + 2) * P, P), :]).then_inc(s_r[s], 16)
                for s in range(2):
                    sp.wait_ge(s_add, NBK + 1 + s)
                    sp.dma_start(dr["x"][(NBK - 2 + s) * P:(NBK - 1 + s) * P, :], row[:, s, :]).then_inc(s_st[s], 16)
                for s in range(2):
                    sp.wait_ge(s_st[s], NBK // 2 * 16)

            @block.tensor
            def _(pe):
                pe.wait_ge(s_w, 80)

                def project(b, s):
                    if not isinstance(b, int):
                        pe.wait_ge(s_h, 2 * b)
                    for o in range(2):
                        for k in range(2):
                            t = pe.matmul(ph[2 * s + o][:, 0:CH], wo[:, k, o * P:o * P + P],
                                          acc[:, k, bass.ds(b * CH, CH)], start=(k == 0), stop=(k == 1))
                    t.then_inc(s_mm, 1)

                project(0, 0)
                with pe.Fori(0, (NCH - 1) // 2) as i:
                    project(2 * i + 1, 1)
                    project(2 * i + 2, 0)

                with pe.Fori(0, NBK // 2) as i:
                    for s in range(2):
                        b = 2 * i + s
                        pe.wait_ge(s_g, b + 1)
                        pe.wait_ge(s_add, b + 1)
                        for o in range(2):
                            t = pe.transpose(pt[s][:, o * P:o * P + P], g[:, s, o, :], c.ident[:, :])
                        t.then_inc(s_t, 1)

            @block.vector
            def _(v):
                v.memset(eps[:, :], EPS).then_inc(s_sc, 1)
                v.sem_inc(s_h, 2)
                v.sem_inc(s_add, 2)

                def add(b, s, k):
                    v.wait_ge(s_mm, b + 1)
                    v.wait_ge(s_x[s], k * 16 + 16)
                    for o in range(2):
                        n = bass.ds(b * CH, CH)
                        v.scalar_tensor_tensor(acc[:, o, n], ph[2 * s + o][:, 0:CH], vec[:, 0, o:o + 1],
                                               xT[:, s, o, :], ALU.add, ALU.add).then_inc(s_h, 1)
                        v.wait_ge(s_h, 2 * b + o + 3)
                        v.tensor_reduce(sums[:, o, bass.ds(b, 1)], acc[:, o, n], AX.X, ALU.add).then_inc(s_own, 1)

                v.wait_ge(s_w, 80)
                add(0, 0, 0)
                with v.Fori(0, (NCH - 1) // 2) as i:
                    add(2 * i + 1, 1, i)
                    add(2 * i + 2, 0, i + 1)
                v.wait_ge(s_own, 2 * NCH)
                own = Step(v, s_own, 2 * NCH)
                own(v.tensor_reduce(st[:, 1, :], sums[:, :, :], AX.X, ALU.add))
                v.scalar_tensor_tensor(st[:, 0, :], st[:, 1, :], -1.0 / N, vec[:, 3, :],
                                       ALU.mult, ALU.mult).then_inc(s_mean, 1)
                v.wait_ge(s_sq, 2 * NSQ)
                own(v.tensor_reduce(st[:, 1, :], squares[:, :, :], AX.X, ALU.add))
                v.tensor_scalar(st[:, 2, :], st[:, 1, :], 1.0 / N, None, ALU.mult).then_inc(s_sc, 1)
                v.wait_ge(s_std, 1)
                own(v.reciprocal(st[:, 3, :], st[:, 1, :]))
                own(v.tensor_tensor(st[:, 4, :], st[:, 3, :], vec[:, 1, :], ALU.mult))
                own(v.tensor_tensor(st[:, 5, :], st[:, 4, :], st[:, 0, :], ALU.mult))
                v.tensor_tensor(st[:, 5, :], st[:, 5, :], vec[:, 2, :], ALU.add).then_inc(s_sc, 1)
                with v.Fori(0, NBK // 2) as i:
                    for s in range(2):
                        b = 2 * i + s
                        v.wait_ge(s_t, b + 1)
                        v.wait_ge(s_r[s], i * 16 + 16)
                        v.tensor_tensor(row[:, s, :], row[:, s, :], pt[s][:, 0:D], ALU.add).then_inc(s_add, 1)

            @block.scalar
            def _(act):
                act.wait_ge(s_mean, 1)
                for o in range(2):
                    for q in range(NSQ):
                        if o + q:
                            act.wait_ge(s_sq, o * NSQ + q)
                        act.activation(junk[:, :], acc[:, o, q * SQ:q * SQ + SQ], ACT.Square, bias=st[:, 0, o:o + 1],
                                       accum_out=squares[:, o, q:q + 1]).then_inc(s_sq, 1)
                act.wait_ge(s_sc, 2)
                act.activation(st[:, 1, :], st[:, 2, :], ACT.Sqrt, bias=eps[:, 0:1]).then_inc(s_std, 1)
                act.wait_ge(s_sc, 3)

                def gelu(i, s):
                    b = 2 * i + s
                    if not isinstance(i, int):
                        act.wait_ge(s_t, b - 1)
                    for o in range(2):
                        t = act.activation(g[:, s, o, :], acc[:, o, bass.ds(b * P, P)], ACT.Gelu,
                                           bias=st[:, 5, o:o + 1], scale=st[:, 4, o:o + 1])
                    t.then_inc(s_g, 1)

                for s in range(2):
                    gelu(0, s)
                with act.Fori(1, NBK // 2) as i:
                    for s in range(2):
                        gelu(i, s)


def moe_top2(nc, c, dr, router_w, w1, b1, w2, b2):
    SBW, NSB = 256, NR // 256
    (s_w, s_c, s_x0, s_x1, s_own, s_bn, s_sd, s_ln, s_tp, s_xT, s_lg, s_ex, s_pr, s_cT, s_cS, s_m1, s_h, s_m2,
     s_y, s_yf, s_st0, s_st1, s_b0, s_go) = sems(
        nc, "top2", "weights", "consts", "rows0", "rows1", "dve", "stats", "std", "normed", "turned", "xT",
        "logits", "exp", "probs", "combT", "combS", "hidden_sums", "hidden", "expert_sums", "weighted",
        "started", "stored0", "stored1", "router", "go")
    s_x, s_st = (s_x0, s_x1), (s_st0, s_st1)
    with Scope(nc, "top2") as m:
        rw = m.sb("rw", [P, 2, 8])
        rw8 = m.sb("rw8", [8, D])
        W1 = m.sb("w1", [P, 8, 2, D])
        W2 = m.sb("w2", [P, 8, 2, D])
        B1 = m.sb("b1", [P, 8, 2])
        B2 = m.sb("b2", [8, D])
        eps = m.sb("eps", [P, 1])
        x = m.sb("x", [P, 2, 2, D])
        st = m.sb("st", [P, 2, 6])
        mv = m.sb("mv", [P, 2, 2])
        sd = m.sb("sd", [P, 2, 2])
        ln = m.sb("ln", [P, 2, 2, D])
        xT = m.sb("xT", [P, 2, 2, SBW])
        lg = m.sb("lg", [P, 2, 8])
        pr = m.sb("pr", [P, 2, 8])
        e1 = m.sb("e1", [P, 2, 8])
        k1 = m.sb("k1", [P, 2, 8])
        k2 = m.sb("k2", [P, 2, 8])
        p2 = m.sb("p2", [P, 2, 8])
        i8 = m.sb("i8", [P, 2, 8])
        sc = m.sb("sc", [P, 8, 2])
        comb = m.sb("comb", [P, 2, 2, 8])
        cT = m.sb("cT", [8, 2, 2, P])
        hT = m.sb("hT", [P, 2, 2, SBW])
        y = m.sb("y", [P, 2, 2, D])
        pT = m.ps("pT", [P, 512])
        pr_ = m.ps("pr_", [P, 512])
        ph = [m.ps(f"ph{i}", [P, 512]) for i in range(2)]
        py = [m.ps(f"py{i}", [P, 512]) for i in range(2)]
        pb = m.ps("pb", [P, 512])
        rows = lambda b: dr["x"][bass.ds(b * SBW, SBW), :].rearrange("(k p) d -> p k d", p=P)
        CV = 23

        def run(eng, front, experts):
            front(0, 0, 0)

            def both(b, s, *following):
                experts(b, s, range(0, 4))
                if following:
                    front(*following)
                experts(b, s, range(4, 8))

            with eng.Fori(0, NSB // 2 - 1) as i:
                both(2 * i, 0, 2 * i + 1, 1, i)
                both(2 * i + 1, 1, 2 * i + 2, 0, i + 1)
            both(NSB - 2, 0, NSB - 1, 1, NSB // 2 - 1)
            both(NSB - 1, 1)

        def wait(eng, sem, value):
            if not isinstance(value, int) or value > 0:
                eng.wait_ge(sem, value)

        with nc.Block() as block:

            @block.sync
            def _(sp):
                sp.dma_start(rw8[:, :], router_w).then_inc(s_w, 16)
                sp.dma_start(B1[:, :, :], b1.rearrange("e (c p) -> p e c", p=P),
                             allow_slow_non_contiguous=True).then_inc(s_w, 16)
                sp.dma_start(B2[:, :], b2).then_inc(s_w, 16)
                for e in range(8):
                    sp.dma_start(W1[:, e, :, :], w1[e].rearrange("(c p) n -> p c n", p=P)).then_inc(s_w, 16)
                    sp.dma_start(W2[:, e, :, :], w2[e].rearrange("(c p) n -> p c n", p=P)).then_inc(s_w, 16)
                for s in range(2):
                    sp.dma_start(x[:, s, :, :], rows(s)).then_inc(s_x[s], 16)
                    sp.sem_inc(s_st[s], 16)

                def store(b, s):
                    sp.wait_ge(s_y, b * 16 + 18)
                    sp.dma_start(rows(b), y[:, s, :, :]).then_inc(s_st[s], 16)

                with sp.Fori(0, NSB // 2 - 1) as i:
                    for s in range(2):
                        b = 2 * i + s
                        store(b, s)
                        sp.dma_start(x[:, s, :, :], rows(b + 2)).then_inc(s_x[s], 16)
                for s in range(2):
                    store(NSB - 2 + s, s)
                for s in range(2):
                    sp.wait_ge(s_st[s], NSB // 2 * 16 + 16)

            @block.vector
            def _(v):
                v.memset(eps[:, :], EPS).then_inc(s_c, 1)
                v.tensor_scalar(i8[:, 0, :], c.iota[:, 0:8], 8.0, None, ALU.subtract)
                v.tensor_scalar(i8[:, 1, :], c.iota[:, 0:8], 8.0, None, ALU.subtract).then_inc(s_c, 1)
                v.sem_inc(s_y, 2)
                v.wait_ge(s_b0, 1)
                v.tensor_copy(rw[:, :, :].rearrange("p c e -> p (c e)"), pr_[:, 0:16]).then_inc(s_c, 1)

                def front(b, s, u):
                    own = Step(v, s_own, b * CV)
                    for k in range(2):
                        if k == 0:
                            v.wait_ge(s_x[s], u * 16 + 16)
                        own(v.bn_stats(st[:, k, :], x[:, s, k, :]))
                        v.sem_inc(s_go, 1)
                        v.bn_aggr(mv[:, k, :], st[:, k, :]).then_inc(s_bn, 1)
                    v.wait_ge(s_sd, b + 1)
                    own(v.reciprocal(sd[:, :, 1], sd[:, :, 0]))
                    for k in range(2):
                        own(v.tensor_scalar(ln[:, s, k, :], x[:, s, k, :], mv[:, k, 0:1], sd[:, k, 1:2],
                                            ALU.subtract, ALU.mult))
                    v.sem_inc(s_ln, 1)
                    bc = lambda t: t.unsqueeze(2).to_broadcast([P, 2, 8])
                    v.wait_ge(s_lg, b + 1)
                    own(v.tensor_copy(lg[:, :, :].rearrange("p k e -> p (k e)"), pr_[:, 0:16]))
                    own(v.tensor_reduce(sc[:, 0, :], lg[:, :, :], AX.X, ALU.max))
                    v.tensor_tensor(lg[:, :, :], lg[:, :, :], bc(sc[:, 0, :]), ALU.subtract).then_inc(s_pr, 1)
                    v.wait_ge(s_ex, b + 1)
                    own(v.tensor_reduce(sc[:, 1, :], e1[:, :, :], AX.X, ALU.add))
                    own(v.reciprocal(sc[:, 2, :], sc[:, 1, :]))
                    own(v.tensor_tensor(pr[:, :, :], e1[:, :, :], bc(sc[:, 2, :]), ALU.mult))
                    own(v.tensor_reduce(sc[:, 3, :], pr[:, :, :], AX.X, ALU.max))
                    own(v.tensor_tensor(k1[:, :, :], pr[:, :, :], bc(sc[:, 3, :]), ALU.is_equal))
                    own(v.tensor_tensor(k2[:, :, :], k1[:, :, :], i8[:, :, :], ALU.mult))
                    own(v.tensor_reduce(sc[:, 4, :], k2[:, :, :], AX.X, ALU.min))
                    own(v.tensor_tensor(k1[:, :, :], i8[:, :, :], bc(sc[:, 4, :]), ALU.is_equal))
                    own(v.scalar_tensor_tensor(p2[:, :, :], k1[:, :, :], -4.0, pr[:, :, :], ALU.mult, ALU.add))
                    own(v.tensor_reduce(sc[:, 5, :], p2[:, :, :], AX.X, ALU.max))
                    own(v.tensor_tensor(p2[:, :, :], p2[:, :, :], bc(sc[:, 5, :]), ALU.is_equal))
                    own(v.tensor_tensor(p2[:, :, :], p2[:, :, :], i8[:, :, :], ALU.mult))
                    own(v.tensor_reduce(sc[:, 4, :], p2[:, :, :], AX.X, ALU.min))
                    own(v.tensor_tensor(k2[:, :, :], i8[:, :, :], bc(sc[:, 4, :]), ALU.is_equal))
                    own(v.tensor_tensor(k1[:, :, :], k1[:, :, :], k2[:, :, :], ALU.add))
                    v.tensor_tensor(sc[:, 6, :], sc[:, 3, :], sc[:, 5, :], ALU.add).then_inc(s_pr, 1)
                    v.wait_ge(s_pr, b * 5 + 2)
                    v.tensor_scalar(sc[:, 6, :], sc[:, 6, :], 1e-12, None, ALU.max).then_inc(s_pr, 1)
                    v.wait_ge(s_pr, b * 5 + 3)
                    v.reciprocal(sc[:, 7, :], sc[:, 6, :]).then_inc(s_pr, 1)
                    v.wait_ge(s_pr, b * 5 + 4)
                    own(v.tensor_tensor(k1[:, :, :], k1[:, :, :], bc(sc[:, 7, :]), ALU.mult))
                    v.tensor_tensor(comb[:, s, :, :], k1[:, :, :], pr[:, :, :], ALU.mult).then_inc(s_pr, 1)
                    v.wait_ge(s_pr, b * 5 + 5)
                    v.wait_ge(s_cT, 2 * b + 1)
                    v.tensor_copy(cT[:, s, :, :].rearrange("e k p -> e (k p)"), pr_[0:8, 256:512]).then_inc(s_cS, 1)
                    v.wait_ge(s_st[s], u * 16 + 16)
                    v.tensor_tensor(y[:, s, :, :], x[:, s, :, :], ln[:, s, :, :], ALU.add).then_inc(s_yf, 1)
                    v.wait_ge(s_yf, 2 * b + 1)
                    v.wait_ge(s_cT, 2 * b + 2)
                    v.tensor_tensor(y[:, s, :, :].rearrange("p k d -> p (k d)"),
                                    y[:, s, :, :].rearrange("p k d -> p (k d)"), pb[:, :], ALU.add).then_inc(s_yf, 1)
                    assert own.n == CV, own.n

                def experts(b, s, which):
                    for e in which:
                        for k in range(2):
                            v.wait_ge(s_m2, (b * 8 + e) * 2 + k + 5)
                            if e:
                                v.wait_ge(s_y, (b * 8 + e) * 2 + k + 1)
                            else:
                                v.wait_ge(s_yf, 2 * b + 2)
                            v.scalar_tensor_tensor(y[:, s, k, :], py[k][:, 0:D], comb[:, s, k, e:e + 1],
                                                   y[:, s, k, :], ALU.mult, ALU.add).then_inc(s_y, 1)

                run(v, front, experts)

            @block.scalar
            def _(act):
                act.wait_ge(s_c, 2)
                act.sem_inc(s_h, 2)
                act.sem_inc(s_m2, 4)
                act.wait_ge(s_w, 16 * 19)

                def front(b, s, u):
                    act.wait_ge(s_bn, 2 * b + 2)
                    act.activation(sd[:, :, 0], mv[:, :, 1], ACT.Sqrt, bias=eps[:, 0:1]).then_inc(s_sd, 1)
                    for k in range(2):
                        act.wait_ge(s_tp, 2 * b + k + 1)
                        act.copy(xT[:, s, :, k * P:k * P + P],
                                 pT[:, 0:D].rearrange("p (c n) -> p c n", c=2)).then_inc(s_xT, 1)
                    act.wait_ge(s_pr, b * 5 + 1)
                    act.activation(e1[:, :, :], lg[:, :, :], ACT.Exp).then_inc(s_ex, 1)

                def experts(b, s, which):
                    for e in which:
                        act.wait_ge(s_m1, b * 8 + e + 1)
                        act.wait_ge(s_m2, (b * 8 + e) * 2 + 2)
                        for f in range(2):
                            t = act.activation(hT[:, e % 2, f, :], ph[e % 2][:, f * SBW:f * SBW + SBW], ACT.Gelu,
                                               bias=B1[:, e, f:f + 1])
                        t.then_inc(s_h, 1)

                run(act, front, experts)

            @block.tensor
            def _(pe):
                pe.wait_ge(s_w, 16 * 19)
                for k in range(2):
                    t = pe.transpose(pr_[:, k * 8:k * 8 + 8], rw8[:, k * P:k * P + P], c.ident[0:8, 0:8])
                t.then_inc(s_b0, 1)
                pe.wait_ge(s_c, 3)

                def front(b, s, u):
                    pe.wait_ge(s_ln, b + 1)
                    for k in range(2):
                        wait(pe, s_xT, 2 * b + k)
                        for j in range(2):
                            t = pe.transpose(pT[:, j * P:j * P + P], ln[:, s, k, j * P:j * P + P], c.ident[:, :])
                        t.then_inc(s_tp, 1)
                    pe.wait_ge(s_xT, 2 * b + 2)
                    for k in range(2):
                        for j in range(2):
                            t = pe.matmul(pr_[:, k * 8:k * 8 + 8], xT[:, s, j, k * P:k * P + P], rw[:, j, :],
                                          start=(j == 0), stop=(j == 1))
                    t.then_inc(s_lg, 1)
                    pe.wait_ge(s_pr, b * 5 + 5)
                    for k in range(2):
                        t = pe.transpose(pr_[0:8, 256 + k * P:256 + k * P + P], comb[:, s, k, :], c.ident[:, :])
                    t.then_inc(s_cT, 1)
                    pe.wait_ge(s_cS, b + 1)
                    for k in range(2):
                        t = pe.matmul(pb[:, k * D:k * D + D], cT[:, s, k, :], B2[:, :], start=True, stop=True)
                    t.then_inc(s_cT, 1)

                def experts(b, s, which):
                    def first(e):
                        pe.wait_ge(s_h, b * 8 + e + 1)
                        for f in range(2):
                            for j in range(2):
                                t = pe.matmul(ph[e % 2][:, f * SBW:f * SBW + SBW], W1[:, e, j, f * P:f * P + P],
                                              xT[:, s, j, :], start=(j == 0), stop=(j == 1))
                        t.then_inc(s_m1, 1)

                    def second(e):
                        pe.wait_ge(s_h, b * 8 + e + 3)
                        for k in range(2):
                            pe.wait_ge(s_y, (b * 8 + e) * 2 + k + 1)
                            for j in range(2):
                                t = pe.matmul(py[k][:, 0:D], hT[:, e % 2, j, k * P:k * P + P], W2[:, e, j, :],
                                              start=(j == 0), stop=(j == 1))
                            t.then_inc(s_m2, 1)

                    for e in which:
                        if e % 4 == 0:
                            first(e)
                        if e % 4 < 3:
                            first(e + 1)
                        second(e)

                run(pe, front, experts)


def moe_switch(nc, c, dr, gate_b, w1, b1, w2, b2, out):
    NBK, FULL, EXP, FF = (N + P - 1) // P, N // P, 8, 1024
    CAP = -(-(5 * N) // (4 * EXP))
    ROWS = -(-CAP // 512) * 512
    SPE = ROWS // 512
    BIGI = float(1 << 20)
    (s_ld, s_c, s_own, s_ex, s_cnt, s_pl, s_zero, s_l0, s_l1, s_i, s_sc0, s_sc1, s_scx,
     s_w0, s_w1, s_r0, s_r1, s_t, s_tx, s_m1, s_h, s_m2, s_y, s_ys0, s_ys1,
     s_g0, s_g1, s_x0, s_x1, s_gi, s_o, s_st0, s_st1, s_nn, s_go) = sems(
        nc, "switch", "loaded", "consts", "dve", "exp", "counts", "pool", "zeroed", "rows0", "rows1", "index",
        "scattered0", "scattered1", "x",
        "weights0", "weights1", "buf0", "buf1", "turned", "copied", "hidden_sums", "hidden", "sums", "y",
        "ystored0", "ystored1", "gathered0", "gathered1", "x0", "x1", "gindex", "result", "stored0", "stored1", "nan", "go")
    s_l, s_sc, s_w, s_r, s_ys, s_g, s_x, s_st = ((s_l0, s_l1), (s_sc0, s_sc1), (s_w0, s_w1), (s_r0, s_r1),
                                                (s_ys0, s_ys1), (s_g0, s_g1), (s_x0, s_x1), (s_st0, s_st1))
    with Scope(nc, "switch") as top:
        sslot = top.sb("sslot", [P, NBK], I32)
        gslot = top.sb("gslot", [P, NBK], I32)
        wgt = top.sb("wgt", [P, NBK])
        flat = lambda t: t[:, :, :].rearrange("p b e -> p (b e)")
        with Scope(nc, "assign") as m:
            lg = m.sb("lg", [P, NBK, 8])
            gb = m.sb("gb", [P, 8])
            i8 = m.sb("i8", [P, 8])
            valid = m.sb("valid", [P, NBK])
            upto = m.sb("upto", [P, P])
            ones = m.sb("ones", [P, P])
            nil = m.sb("nil", [P, NBK])
            ex = m.sb("ex", [P, NBK, 8])
            oh = m.sb("oh", [P, NBK, 8])
            tt = m.sb("tt", [P, NBK, 8])
            tot = m.sb("tot", [P, 8, NBK])
            inc = m.sb("inc", [P, 8, NBK])
            a = m.sb("a", [P, 8, NBK])
            pw = [m.ps(f"pw{i}", [P, 512]) for i in range(2)]
            pt = [m.ps(f"pt{i}", [P, 512]) for i in range(2)]
            HB = NBK // 2
            assert NBK % 2 == 0
            with nc.Block() as block:

                @block.sync
                def _(sp):
                    sp.dma_start(lg[:, :, :], dr["logits"][0:NBK * P, :].rearrange(
                        "(b p) e -> p b e", p=P)).then_inc(s_ld, 16)
                    sp.dma_start(gb[:, :], gate_b.rearrange("(a e) -> a e", a=1).to_broadcast([P, 8])).then_inc(s_ld, 16)

                @block.gpsimd
                def _(pool):
                    pool.wait_ge(s_c, 1)
                    pool.affine_select(out=upto[:, :], in_=upto[:, :], compare_op=ALU.is_ge, fill=0.0, base=0,
                                       pattern=[[1, P]], channel_multiplier=-1)
                    pool.affine_select(out=valid[:, NBK - 1:NBK], in_=valid[:, NBK - 1:NBK], compare_op=ALU.is_ge,
                                       fill=0.0, base=N - FULL * P - 1, pattern=[[0, 1]],
                                       channel_multiplier=-1).then_inc(s_pl, 1)

                @block.scalar
                def _(act):
                    act.wait_ge(s_own, 4)
                    act.activation(ex[:, :, :], tt[:, :, :], ACT.Exp).then_inc(s_ex, 1)

                @block.tensor
                def _(pe):
                    pe.wait_ge(s_cnt, 1)
                    for i in range(2):
                        cols = oh[:, i * HB:i * HB + HB, :].rearrange("p b e -> p (b e)")
                        pe.matmul(pw[i][:, 0:HB * 8], upto[:, :], cols, start=True, stop=True)
                        t = pe.matmul(pt[i][:, 0:HB * 8], ones[:, :], cols, start=True, stop=True)
                    t.then_inc(s_cnt, 1)

                @block.vector
                def _(v):
                    bc = lambda t: t.unsqueeze(2).to_broadcast([P, NBK, 8])
                    row8 = lambda t: t[:, :].unsqueeze(1).to_broadcast([P, NBK, 8])
                    v.memset(upto[:, :], 1.0)
                    v.memset(ones[:, :], 1.0)
                    v.memset(nil[:, :], 0.0)
                    v.memset(valid[:, :], 1.0).then_inc(s_c, 1)
                    own = Step(v, s_own)
                    own(v.tensor_scalar(i8[:, :], c.iota[:, 0:8], 8.0, None, ALU.subtract))
                    v.wait_ge(s_ld, 32)
                    own(v.tensor_tensor(lg[:, :, :], lg[:, :, :], row8(gb), ALU.add))
                    own(v.tensor_reduce(a[:, 0, :], lg[:, :, :], AX.X, ALU.max))
                    own(v.tensor_tensor(tt[:, :, :], lg[:, :, :], bc(a[:, 0, :]), ALU.subtract))
                    v.wait_ge(s_ex, 1)
                    own(v.tensor_reduce(a[:, 1, :], ex[:, :, :], AX.X, ALU.add))
                    own(v.reciprocal(a[:, 2, :], a[:, 1, :]))
                    own(v.tensor_tensor(lg[:, :, :], ex[:, :, :], bc(a[:, 2, :]), ALU.mult))
                    own(v.tensor_reduce(a[:, 3, :], lg[:, :, :], AX.X, ALU.max))
                    own(v.tensor_tensor(tt[:, :, :], lg[:, :, :], bc(a[:, 3, :]), ALU.is_equal))
                    own(v.tensor_tensor(tt[:, :, :], tt[:, :, :], row8(i8), ALU.mult))
                    own(v.tensor_reduce(a[:, 4, :], tt[:, :, :], AX.X, ALU.min))
                    own(v.tensor_tensor(oh[:, :, :], row8(i8), bc(a[:, 4, :]), ALU.is_equal))
                    v.wait_ge(s_pl, 1)
                    v.tensor_tensor(oh[:, :, :], oh[:, :, :], bc(valid[:, :]), ALU.mult).then_inc(s_cnt, 1)
                    v.wait_ge(s_cnt, 2)
                    for i in range(2):
                        own(v.tensor_copy(tot[:, :, i * HB:i * HB + HB].rearrange("p e b -> p b e"),
                                          pt[i][:, 0:HB * 8].rearrange("p (b e) -> p b e", e=8)))
                    for e in range(8):
                        own(v.tensor_tensor_scan(inc[:, e, :], nil[:, :], tot[:, e, :], 0.0, ALU.add, ALU.add))
                    own(v.tensor_tensor(inc[:, :, :], inc[:, :, :], tot[:, :, :], ALU.subtract))
                    for i in range(2):
                        bl = slice(i * HB, i * HB + HB)
                        own(v.tensor_tensor(tt[:, bl, :], inc[:, :, bl].rearrange("p e b -> p b e"),
                                            pw[i][:, 0:HB * 8].rearrange("p (b e) -> p b e", e=8), ALU.add))
                    own(v.tensor_tensor(tt[:, :, :], tt[:, :, :], oh[:, :, :], ALU.mult))
                    own(v.tensor_reduce(a[:, 5, :], tt[:, :, :], AX.X, ALU.add))
                    own(v.tensor_scalar(a[:, 6, :], a[:, 5, :], float(CAP), None, ALU.is_le))
                    own(v.tensor_tensor(a[:, 6, :], a[:, 6, :], valid[:, :], ALU.mult))
                    own(v.tensor_tensor(wgt[:, :], a[:, 3, :], a[:, 6, :], ALU.mult))
                    own(v.tensor_scalar(a[:, 4, :], a[:, 4, :], float(ROWS), 8.0 * ROWS - 1.0, ALU.mult, ALU.add))
                    own(v.tensor_tensor(a[:, 0, :], a[:, 4, :], a[:, 5, :], ALU.add))
                    own(v.tensor_scalar(a[:, 6, :], a[:, 6, :], -BIGI, BIGI, ALU.mult, ALU.add))
                    own(v.tensor_tensor(a[:, 0, :], a[:, 0, :], a[:, 6, :], ALU.add))
                    own(v.tensor_copy(sslot[:, :], a[:, 0, :]))
                    own(v.tensor_scalar(a[:, 5, :], a[:, 5, :], 1.0, float(CAP), ALU.max, ALU.min))
                    own(v.tensor_tensor(a[:, 5, :], a[:, 5, :], a[:, 4, :], ALU.add))
                    own(v.tensor_copy(gslot[:, :], a[:, 5, :]))
                    v.sem_inc(s_i, 1)

        with Scope(nc, "scatter") as m:
            zero = m.sb("zero", [P, 4 * D])
            row = m.sb("row", [P, 2, D])
            slot = m.sb("slot", [P, 2, 2], I32)
            with nc.Block() as block:

                @block.vector
                def _(v):
                    v.memset(zero[:, :], 0.0).then_inc(s_zero, 1)
                    for s in range(2):
                        v.tensor_copy(slot[:, s, 0:1], sslot[:, s:s + 1]).then_inc(s_i, 1)
                    with v.Fori(1, NBK // 2) as i:
                        for s in range(2):
                            v.wait_ge(s_sc[s], i * 16)
                            v.tensor_copy(slot[:, s, 0:1], sslot[:, bass.ds(2 * i + s, 1)]).then_inc(s_i, 1)

                @block.scalar
                def _(act):
                    act.wait_ge(s_zero, 1)
                    with act.Fori(0, EXP * ROWS // 512) as i:
                        act.dma_start(dr["buf"][bass.ds(i * 512, 512), :].rearrange("(p r) d -> p (r d)", p=P),
                                      zero[:, :]).then_inc(s_zero, 16)

                @block.sync
                def _(sp):
                    for s in range(2):
                        sp.dma_start(row[:, s, :], dr["ln"][s * P:s * P + P, :]).then_inc(s_l[s], 16)
                    with sp.Fori(1, NBK // 2) as i:
                        for s in range(2):
                            sp.wait_ge(s_sc[s], i * 16)
                            sp.dma_start(row[:, s, :], dr["ln"][bass.ds((2 * i + s) * P, P), :]).then_inc(s_l[s], 16)

                @block.gpsimd
                def _(pool):
                    pool.wait_ge(s_zero, 1 + 16 * (EXP * ROWS // 512))
                    with pool.Fori(0, NBK // 2) as i:
                        for s in range(2):
                            pool.wait_ge(s_l[s], i * 16 + 16)
                            pool.wait_ge(s_i, 2 * i + s + 2)
                            pool.sem_inc(s_scx, 1)
                            pool.indirect_dma_start(dr["buf"], IndirectOffsetOnAxis(ap=slot[:, s, 0:1], axis=0),
                                                    row[:, s, :], None, bounds_check=EXP * ROWS - 1,
                                                    oob_is_err=False).then_inc(s_sc[s], 16)
                    for s in range(2):
                        pool.wait_ge(s_sc[s], NBK // 2 * 16)

        with Scope(nc, "experts") as m:
            W1 = m.sb("w1", [P, 2, 2, FF])
            W2 = m.sb("w2", [P, 2, 8, D])
            B1 = m.sb("b1", [P, 2, 8])
            B2 = m.sb("b2", [P, 2, D])
            row = m.sb("row", [P, 2, 4, D])
            xT = m.sb("xT", [P, 2, 2, 512])
            hT = m.sb("hT", [P, 2, 8, 512])
            y = m.sb("y", [P, 2, 4, D])
            pT = [m.ps(f"pT{i}", [P, 512]) for i in range(2)]
            ph = [m.ps(f"ph{i}", [P, 512]) for i in range(2)]
            py = [m.ps(f"py{i}", [P, 512]) for i in range(2)]
            assert SPE == 4
            NSUP = EXP * SPE
            rows = lambda t, n: dr[t][bass.ds(n * 512, 512), :].rearrange("(k p) d -> p k d", p=P)

            def weights(sp, e, s):
                ex_ = lambda a: a[bass.ds(e, 1)]
                sp.dma_start(W1[:, s, :, :], ex_(w1).rearrange("e (c p) n -> (e p) c n", p=P)).then_inc(s_w[s], 16)
                sp.dma_start(W2[:, s, :, :], ex_(w2).rearrange("e (c p) n -> (e p) c n", p=P)).then_inc(s_w[s], 16)
                sp.dma_start(B1[:, s, :], ex_(b1).rearrange("e (c p) -> (e p) c", p=P),
                             allow_slow_non_contiguous=True).then_inc(s_w[s], 16)
                sp.dma_start(B2[:, s, :], ex_(b2).to_broadcast([P, D])).then_inc(s_w[s], 16)

            with nc.Block() as block:

                @block.sync
                def _(sp):
                    sp.wait_ge(s_sc[0], NBK // 2 * 16)
                    sp.wait_ge(s_sc[1], NBK // 2 * 16)
                    for s in range(2):
                        weights(sp, s, s)
                        sp.dma_start(row[:, s, :, :], rows("buf", s)).then_inc(s_r[s], 16)
                        sp.sem_inc(s_ys[s], 16)

                    def pair(i, s, q, load):
                        n = (2 * i + s) * SPE + q
                        if load:
                            sp.wait_ge(s_t, n * 4 + 4)
                            sp.dma_start(row[:, q % 2, :, :], rows("buf", n + 2)).then_inc(s_r[q % 2], 16)
                        sp.wait_ge(s_y, n * 8 + 12)
                        sp.dma_start(rows("ybuf", n), y[:, q % 2, :, :]).then_inc(s_ys[q % 2], 16)

                    with sp.Fori(0, EXP // 2 - 1) as i:
                        for s in range(2):
                            for q in range(SPE):
                                pair(i, s, q, True)
                            weights(sp, 2 * i + s + 2, s)
                    for s in range(2):
                        for q in range(SPE):
                            pair(EXP // 2 - 1, s, q, s * SPE + q < 2 * SPE - 2)
                    for s in range(2):
                        sp.wait_ge(s_ys[s], NSUP // 2 * 16 + 16)

                def loop(eng, body):
                    with eng.Fori(0, EXP // 2) as i:
                        for s in range(2):
                            for q in range(SPE):
                                body(i, s, q, (2 * i + s) * SPE + q)

                @block.tensor
                def _(pe):
                    def body(i, s, q, n):
                        pe.wait_ge(s_r[q % 2], (2 * SPE * i + SPE * s + q - q % 2) * 8 + 16)
                        for k in range(4):
                            pe.wait_ge(s_tx, n * 4 + k + 1)
                            for j in range(2):
                                t = pe.transpose(pT[k % 2][:, j * P:j * P + P], row[:, q % 2, k, j * P:j * P + P],
                                                 c.ident[:, :])
                            t.then_inc(s_t, 1)
                        if q == 0:
                            pe.wait_ge(s_w[s], i * 64 + 64)
                        pe.wait_ge(s_tx, n * 4 + 6)
                        for f in range(8):
                            pe.wait_ge(s_h, n * 8 + f + 1)
                            for j in range(2):
                                t = pe.matmul(ph[f % 2][:, :], W1[:, s, j, f * P:f * P + P], xT[:, q % 2, j, :],
                                              start=(j == 0), stop=(j == 1))
                            t.then_inc(s_m1, 1)
                        for k in range(4):
                            pe.wait_ge(s_y, n * 8 + 2 * k + 2)
                            for f in range(8):
                                if k == 0:
                                    pe.wait_ge(s_h, n * 8 + f + 3)
                                t = pe.matmul(py[k % 2][:, 0:D], hT[:, q % 2, f, k * P:k * P + P], W2[:, s, f, :],
                                              start=(f == 0), stop=(f == 7))
                            t.then_inc(s_m2, 1)

                    loop(pe, body)

                @block.scalar
                def _(act):
                    act.sem_inc(s_tx, 2)
                    act.sem_inc(s_h, 2)

                    def body(i, s, q, n):
                        for k in range(4):
                            act.wait_ge(s_t, n * 4 + k + 1)
                            act.copy(xT[:, q % 2, :, k * P:k * P + P],
                                     pT[k % 2][:, 0:D].rearrange("p (c n) -> p c n", c=2)).then_inc(s_tx, 1)
                        if q == 0:
                            act.wait_ge(s_w[s], i * 64 + 64)
                        for f in range(8):
                            act.wait_ge(s_m1, n * 8 + f + 1)
                            act.activation(hT[:, q % 2, f, :], ph[f % 2][:, :], ACT.Relu,
                                           bias=B1[:, s, f:f + 1]).then_inc(s_h, 1)

                    loop(act, body)

                @block.vector
                def _(v):
                    v.sem_inc(s_y, 4)

                    def body(i, s, q, n):
                        v.wait_ge(s_ys[q % 2], (2 * SPE * i + SPE * s + q - q % 2) * 8 + 16)
                        for k in range(4):
                            v.wait_ge(s_m2, n * 4 + k + 1)
                            if k == 0 and q == 0:
                                v.wait_ge(s_w[s], i * 64 + 64)
                            v.tensor_tensor(y[:, q % 2, k, :], py[k % 2][:, 0:D], B2[:, s, :], ALU.add).then_inc(s_y, 2)

                    loop(v, body)

        with Scope(nc, "combine") as m:
            x = m.sb("x", [P, 2, D])
            yg = m.sb("yg", [P, 2, D])
            t_ = m.sb("t", [P, 2, D])
            bad = m.sb("bad", [P, 3, D], U32)
            lim = m.sb("lim", [P, 3, D])
            slot = m.sb("slot", [P, 2, 2], I32)
            with nc.Block() as block:

                @block.sync
                def _(sp):
                    def load(b, s):
                        sp.dma_start(x[:, s, :], dr["x"][bass.ds(b * P, P), :]).then_inc(s_x[s], 16)

                    def store(b, s, n=P):
                        sp.wait_ge(s_o, b + 1)
                        sp.dma_start(out[bass.ds(b * P, n), :], t_[0:n, s, :]).then_inc(s_st[s], 16)

                    for s in range(2):
                        sp.sem_inc(s_st[s], 16)
                        load(s, s)
                    with sp.Fori(0, NBK // 2 - 1) as i:
                        for s in range(2):
                            store(2 * i + s, s)
                            load(2 * i + s + 2, s)
                    store(NBK - 2, 0)
                    store(NBK - 1, 1, N - FULL * P)
                    for s in range(2):
                        sp.wait_ge(s_st[s], NBK // 2 * 16 + 16)

                @block.gpsimd
                def _(pool):
                    with pool.Fori(0, NBK // 2) as i:
                        for s in range(2):
                            b = 2 * i + s
                            pool.wait_ge(s_gi, b + 1)
                            pool.sem_inc(s_scx, 1)
                            pool.indirect_dma_start(yg[:, s, :], None, dr["ybuf"], IndirectOffsetOnAxis(
                                ap=slot[:, s, 0:1], axis=0)).then_inc(s_g[s], 16)

                @block.vector
                def _(v):
                    for j, value in enumerate((0.0, 1e4, -1e4)):
                        t = v.memset(lim[:, j, :], value)
                    t.then_inc(s_nn, 1)
                    v.wait_ge(s_nn, 1)
                    for s in range(2):
                        v.tensor_copy(slot[:, s, 0:1], gslot[:, s:s + 1]).then_inc(s_gi, 1)

                    def body(i, s, b, last=False):
                        own = Step(v, s_nn, b * 6 + 1)
                        v.wait_ge(s_g[s], i * 16 + 16)
                        v.wait_ge(s_st[s], i * 16 + 16)
                        own(v.tensor_scalar(t_[:, s, :], yg[:, s, :], wgt[:, bass.ds(b, 1)], None, ALU.mult))
                        if not last:
                            v.tensor_copy(slot[:, s, 0:1], gslot[:, bass.ds(b + 2, 1)]).then_inc(s_gi, 1)
                        v.tensor_tensor(bad[:, 0, :], t_[:, s, :], t_[:, s, :], ALU.not_equal)
                        v.tensor_scalar(bad[:, 1, :], t_[:, s, :], 3.4028235e38, None, ALU.is_gt)
                        own(v.tensor_scalar(bad[:, 2, :], t_[:, s, :], -3.4028235e38, None, ALU.is_lt))
                        for j in range(3):
                            v.sem_inc(s_go, 1)
                            own(v.copy_predicated(t_[:, s, :], bad[:, j, :], lim[:, j, :]))
                        v.wait_ge(s_x[s], i * 16 + 16)
                        own(v.tensor_tensor(t_[:, s, :], t_[:, s, :], x[:, s, :], ALU.add))
                        v.sem_inc(s_o, 1)

                    with v.Fori(0, NBK // 2 - 1) as i:
                        for s in range(2):
                            body(i, s, 2 * i + s)
                    for s in range(2):
                        body(NBK // 2 - 1, s, NBK - 2 + s, True)


def add_rows(nc, c, dr, acc):
    NBK = (N + P - 1) // P
    s_cp, s_t, s_r0, s_r1, s_add, s_st0, s_st1 = sems(
        nc, "rows", "copied", "turned", "rows0", "rows1", "added", "stored0", "stored1")
    s_r, s_st = (s_r0, s_r1), (s_st0, s_st1)
    with Scope(nc, "rows") as m:
        g = m.sb("g", [P, 2, 2, P])
        row = m.sb("row", [P, 2, D])
        pt = [m.ps(f"pt{i}", [P, 512]) for i in range(2)]
        with nc.Block() as block:

            @block.sync
            def _(sp):
                for s in range(2):
                    sp.dma_start(row[:, s, :], dr["x"][s * P:s * P + P, :]).then_inc(s_r[s], 16)
                with sp.Fori(0, NBK // 2 - 1) as i:
                    for s in range(2):
                        b = 2 * i + s
                        sp.wait_ge(s_add, b + 3)
                        sp.dma_start(dr["x"][bass.ds(b * P, P), :], row[:, s, :]).then_inc(s_st[s], 16)
                        sp.wait_ge(s_st[s], i * 16 + 16)
                        sp.dma_start(row[:, s, :], dr["x"][bass.ds((b + 2) * P, P), :]).then_inc(s_r[s], 16)
                for s in range(2):
                    sp.wait_ge(s_add, NBK + 1 + s)
                    sp.dma_start(dr["x"][(NBK - 2 + s) * P:(NBK - 1 + s) * P, :], row[:, s, :]).then_inc(s_st[s], 16)
                for s in range(2):
                    sp.wait_ge(s_st[s], NBK // 2 * 16)

            @block.scalar
            def _(act):
                act.sem_inc(s_t, 2)
                with act.Fori(0, NBK // 2) as i:
                    for s in range(2):
                        b = 2 * i + s
                        act.wait_ge(s_t, b + 1)
                        act.copy(g[:, s, :, :], acc[:, :, bass.ds(b * P, P)]).then_inc(s_cp, 1)

            @block.tensor
            def _(pe):
                with pe.Fori(0, NBK // 2) as i:
                    for s in range(2):
                        b = 2 * i + s
                        pe.wait_ge(s_cp, b + 1)
                        pe.wait_ge(s_add, b + 1)
                        for o in range(2):
                            t = pe.transpose(pt[s][:, o * P:o * P + P], g[:, s, o, :], c.ident[:, :])
                        t.then_inc(s_t, 1)

            @block.vector
            def _(v):
                v.sem_inc(s_add, 2)
                with v.Fori(0, NBK // 2) as i:
                    for s in range(2):
                        b = 2 * i + s
                        v.wait_ge(s_t, b + 3)
                        v.wait_ge(s_r[s], i * 16 + 16)
                        v.tensor_tensor(row[:, s, :], row[:, s, :], pt[s][:, 0:D], ALU.add).then_inc(s_add, 1)


def run_phase(nc, f, *args, **kw):
    before = set(nc.free_semaphores)
    f(nc, *args, **kw)
    used = sorted(before - set(nc.free_semaphores))
    nc.clear_and_free_semaphores(used)
    nc.all_engine_barrier()


def graph_program(nc, a, out):
    phase = lambda f, *args, **kw: run_phase(nc, f, *args, **kw)
    dram = lambda name, shape, dt=F32: nc.dram_tensor(name, shape, dt).ap()
    dr = dict(x=dram("xs", (NR, D)), src=dram("srcp", (1, NE), I32), dst=dram("dstp", (1, NE + 1), I32),
              dist=dram("distp", (1, NE)), mask=dram("mask", (NT, MW)), d0=dram("d0", (NT, 1), I32),
              srcT=dram("srcT", (P, NT + G), I32), relT=dram("relT", (P, NT + G)), distT=dram("distT", (P, NT)),
              q=dram("q", (NR, D)), kv=dram("kv", (NR, 2 * D)), xT=dram("xT", (P, 2, NR)),
              ft=dram("ft", (NR, 260)), ed=dram("ed", (NR, 4)), logits=dram("logits", (NR, 8)),
              ln=dram("ln", (NR, D)), buf=dram("buf", (8 * 2048, D)), ybuf=dram("ybuf", (8 * 2048, D)))
    NA = N + P + 12
    with Scope(nc, "all") as m:
        c = Constants(nc, m)
        phase(prepare_edges, c.ident, a["x"], a["src"], a["dst"], a["edge_attr3_1x1"], dr)
        phase(node_tables, c.ident, "qkv", dr["x"],
                    [(0, a["L0_gnn_WQ"]), (D, a["L0_gnn_WK"]), (2 * D, a["L0_gnn_WV"])], 3 * D,
                    [(dr["q"], 0, 0, D), (dr["kv"], 0, D, 2 * D)], xT_out=dr["xT"])
        with Scope(nc, "sum0") as s:
            acc = s.sb("acc", [P, 2, NA])
            phase(edge_phase, "att", c, dr, acc, 8, float(np.float32(1 / np.sqrt(np.float32(D // 8)))),
                       dr["kv"], dr["q"], None)
            phase(graph_norm, c, dr, acc, a["L0_gnn_W_out"], a["L0_gnn_b_out"], a["L0_gnn_gn_weight"],
                       a["L0_gnn_gn_bias"], a["L0_gnn_gn_mean_scale"])
        phase(moe_top2, c, dr, a["L0_ffn_router_w"], a["L0_ffn_w1"], a["L0_ffn_b1"], a["L0_ffn_w2"], a["L0_ffn_b2"])
        phase(node_tables, c.ident, "gat", dr["x"], [(0, a["L1_gnn_W"])], 264,
                    [(dr["ft"], 0, 0, 260), (dr["ed"], 0, 260, 4)],
                    attention=(a["L1_gnn_w_att_src"], a["L1_gnn_w_att_dst"]))
        with Scope(nc, "sum1") as s:
            acc = s.sb("acc", [P, 2, NA])
            phase(edge_phase, "gate", c, dr, acc, 4, 1.0, dr["ft"], dr["ed"], dr["distT"])
            phase(add_rows, c, dr, acc)
        phase(node_tables, c.ident, "gate_ln", dr["x"], [(0, a["L1_ffn_gate_w"])], 8,
                    [(dr["logits"], 0, 0, 8)], ln_out=dr["ln"])
        moe_switch(nc, c, dr, a["L1_ffn_gate_b"], a["L1_ffn_w1"], a["L1_ffn_b1"], a["L1_ffn_w2"],
                   a["L1_ffn_b2"], out)


_NAMES = ["x", "src", "dst", "edge_attr3_1x1", "L0_gnn_WQ", "L0_gnn_WK", "L0_gnn_WV", "L0_gnn_W_out", "L0_gnn_b_out",
          "L0_gnn_gn_weight", "L0_gnn_gn_bias", "L0_gnn_gn_mean_scale", "L0_ffn_router_w", "L0_ffn_w1", "L0_ffn_b1",
          "L0_ffn_w2", "L0_ffn_b2", "L1_gnn_W", "L1_gnn_w_att_src", "L1_gnn_w_att_dst", "L1_ffn_gate_w",
          "L1_ffn_gate_b", "L1_ffn_w1", "L1_ffn_b1", "L1_ffn_w2", "L1_ffn_b2"]


def kernel(**inputs):
    import numpy as _np
    import concourse.bacc as _bacc
    from concourse import mybir as _mybir
    from concourse.bass_utils import run_bass_kernel_spmd as _run

    nc = _bacc.Bacc("TRN2", target_bir_lowering=False, num_devices=1)
    arrays, aps = {}, {}
    for name in _NAMES:
        a = _np.ascontiguousarray(inputs[name])
        arrays[f"in_{name}_dram"] = a
        aps[name] = nc.dram_tensor(f"in_{name}_dram", a.shape, _mybir.dt.from_np(a.dtype), kind="ExternalInput").ap()
    out = nc.dram_tensor("out_0_dram", (N, D), F32, kind="ExternalOutput").ap()
    graph_program(nc, aps, out)
    r = _run(nc, [arrays], core_ids=[0])
    return r.results[0]["out_0_dram"]
```

```python
from contextlib import ExitStack

import numpy as np
import concourse.bass as bass
from concourse import mybir
from concourse.bass import IndirectOffsetOnAxis

ALU = mybir.AluOpType
ACT = mybir.ActivationFunctionType
AX = mybir.AxisListType
F32 = mybir.dt.float32
I32 = mybir.dt.int32
U32 = mybir.dt.uint32
BF16 = mybir.dt.bfloat16
SP_ENG, ACT_ENG, DVE_ENG = mybir.EngineType.SP, mybir.EngineType.Activation, mybir.EngineType.DVE

P = 128
N = 12500
D = 256
E = 212500
EPS = 1e-5
NB = 100
NR = NB * P
G = 16
NG = 105
NT = NG * G
NE = NT * P
TB = 120
MW = 132
BIG = 1e30
assert NT % TB == 0 and NE > E and NR >= N + P and E > (NT - 8) * P - 8 * P * G


class Step:

    def __init__(self, eng, sem, base=0):
        self.eng, self.sem, self.base, self.n = eng, sem, base, 0

    def __call__(self, ins):
        ins.then_inc(self.sem, 1)
        self.n += 1
        self.eng.wait_ge(self.sem, self.base + self.n)


class Scope(ExitStack):

    def __init__(self, nc, tag):
        super().__init__()
        self.nc, self.tag = nc, tag

    def sb(self, name, shape, dt=F32):
        return self.enter_context(self.nc.sbuf_tensor(f"{self.tag}_{name}", shape, dt))

    def ps(self, name, shape, dt=F32):
        return self.enter_context(self.nc.psum_tensor(f"{self.tag}_{name}", shape, dt))


def sems(nc, tag, *names):
    return [nc.alloc_semaphore(name=f"{tag}_{n}") for n in names]



def prepare_edges(nc, ident, x, src, dst, dist, dr):
    s_fill, s_pad, s_nat, s_free, s_dve, s_turn, s_out, s_st = sems(
        nc, "prep", "filled", "padded", "loaded", "read", "dve", "turned", "copied", "stored")
    NP_ = NE - E
    with Scope(nc, "prep") as m:
        zero = m.sb("zero", [P, (NR - N) * D // 100])
        tail = m.sb("tail", [1, 3, NP_], I32)
        ftail = m.sb("ftail", [1, NP_])
        spare = m.sb("spare", [P, G], I32)
        nat = m.sb("nat", [P, 3, P], I32)
        natd = m.sb("natd", [P, P])
        f = m.sb("f", [P, 3, P])
        rel = m.sb("rel", [P, P])
        cont = m.sb("cont", [P, P])
        mask = m.sb("mask", [P, MW])
        tsrc = m.sb("tsrc", [P, P], I32)
        trel = m.sb("trel", [P, P])
        tdist = m.sb("tdist", [P, P])
        pt = m.ps("pt", [P, 3, P])
        with nc.Block() as block:

            @block.sync
            def _(sp):
                sp.dma_start(dr["x"][0:N, :], x).then_inc(s_pad, 16)
                sp.dma_start(dr["src"][0:1, 0:E], src.rearrange("(a e) -> a e", a=1)).then_inc(s_pad, 16)
                sp.dma_start(dr["dst"][0:1, 1:E + 1], dst.rearrange("(a e) -> a e", a=1)).then_inc(s_pad, 16)
                sp.dma_start(dr["dist"][0:1, 0:E], dist.rearrange("e a b -> (a b) e")).then_inc(s_pad, 16)
                sp.wait_ge(s_fill, 7)
                sp.dma_start(dr["x"][N:NR, :].rearrange("(p r) d -> p (r d)", p=100),
                             zero[0:100, :]).then_inc(s_pad, 16)
                sp.dma_start(dr["src"][0:1, E:NE], tail[:, 0, :]).then_inc(s_pad, 16)
                sp.dma_start(dr["dst"][0:1, E + 1:NE + 1], tail[:, 1, :]).then_inc(s_pad, 16)
                sp.dma_start(dr["dst"][0:1, 0:1], tail[:, 2, 0:1]).then_inc(s_pad, 16)
                sp.dma_start(dr["dist"][0:1, E:NE], ftail[:, :]).then_inc(s_pad, 16)
                sp.dma_start(dr["srcT"][:, NT:NT + G], spare[:, :]).then_inc(s_pad, 16)
                sp.dma_start(dr["relT"][:, NT:NT + G], zero[:, 0:G]).then_inc(s_pad, 16)
                sp.wait_ge(s_pad, 11 * 16)
                with sp.Fori(0, NT // TB) as b:
                    sp.wait_ge(s_free, b + 1)
                    e0 = b * (TB * P)
                    for i, (name, off) in enumerate((("src", 0), ("dst", 1), ("dst", 0))):
                        sp.dma_start(nat[0:TB, i, :], dr[name][0:1, bass.ds(e0 + off, TB * P)].rearrange(
                            "a (t e) -> (a t) e", e=P)).then_inc(s_nat, 16)
                    sp.dma_start(natd[0:TB, :], dr["dist"][0:1, bass.ds(e0, TB * P)].rearrange(
                        "a (t e) -> (a t) e", e=P)).then_inc(s_nat, 16)
                    sp.wait_ge(s_out, b + 1)
                    c = bass.ds(b * TB, TB)
                    sp.dma_start(dr["mask"][c, :], mask[0:TB, :]).then_inc(s_st, 16)
                    sp.dma_start(dr["d0"][c, :], nat[0:TB, 1, 0:1]).then_inc(s_st, 16)
                    sp.dma_start(dr["srcT"][:, c], tsrc[:, 0:TB]).then_inc(s_st, 16)
                    sp.dma_start(dr["relT"][:, c], trel[:, 0:TB]).then_inc(s_st, 16)
                    sp.dma_start(dr["distT"][:, c], tdist[:, 0:TB]).then_inc(s_st, 16)

            @block.vector
            def _(v):
                v.memset(zero[:, :], 0.0).then_inc(s_fill, 1)
                v.memset(tail[:, 0, :], 0).then_inc(s_fill, 1)
                v.memset(tail[:, 1, :], N).then_inc(s_fill, 1)
                v.memset(tail[:, 2, :], -1).then_inc(s_fill, 1)
                v.memset(ftail[:, :], 0.0).then_inc(s_fill, 1)
                v.memset(spare[:, :], 0).then_inc(s_fill, 1)
                v.memset(mask[:, :], 1.0).then_inc(s_fill, 1)
                v.wait_ge(s_fill, 7)
                v.sem_inc(s_free, 1)
                with v.Fori(0, NT // TB) as b:
                    own = Step(v, s_dve, b * 5)
                    v.wait_ge(s_nat, b * 64 + 64)
                    own(v.tensor_copy(f[0:TB, :, :], nat[0:TB, :, :]))
                    own(v.tensor_scalar(rel[0:TB, :], f[0:TB, 1, :], f[0:TB, 1, 0:1], None, ALU.subtract))
                    own(v.tensor_tensor(cont[0:TB, :], f[0:TB, 1, :], f[0:TB, 2, :], ALU.is_equal))
                    v.wait_ge(s_st, b * 80 + 16)
                    own(v.tensor_copy(mask[0:TB, 1:P], cont[0:TB, 1:P]))
                    v.tensor_copy(mask[0:TB, 129:130], cont[0:TB, 0:1])
                    own(v.scalar_tensor_tensor(mask[0:TB, 130:131], rel[0:TB, 127:128], 0.0, cont[0:TB, 0:1],
                                               ALU.is_equal, ALU.mult))
                    v.wait_ge(s_turn, b + 1)
                    v.tensor_copy(tsrc[:, 0:TB], pt[:, 0, 0:TB])
                    v.tensor_copy(trel[:, 0:TB], pt[:, 1, 0:TB])
                    v.tensor_copy(tdist[:, 0:TB], pt[:, 2, 0:TB]).then_inc(s_out, 1)
                    v.wait_ge(s_st, b * 80 + 96)
                    v.sem_inc(s_free, 1)

            @block.scalar
            def _(act):
                act.wait_ge(s_fill, 7)
                act.sem_inc(s_st, 16)

            @block.tensor
            def _(pe):
                with pe.Fori(0, NT // TB) as b:
                    pe.wait_ge(s_dve, b * 5 + 2)
                    pe.transpose(pt[:, 0, 0:TB], f[0:TB, 0, :], ident[0:TB, 0:TB])
                    pe.transpose(pt[:, 1, 0:TB], rel[0:TB, :], ident[0:TB, 0:TB])
                    pe.transpose(pt[:, 2, 0:TB], natd[0:TB, :], ident[0:TB, 0:TB]).then_inc(s_turn, 1)


def node_tables(nc, ident, tag, src_rows, weights, NC, outs, xT_out=None, attention=None, ln_out=None):
    (s_w, s_c, s_x0, s_x1, s_bn, s_sd, s_ln, s_tp, s_xt, s_mm, s_evd, s_eva, s_st0, s_st1, s_own, s_att, s_go) = sems(
        nc, tag, "weights", "consts", "rows0", "rows1", "stats", "std", "normed", "turned", "xT", "product",
        "copied_dve", "copied_act", "stored0", "stored1", "dve", "att", "go")
    s_x, s_st = (s_x0, s_x1), (s_st0, s_st1)
    nst = len(outs) + (xT_out is not None) + (ln_out is not None)
    split = 384 if NC > 512 else NC // 2
    with Scope(nc, tag) as m:
        w = m.sb("w", [P, 2, NC])
        xin = m.sb("xin", [P, 2, D])
        st = m.sb("st", [P, 2, 6])
        mv = m.sb("mv", [P, 2, 2])
        sd = m.sb("sd", [P, 2, 2])
        eps = m.sb("eps", [P, 1])
        xln = m.sb("xln", [P, 2, D])
        xT = m.sb("xT", [P, 2, 2, P])
        row = m.sb("row", [P, 2, NC])
        att = m.sb("att", [P, 2, D])
        prod = m.sb("prod", [P, 2, D])
        pT = m.ps("pT", [P, 2, 512])
        pq = m.ps("pq", [P, 2, 1024])
        halves = [(0, min(512, NC))] + ([(512, NC)] if NC > 512 else [])
        with nc.Block() as block:

            @block.sync
            def _(sp):
                for i, (c0, ap) in enumerate(weights):
                    sp.dma_start(w[:, :, c0:c0 + ap.shape[1]], ap.rearrange("(c p) n -> p c n", p=P)).then_inc(s_w, 16)
                if attention:
                    for i in range(2):
                        sp.dma_start(att[:, i, :], attention[i].rearrange("a h o -> a (h o)").to_broadcast(
                            [P, D])).then_inc(s_w, 16)

                def store(b, s):
                    rows = bass.ds(b * P, P)
                    if xT_out is not None:
                        sp.wait_ge(s_xt, b + 1)
                    sp.wait_ge(s_evd, b + 1)
                    sp.wait_ge(s_eva, b + 1)
                    for ap, o0, c0, n in outs:
                        sp.dma_start(ap[rows, o0:o0 + n], row[:, s, c0:c0 + n]).then_inc(s_st[s], 16)
                    if xT_out is not None:
                        sp.dma_start(xT_out[:, :, rows], xT[:, s, :, :]).then_inc(s_st[s], 16)
                    if ln_out is not None:
                        sp.dma_start(ln_out[rows, :], xln[:, s, :]).then_inc(s_st[s], 16)

                for s in range(2):
                    sp.dma_start(xin[:, s, :], src_rows[s * P:s * P + P, :]).then_inc(s_x[s], 16)
                with sp.Fori(0, NB // 2 - 1) as i:
                    for s in range(2):
                        b = 2 * i + s
                        sp.wait_ge(s_ln, b + 1)
                        sp.dma_start(xin[:, s, :], src_rows[bass.ds(b * P + 2 * P, P), :]).then_inc(s_x[s], 16)
                        store(b, s)
                for s in range(2):
                    store(NB - 2 + s, s)
                for s in range(2):
                    sp.wait_ge(s_st[s], NB // 2 * nst * 16)

            @block.vector
            def _(v):
                v.memset(eps[:, :], EPS).then_inc(s_c, 1)
                if attention:
                    H = attention[0].shape[1]
                    v.wait_ge(s_w, 16 * (len(weights) + 2))
                    for a in range(2):
                        for c in range(2):
                            if a + c:
                                v.wait_ge(s_att, 2 * (2 * a + c))
                            v.tensor_tensor(prod[:, c, :], w[:, c, 0:D], att[:, a, :], ALU.mult).then_inc(s_att, 1)
                            v.wait_ge(s_att, 2 * (2 * a + c) + 1)
                            v.tensor_reduce(w[:, c, D + a * H:D + a * H + H],
                                            prod[:, c, :].rearrange("p (h o) -> p h o", h=H),
                                            AX.X, ALU.add).then_inc(s_att, 1)

                def body(i, s, first=False):
                    b = 2 * i + s
                    own = Step(v, s_own, b * 2)
                    v.wait_ge(s_x[s], i * 16 + 16)
                    own(v.bn_stats(st[:, s, :], xin[:, s, :]))
                    v.sem_inc(s_go, 1)
                    v.bn_aggr(mv[:, s, :], st[:, s, :]).then_inc(s_bn, 1)
                    if not first:
                        evac(b - 1, 1 - s, i - 1 + s)
                    v.wait_ge(s_sd, b + 1)
                    own(v.reciprocal(sd[:, s, 1:2], sd[:, s, 0:1]))
                    if ln_out is not None and not isinstance(i, int):
                        v.wait_ge(s_st[s], i * (nst * 16))
                    v.tensor_scalar(xln[:, s, :], xin[:, s, :], mv[:, s, 0:1], sd[:, s, 1:2],
                                    ALU.subtract, ALU.mult).then_inc(s_ln, 1)

                def evac(b, s, k):
                    v.wait_ge(s_mm, b + 1)
                    if not isinstance(k, int) or k > 0:
                        v.wait_ge(s_st[s], k * (nst * 16))
                    v.tensor_copy(row[:, s, 0:split], pq[:, s, 0:split]).then_inc(s_evd, 1)

                for s in range(2):
                    body(0, s, first=(s == 0))
                with v.Fori(1, NB // 2) as i:
                    for s in range(2):
                        body(i, s)
                evac(NB - 1, 1, NB // 2 - 1)

            @block.scalar
            def _(act):
                act.wait_ge(s_c, 1)

                def body(i, s):
                    b = 2 * i + s
                    act.wait_ge(s_bn, b + 1)
                    act.activation(sd[:, s, 0:1], mv[:, s, 1:2], ACT.Sqrt, bias=eps[:, 0:1]).then_inc(s_sd, 1)
                    act.wait_ge(s_tp, b + 1)
                    if not isinstance(i, int):
                        if xT_out is not None:
                            act.wait_ge(s_st[s], i * (nst * 16))
                        act.wait_ge(s_mm, b - 1)
                    act.copy(xT[:, s, :, :], pT[:, s, 0:D]).then_inc(s_xt, 1)
                    act.wait_ge(s_evd, b + 1)
                    if not isinstance(i, int):
                        act.wait_ge(s_st[s], i * (nst * 16))
                    act.copy(row[:, s, split:NC], pq[:, s, split:NC]).then_inc(s_eva, 1)

                for s in range(2):
                    body(0, s)
                with act.Fori(1, NB // 2) as i:
                    for s in range(2):
                        body(i, s)

            @block.tensor
            def _(pe):
                pe.wait_ge(s_w, 16 * (len(weights) + (2 if attention else 0)))
                if attention:
                    pe.wait_ge(s_att, 8)

                def body(i, s):
                    b = 2 * i + s
                    pe.wait_ge(s_ln, b + 1)
                    if not isinstance(i, int):
                        pe.wait_ge(s_xt, b - 1)
                    for c in range(2):
                        t = pe.transpose(pT[:, s, c * P:c * P + P], xln[:, s, c * P:c * P + P], ident[:, :])
                    t.then_inc(s_tp, 1)
                    pe.wait_ge(s_xt, b + 1)
                    if not isinstance(i, int):
                        pe.wait_ge(s_eva, b - 1)
                    for h0, h1 in halves:
                        for c in range(2):
                            t = pe.matmul(pq[:, s, h0:h1], xT[:, s, c, :], w[:, c, h0:h1],
                                          start=(c == 0), stop=(c == 1))
                    t.then_inc(s_mm, 1)

                for s in range(2):
                    body(0, s)
                with pe.Fori(1, NB // 2) as i:
                    for s in range(2):
                        body(i, s)


def edge_phase(nc, tag, c, dr, acc, H, scale, rows_t, dst_t, dist_t):
    gat = dist_t is not None
    RW, DW = rows_t.shape[1], dst_t.shape[1]
    Dh, HT, VW = D // H, H * G, (RW if gat else D)
    GP, NP2 = G // 2, NG * (G // 2)
    RG = 3 if gat else 2
    LAG = 15 if gat else 12
    R, Q = (8 if gat else 4), 4
    if gat:
        PE_AT = {(0, 1): 0, (1, 1): 1, (2, 0): 2, (4, 0): 3, (5, 0): 4, (6, 0): 5}
        ACT_AT = {0: 0, 3: 1, 6: 2}
        DVE_AT = {(1, 0): 0, (1, 1): 1, (2, 1): 2, (3, 1): 3, (4, 1): 4, (5, 1): 5, (6, 1): 6}
    else:
        PE_AT = {(0, 1): 0, (1, 0): 1, (1, 1): 2, (2, 1): 3, (3, 0): 4, (3, 1): 5}
        ACT_AT = {0: 0, 2: 1, 3: 2}
        DVE_AT = {(0, 1): 0, (1, 0): 1, (1, 1): 2, (2, 0): 3, (2, 1): 4, (3, 0): 5}
    (s_d0, s_init, s_go) = sems(nc, tag, "firsts", "init", "go")
    s_fl = sems(nc, tag, *[f"lists{r}" for r in range(RG)])
    s_cl = sems(nc, tag, *[f"masks{r}" for r in range(RG)])
    s_g = sems(nc, tag, *[f"gathered{r}" for r in range(R)])
    s_q = sems(nc, tag, *[f"window{r}" for r in range(Q)])
    (s_S, s_turn, s_ST, s_qd, s_front, s_score, s_v, s_msg, s_agg, s_mul, s_add, s_cp, s_ca, s_cd, s_cn,
     s_pgo) = sems(
        nc, tag, "onehot", "turned", "onehotT", "expanded", "front", "scores", "values", "messages",
        "summed", "rescaled", "added", "chain_pe", "chain_act", "chain_dve", "chain_own", "pe_go")
    if gat:
        s_score = s_front
    CD, CN = (8, 15) if gat else (7, 14)
    NL = 2
    NC_ = 2 if gat else 1
    with Scope(nc, tag) as m:
        idx = m.sb("idx", [P, RG, G], I32)
        rel = m.sb("rel", [P, RG, G])
        mrow = m.sb("mrow", [G, RG, MW])
        dist = m.sb("dist", [P, RG, G]) if gat else None
        d0 = m.sb("d0", [1, NT], I32)
        S = m.sb("S", [P, RG, G, P])
        ST = m.sb("ST", [P, 2, 2 * P])
        vst = m.sb("vst", [P, RG, G, VW])
        kv = None if gat else m.sb("kv", [P, R, 2, RW])
        win = m.sb("win", [P, Q, 2, DW])
        prod = None if gat else m.sb("prod", [P, 2 * D])
        score = m.sb("score", [P, RG, H, G])
        msg = m.sb("msg", [P, 2, 2 * D])
        alpha = m.sb("alpha", [P, RG, H, G])
        fac = m.sb("fac", [P, RG, 2, G])
        X = m.sb("X", [HT, P])
        X0 = m.sb("X0", [HT, P]) if gat else X
        M = m.sb("M", [HT, 131])
        NBm = m.sb("NB", [HT, 129])
        F = m.sb("F", [HT, P])
        B = m.sb("B", [HT, P])
        Y = m.sb("Y", [HT, 129])
        EX = m.sb("EX", [HT, 129])
        AL = m.sb("AL", [HT, P])
        Df = m.sb("Df", [HT, G])
        col = m.sb("col", [HT, 2])
        r3 = m.sb("r3", [1, 3, H, G])
        r2 = m.sb("r2", [1, 2, H, G])
        wn = m.sb("wn", [1, H, G + 1])
        Lx = m.sb("Lx", [1, H, G + 1])
        Rm = m.sb("Rm", [1, H, G + 1])
        wg = m.sb("wg", [1, H, G + 1])
        Ls = m.sb("Ls", [1, H, G + 1])
        Rs = m.sb("Rs", [1, H, G + 1])
        cn = m.sb("cn", [1, H, G])
        back_row = m.sb("brow", [1, H, G])
        pST = [m.ps(f"pST{i}", [P, 512]) for i in range(2)]
        pqd = [m.ps(f"pqd{i}", [P, 512]) for i in range(2)]
        pag = [m.ps(f"pag{i}", [P, 512]) for i in range(2)]
        cA = m.ps("cA", [P, 512])
        cB = m.ps("cB", [P, 512])
        flat = lambda t: t[:, :, :].rearrange("a h g -> a (h g)")

        def wait(eng, sem, value):
            if not isinstance(value, int) or value > 0:
                eng.wait_ge(sem, value)

        def near(g, gs, p, off):
            dg, q = (p + off) // GP, (p + off) % GP
            return g + dg, (gs + dg) % RG, q, 0 <= gs + dg < NG

        def run(eng, step):
            assert (NG - 3) % RG == 0
            for g in range(2):
                step(g, g)
            with eng.Fori(0, (NG - 3) // RG) as it:
                for j in range(RG):
                    step(it * RG + (2 + j), 2 + RG + j)
            for g in range(NG - 1, NG + 2):
                step(g, g)

        def firsts(engine, tile, n=4):
            return nc.values_load_multi_w_load_instructions(
                d0[0:1, bass.ds(tile, n)], engines=[engine], min_val=0, max_val=N,
                skip_runtime_bounds_check_because="d0 is clamped to [0, N] when it has been loaded")[1]

        def use(g, gs):
            return gs // RG + 1 if isinstance(g, int) else (g - (gs % RG)) // RG + 1

        def arrived(g, p, R):
            return (g * (GP // R) + (p // R + 1)) * 32

        with nc.Block() as block:

            @block.sync
            def _(sp):
                sp.dma_start(d0[:, :], dr["d0"].rearrange("t a -> a t")).then_inc(s_d0, 16)

                def lists(g, k):
                    t = bass.ds(g * G, G)
                    sp.dma_start(idx[:, k, :], dr["srcT"][:, t]).then_inc(s_fl[k], 16)
                    sp.dma_start(rel[:, k, :], dr["relT"][:, t]).then_inc(s_fl[k], 16)

                lists(0, 0)
                sp.wait_ge(s_d0, 17)

                def step(g, gs):
                    if gs >= NG:
                        return
                    for p in range(GP):
                        if p % 2 == 0:
                            first = firsts(SP_ENG, g * G + 2 * p)
                        wait(sp, s_qd, g * GP + p - Q + 1)
                        for i in range(2):
                            sp.dma_start(win[:, p % Q, i, :],
                                         dst_t[bass.ds(first[2 * (p % 2) + i], P), :]).then_inc(s_q[p % Q], 16)
                        if p == 3:
                            k = gs % RG
                            wait(sp, s_front, g * GP)
                            lists(g + 1, (k + 1) % RG)
                            t = bass.ds(g * G, G)
                            sp.dma_start(mrow[:, k, :], dr["mask"][t, :]).then_inc(s_cl[k], 16)
                            if gat:
                                sp.dma_start(dist[:, k, :], dist_t[:, t]).then_inc(s_cl[k], 16)

                run(sp, step)
                sp.wait_ge(s_fl[NG % RG], 16 * NL * (NG // RG + 1))

            @block.gpsimd
            def _(pool):
                def step(g, gs):
                    if gs >= NG:
                        return
                    k = gs % RG
                    for p in range(GP):
                        T = g * GP + p
                        if p == 0:
                            pool.wait_ge(s_fl[k], use(g, gs) * (16 * NL))
                        if gat:
                            wait(pool, s_front, T - GP + 1)
                        else:
                            wait(pool, s_front, T - R + 1)
                            wait(pool, s_v, T - R + 1)
                        pool.sem_inc(s_go, 1)
                        for i in range(2):
                            row = vst[:, k, 2 * p + i, :] if gat else kv[:, p % R, i, :]
                            pool.indirect_dma_start(row, None, rows_t, IndirectOffsetOnAxis(
                                ap=idx[:, k, 2 * p + i:2 * p + i + 1], axis=0)).then_inc(s_g[p % R], 16)

                run(pool, step)

            @block.tensor
            def _(pe):
                pe.wait_ge(s_init, 12)

                def turn(g, gs, p):
                    k, T = gs % RG, g * GP + p
                    pe.wait_ge(s_S, T + 1)
                    for i in range(2):
                        t = pe.transpose(pST[p % 2][:, i * P:i * P + P], S[:, k, 2 * p + i, :], c.ident[:, :])
                    t.then_inc(s_turn, 1)

                def expand(g, gs, p):
                    T = g * GP + p
                    pe.wait_ge(s_ST, T + 1)
                    pe.wait_ge(s_q[p % Q], arrived(g, p, Q))
                    wait(pe, s_front, T - 1)
                    for i in range(2):
                        t = pe.matmul(pqd[p % 2][:, i * DW:i * DW + DW], ST[:, p % 2, i * P:i * P + P],
                                      win[:, p % Q, i, :], start=True, stop=True)
                    t.then_inc(s_qd, 1)

                def chain(n, h, hs):
                    b = hs % RG
                    if n == 0:
                        pe.wait_ge(s_score, h * GP + GP)
                        pe.wait_ge(s_cl[b], use(h, hs) * (16 * NC_))
                        pe.sem_inc(s_pgo, 1)
                        pe.transpose(cA[0:HT, 0:P], score[:, b, :, :].rearrange("p h g -> p (h g)"), c.ident[:, :])
                        pe.matmul(cA[0:HT, P:P + 131], c.rep[:, 0:HT], mrow[:, b, 0:131],
                                  start=True, stop=True).then_inc(s_cp, 1)
                    elif n == 1:
                        pe.wait_ge(s_cd, h * CD + 2)
                        pe.sem_inc(s_pgo, 1)
                        pe.matmul(cB[0:1, 0:HT], F[:, 127:128], c.ident[0:HT, 0:HT], start=True, stop=True)
                        for j in range(2):
                            t = pe.matmul(cB[0:1, HT + j * HT:2 * HT + j * HT], M[:, 129 + j:130 + j],
                                          c.ident[0:HT, 0:HT], start=True, stop=True)
                        t.then_inc(s_cp, 1)
                    elif n in (2, 4):
                        pe.wait_ge(s_cd, h * CD + (3 if n == 2 else 6))
                        pe.sem_inc(s_pgo, 1)
                        pe.matmul(cB[0:HT, 400:401], flat(back_row), c.one[0:1, 0:1],
                                  start=True, stop=True).then_inc(s_cp, 1)
                    elif n == 3:
                        pe.wait_ge(s_cd, h * CD + 5)
                        pe.sem_inc(s_pgo, 1)
                        pe.matmul(cB[0:1, 0:HT], F[:, 127:128], c.ident[0:HT, 0:HT], start=True, stop=True)
                        pe.matmul(cB[0:1, HT:2 * HT], EX[:, 128:129], c.ident[0:HT, 0:HT],
                                  start=True, stop=True).then_inc(s_cp, 1)
                    else:
                        pe.wait_ge(s_cd, h * CD + 7)
                        pe.sem_inc(s_pgo, 1)
                        pe.transpose(cA[:, 0:HT], AL[:, :], c.ident[0:HT, 0:HT])
                        for j in range(2):
                            t = pe.matmul(cA[:, P + j * G:P + j * G + G], c.heads[H][:, j, :], Df[:, :],
                                          start=True, stop=True)
                        t.then_inc(s_cp, 1)

                def aggregate(g, gs, p):
                    pe.wait_ge(s_msg, g * GP + p + 1)
                    for i in range(2):
                        for j in range(2):
                            t = pe.matmul(pag[p % 2][:, i * D + j * P:i * D + j * P + P],
                                          msg[:, p % 2, i * D + j * P:i * D + j * P + P],
                                          S[:, gs % RG, 2 * p + i, :], start=True, stop=True)
                    t.then_inc(s_agg, 1)

                turn(0, 0, 0)
                turn(0, 0, 1)
                expand(0, 0, 0)

                def step(g, gs):
                    for p in range(GP):
                        chained = 0 < gs <= NG
                        if chained and (p, 0) in PE_AT:
                            chain(PE_AT[p, 0], g - 1, gs - 1)
                        for f, off in ((expand, 1), (turn, 2)):
                            fg, fs, fp, real = near(g, gs, p, off)
                            if real:
                                f(fg, fs if not isinstance(fg, int) else fg, fp)
                        if chained and (p, 1) in PE_AT:
                            chain(PE_AT[p, 1], g - 1, gs - 1)
                        ug, us, up, real = near(g, gs, p, -LAG)
                        if real:
                            aggregate(ug, us, up)

                run(pe, step)

            @block.scalar
            def _(act):
                def turned(g, p):
                    act.wait_ge(s_turn, g * GP + p + 1)
                    act.copy(ST[:, p % 2, :], pST[p % 2][:, 0:2 * P]).then_inc(s_ST, 1)

                def values(g, k, p):
                    act.wait_ge(s_g[p % R], arrived(g, p, R))
                    act.copy(vst[:, k, 2 * p:2 * p + 2, :], kv[:, p % R, :, D:2 * D]).then_inc(s_v, 1)

                def chain(n, h, b):
                    if n == 0:
                        act.wait_ge(s_cp, h * 6 + 1)
                        act.activation(X0[:, :], cA[0:HT, 0:P], ACT.Copy, scale=scale).then_inc(s_ca, 1)
                    elif n == 1:
                        act.wait_ge(s_cd, h * CD + 4)
                        act.activation(EX[:, :], Y[:, :], ACT.Exp).then_inc(s_ca, 1)
                    else:
                        act.wait_ge(s_cp, h * 6 + 6)
                        if not gat:
                            act.copy(alpha[:, b, :, :].rearrange("p h g -> p (h g)"), cA[:, 0:HT])
                        act.copy(fac[:, b, :, :].rearrange("p c g -> p (c g)"),
                                 cA[:, P:P + 2 * G]).then_inc(s_ca, 1)

                turned(0, 0)
                turned(0, 1)

                def step(g, gs):
                    for p in range(GP):
                        fg, _, fp, real = near(g, gs, p, 2)
                        if real:
                            turned(fg, fp)
                        if gs < NG and not gat:
                            values(g, gs % RG, p)
                        if 0 < gs <= NG and p in ACT_AT:
                            chain(ACT_AT[p], g - 1, (gs - 1) % RG)

                run(act, step)

            @block.vector
            def _(v):
                ini = Step(v, s_init)
                ini(v.memset(acc[:, :, :], 0.0))
                for t, value in ((wn, -BIG), (Rm, -BIG), (Lx, -BIG), (wg, 0.0), (Rs, 0.0), (Ls, 0.0)):
                    ini(v.memset(t[:, :, :], value))
                for t in (r3, r2):
                    ini(v.memset(t[:, :, :, :], 0.0))
                ini(v.memset(cn[:, :, :], 0.0))
                ini(v.memset(back_row[:, :, :], 0.0))
                ini(v.memset(col[:, :], 0.0))
                v.wait_ge(s_d0, 16)
                v.tensor_scalar(d0[:, :], d0[:, :], 0, N, ALU.max, ALU.min).then_inc(s_d0, 1)
                v.wait_ge(s_d0, 17)
                v.sem_inc(s_add, 2)

                def chain(n, h, b, own):
                    if n == 0:
                        v.wait_ge(s_ca, h * 3 + 1)
                        v.tensor_copy(M[:, :], cA[0:HT, P:P + 131]).then_inc(s_cd, 1)
                        own(v.tensor_scalar(NBm[:, :], cA[0:HT, P:P + 129], 1.0, BIG, ALU.subtract, ALU.mult))
                        if gat:
                            own(v.scalar_tensor_tensor(X[:, :], X0[:, :], 0.2, X0[:, :], ALU.mult, ALU.max))
                        v.tensor_tensor_scan(F[:, :], NBm[:, 0:P], X[:, :], -BIG, ALU.add, ALU.max).then_inc(s_cd, 1)
                    elif n == 1:
                        v.wait_ge(s_cp, h * 6 + 2)
                        v.tensor_copy(Lx[:, :, 0:1], Rm[:, :, G:G + 1])
                        own(v.tensor_copy(r3[:, :, :, :].rearrange("a c h g -> a (c h g)"), cB[0:1, 0:3 * HT]))
                        v.tensor_scalar(wn[:, :, 1:G + 1], r3[:, 2, :, :], 1.0, BIG, ALU.subtract, ALU.mult)
                        v.tensor_scalar(cn[:, :, :], r3[:, 1, :, :], 1.0, BIG, ALU.subtract, ALU.mult)
                        own(v.tensor_copy(Lx[:, :, 1:G + 1], r3[:, 0, :, :]))
                        own(v.tensor_tensor_scan(flat(Rm), flat(wn), flat(Lx), -BIG, ALU.add, ALU.max))
                        v.tensor_tensor(back_row[:, :, :], Rm[:, :, 0:G], cn[:, :, :], ALU.add).then_inc(s_cd, 1)
                    elif n == 2:
                        v.wait_ge(s_cp, h * 6 + 3)
                        own(v.tensor_copy(col[:, 0:1], cB[0:HT, 400:401]))
                        own(v.tensor_tensor_scan(F[:, :], NBm[:, 0:P], X[:, :], col[:, 0:1], ALU.add, ALU.max))
                        own(v.tensor_tensor_scan(B[:, ::-1], NBm[:, 128:0:-1], F[:, ::-1], -BIG, ALU.add, ALU.max))
                        v.tensor_tensor(Y[:, 128:129], col[:, 0:1], B[:, 0:1], ALU.subtract)
                        v.tensor_tensor(Y[:, 0:P], X[:, :], B[:, :], ALU.subtract).then_inc(s_cd, 1)
                    elif n == 3:
                        v.wait_ge(s_ca, h * 3 + 2)
                        v.tensor_tensor_scan(F[:, :], M[:, 0:P], EX[:, 0:P], 0.0, ALU.mult, ALU.add).then_inc(s_cd, 1)
                    elif n == 4:
                        v.wait_ge(s_cp, h * 6 + 4)
                        v.tensor_copy(Ls[:, :, 0:1], Rs[:, :, G:G + 1])
                        own(v.tensor_copy(r2[:, :, :, :].rearrange("a c h g -> a (c h g)"), cB[0:1, 0:2 * HT]))
                        v.tensor_tensor(wg[:, :, 1:G + 1], r3[:, 2, :, :], r2[:, 1, :, :], ALU.mult)
                        own(v.tensor_copy(Ls[:, :, 1:G + 1], r2[:, 0, :, :]))
                        own(v.tensor_tensor_scan(flat(Rs), flat(wg), flat(Ls), 0.0, ALU.mult, ALU.add))
                        v.tensor_tensor(back_row[:, :, :], Rs[:, :, 0:G], r2[:, 1, :, :], ALU.mult).then_inc(s_cd, 1)
                    elif n == 5:
                        v.wait_ge(s_cp, h * 6 + 5)
                        own(v.tensor_copy(col[:, 1:2], cB[0:HT, 400:401]))
                        own(v.tensor_tensor_scan(F[:, :], M[:, 0:P], EX[:, 0:P], col[:, 1:2], ALU.mult, ALU.add))
                        v.tensor_tensor_scan(B[:, ::-1], M[:, 128:0:-1], F[:, ::-1], 0.0,
                                             ALU.mult, ALU.max).then_inc(s_cn, 1)
                        own.n += 1
                        v.wait_ge(s_cn, own.base + own.n)
                        v.reciprocal(Y[:, 0:P], B[:, :]).then_inc(s_cn, 1)
                        v.wait_ge(s_cn, own.base + own.n + 1)
                        own.n += 1
                        v.tensor_scalar(Df[:, :], c.same[0:HT, :], col[:, 1:2], Y[:, 0:1], ALU.mult, ALU.mult)
                        v.tensor_tensor(AL[:, :], EX[:, 0:P], Y[:, 0:P], ALU.mult).then_inc(s_cd, 1)
                    elif n == 6:
                        v.wait_ge(s_ca, h * 3 + 3)
                        if gat:
                            v.tensor_tensor(alpha[:, b, :, :], cA[:, 0:HT].rearrange("p (h g) -> p h g", h=H),
                                            dist[:, b, :].unsqueeze(1).to_broadcast([P, H, G]),
                                            ALU.mult).then_inc(s_cd, 1)
                            v.wait_ge(s_cd, h * CD + CD)

                def onehot(g, gs, p):
                    k = gs % RG
                    if p == 0:
                        v.wait_ge(s_fl[k], use(g, gs) * (16 * NL))
                    v.tensor_tensor(S[:, k, 2 * p:2 * p + 2, :], c.iota[:, :].unsqueeze(1).to_broadcast([P, 2, P]),
                                    rel[:, k, 2 * p:2 * p + 2].unsqueeze(2).to_broadcast([P, 2, P]),
                                    ALU.is_equal).then_inc(s_S, 1)

                def products(g, k, p):
                    T = g * GP + p
                    v.wait_ge(s_g[p % R], arrived(g, p, R))
                    if gat:
                        v.wait_ge(s_qd, T + 1)
                        v.tensor_tensor(score[:, k, :, 2 * p:2 * p + 2].rearrange("p h i -> p i h"),
                                        vst[:, k, 2 * p:2 * p + 2, D:D + H],
                                        pqd[p % 2][:, 0:2 * H].rearrange("p (i h) -> p i h", i=2),
                                        ALU.add).then_inc(s_front, 1)
                    else:
                        wait(v, s_score, T)
                        v.wait_ge(s_qd, T + 1)
                        v.tensor_tensor(prod[:, :].rearrange("p (i d) -> p i d", i=2), kv[:, p % R, :, 0:D],
                                        pqd[p % 2][:, :].rearrange("p (i d) -> p i d", i=2),
                                        ALU.mult).then_inc(s_front, 1)

                def reduce(g, k, p):
                    v.wait_ge(s_front, g * GP + p + 1)
                    v.tensor_reduce(score[:, k, :, 2 * p:2 * p + 2].rearrange("p h i -> p i h"),
                                    prod[:, :].rearrange("p (i h o) -> p i h o", i=2, h=H),
                                    AX.X, ALU.add).then_inc(s_score, 1)

                def message(g, b, p):
                    if p == 0:
                        if gat:
                            v.wait_ge(s_cd, g * CD + CD)
                        else:
                            v.wait_ge(s_ca, g * 3 + 3)
                    v.tensor_tensor(msg[:, p % 2, :].rearrange("p (i h o) -> p i h o", i=2, h=H),
                                    vst[:, b, 2 * p:2 * p + 2, 0:D].rearrange("p i (h o) -> p i h o", h=H),
                                    alpha[:, b, :, 2 * p:2 * p + 2].rearrange("p h i -> p i h").unsqueeze(
                                        3).to_broadcast([P, 2, H, Dh]), ALU.mult).then_inc(s_msg, 1)

                first = [None]

                def rescale(g, b, p, i, fresh):
                    V, t = g * GP + p, 2 * p + i
                    if fresh or (p % 2 == 0 and i == 0):
                        first[0] = firsts(DVE_ENG, 2 * V - 2 * (p % 2))
                    n0 = first[0][2 * (p % 2) + i]
                    v.wait_ge(s_add, 2 * V + 2 + i)
                    v.tensor_tensor(acc[:, :, bass.ds(n0, 1)], acc[:, :, bass.ds(n0, 1)],
                                    fac[:, b, :, t:t + 1], ALU.mult).then_inc(s_mul, 1)

                def add(g, b, p, i):
                    V = g * GP + p
                    n0 = first[0][2 * (p % 2) + i]
                    if i == 0:
                        v.wait_ge(s_agg, V + 1)
                    v.wait_ge(s_mul, 2 * V + 1 + i)
                    n = bass.ds(n0, P)
                    v.tensor_tensor(acc[:, :, n], acc[:, :, n],
                                    pag[p % 2][:, i * D:i * D + D].rearrange("p (j r) -> p j r", j=2),
                                    ALU.add).then_inc(s_add, 1)

                for p in range(3):
                    onehot(0, 0, p)

                def step(g, gs):
                    own = Step(v, s_cn, (g - 1) * CN)
                    for p in range(GP):
                        k, front, chained = gs % RG, gs < NG, 0 < gs <= NG
                        vg, vk, vp, adds = near(g, gs, p, -LAG - 1)
                        ug, uk, up, sends = near(g, gs, p, -LAG)
                        if adds:
                            rescale(vg, vk, vp, 0, p == 0)
                        if adds:
                            add(vg, vk, vp, 0)
                        og, ok, op, ahead = near(g, gs, p, 3)
                        if ahead:
                            onehot(og, og if isinstance(og, int) else gs + (p + 3) // GP, op)
                        if front:
                            products(g, k, p)
                        if chained and (p, 0) in DVE_AT:
                            chain(DVE_AT[p, 0], g - 1, (gs - 1) % RG, own)
                        if adds:
                            rescale(vg, vk, vp, 1, False)
                        if sends:
                            message(ug, uk, up)
                        if adds:
                            add(vg, vk, vp, 1)
                        if front and not gat:
                            reduce(g, k, p)
                        if chained and (p, 1) in DVE_AT:
                            chain(DVE_AT[p, 1], g - 1, (gs - 1) % RG, own)

                run(v, step)


class Constants:

    def __init__(self, nc, m):
        s_c, s_p, s_o = sems(nc, "const", "dve", "pool", "own")
        self.ident = m.sb("ident", [P, P])
        self.iota = m.sb("iota", [P, P])
        self.one = m.sb("one", [P, 2])
        self.rep = m.sb("rep", [G, 8 * G])
        self.same = m.sb("same", [P, G])
        self.heads = {H: m.sb(f"heads{H}", [H * G, 2, P]) for H in (8, 4)}
        ints = m.sb("ints", [P, P], I32)
        with nc.Block() as block:

            @block.vector
            def _(v):
                own = Step(v, s_o)
                v.memset(self.one[:, :], 1.0)
                v.memset(self.ident[:, :], 1.0)
                for H in (8, 4):
                    v.memset(self.heads[H][:, :, :], 1.0)
                v.engine_nop().then_inc(s_c, 1)
                v.wait_ge(s_p, 6)
                v.tensor_copy(self.iota[:, :], ints[:, :])
                for h in range(8):
                    v.tensor_copy(self.rep[:, h * G:h * G + G], self.ident[0:G, 0:G])
                own(v.tensor_reduce(self.same[:, :], self.ident[:, :].rearrange("p (h t) -> p t h", t=G),
                                    AX.X, ALU.add))

            @block.gpsimd
            def _(pool):
                pool.wait_ge(s_c, 1)
                own = Step(pool, s_p)
                own(pool.affine_select(out=self.ident[:, :], in_=self.ident[:, :], compare_op=ALU.is_equal,
                                       fill=0.0, base=0, pattern=[[-1, P]], channel_multiplier=1))
                own(pool.iota(ints[:, :], [[1, P]], base=0, channel_multiplier=0))
                for H in (8, 4):
                    HH, Dh = H // 2, D // H
                    t = self.heads[H][:, :, :].rearrange("p j (a o) -> p j a o", a=HH)
                    own(pool.affine_select(out=t, in_=t, compare_op=ALU.is_ge, fill=0.0, base=0,
                                           pattern=[[-G * HH, 2], [-G, HH], [0, Dh]], channel_multiplier=1))
                    own(pool.affine_select(out=t, in_=t, compare_op=ALU.is_ge, fill=0.0, base=G - 1,
                                           pattern=[[G * HH, 2], [G, HH], [0, Dh]], channel_multiplier=-1))


def graph_norm(nc, c, dr, acc, w_out, b_out, gw, gb, gms):
    CH, SQ = 500, 2500
    NCH, NSQ, NBK = N // CH, N // SQ, 98
    (s_w, s_x0, s_x1, s_mm, s_h, s_own, s_mean, s_sq, s_std, s_sc, s_g, s_t, s_r0, s_r1, s_add, s_st0, s_st1) = sems(
        nc, "gn", "weights", "xT0", "xT1", "product", "h", "dve", "mean", "squares", "std", "scale",
        "gelu", "turned", "rows0", "rows1", "added", "stored0", "stored1")
    s_x, s_r, s_st = (s_x0, s_x1), (s_r0, s_r1), (s_st0, s_st1)
    with Scope(nc, "gn") as m:
        wo = m.sb("wo", [P, 2, D])
        vec = m.sb("vec", [P, 4, 2])
        xT = m.sb("xT", [P, 2, 2, CH])
        sums = m.sb("sums", [P, 2, NCH])
        squares = m.sb("squares", [P, 2, NSQ])
        junk = m.sb("junk", [P, SQ])
        st = m.sb("st", [P, 6, 2])
        eps = m.sb("eps", [P, 1])
        g = m.sb("g", [P, 2, 2, P])
        row = m.sb("row", [P, 2, D])
        ph = [m.ps(f"ph{i}", [P, 512]) for i in range(4)]
        pt = [m.ps(f"pt{i}", [P, 512]) for i in range(2)]
        with nc.Block() as block:

            @block.sync
            def _(sp):
                sp.dma_start(wo[:, :, :], w_out.rearrange("(c p) n -> p c n", p=P)).then_inc(s_w, 16)
                for j, a in enumerate((b_out, gw, gb, gms)):
                    sp.dma_start(vec[:, j, :], a.rearrange("(c p) -> p c", p=P),
                                 allow_slow_non_contiguous=True).then_inc(s_w, 16)
                for s in range(2):
                    sp.dma_start(xT[:, s, :, :], dr["xT"][:, :, s * CH:s * CH + CH]).then_inc(s_x[s], 16)
                with sp.Fori(0, (NCH - 3) // 2) as i:
                    for s in range(2):
                        b = 2 * i + s
                        sp.wait_ge(s_h, 2 * b + 4)
                        sp.dma_start(xT[:, s, :, :], dr["xT"][:, :, bass.ds((b + 2) * CH, CH)]).then_inc(s_x[s], 16)
                sp.wait_ge(s_h, 2 * NCH - 2)
                sp.dma_start(xT[:, 0, :, :], dr["xT"][:, :, (NCH - 1) * CH:NCH * CH]).then_inc(s_x[0], 16)
                for s in range(2):
                    sp.dma_start(row[:, s, :], dr["x"][s * P:s * P + P, :]).then_inc(s_r[s], 16)
                with sp.Fori(0, NBK // 2 - 1) as i:
                    for s in range(2):
                        b = 2 * i + s
                        sp.wait_ge(s_add, b + 3)
                        sp.dma_start(dr["x"][bass.ds(b * P, P), :], row[:, s, :]).then_inc(s_st[s], 16)
                        sp.wait_ge(s_st[s], i * 16 + 16)
                        sp.dma_start(row[:, s, :], dr["x"][bass.ds((b + 2) * P, P), :]).then_inc(s_r[s], 16)
                for s in range(2):
                    sp.wait_ge(s_add, NBK + 1 + s)
                    sp.dma_start(dr["x"][(NBK - 2 + s) * P:(NBK - 1 + s) * P, :], row[:, s, :]).then_inc(s_st[s], 16)
                for s in range(2):
                    sp.wait_ge(s_st[s], NBK // 2 * 16)

            @block.tensor
            def _(pe):
                pe.wait_ge(s_w, 80)

                def project(b, s):
                    if not isinstance(b, int):
                        pe.wait_ge(s_h, 2 * b)
                    for o in range(2):
                        for k in range(2):
                            t = pe.matmul(ph[2 * s + o][:, 0:CH], wo[:, k, o * P:o * P + P],
                                          acc[:, k, bass.ds(b * CH, CH)], start=(k == 0), stop=(k == 1))
                    t.then_inc(s_mm, 1)

                project(0, 0)
                with pe.Fori(0, (NCH - 1) // 2) as i:
                    project(2 * i + 1, 1)
                    project(2 * i + 2, 0)

                with pe.Fori(0, NBK // 2) as i:
                    for s in range(2):
                        b = 2 * i + s
                        pe.wait_ge(s_g, b + 1)
                        pe.wait_ge(s_add, b + 1)
                        for o in range(2):
                            t = pe.transpose(pt[s][:, o * P:o * P + P], g[:, s, o, :], c.ident[:, :])
                        t.then_inc(s_t, 1)

            @block.vector
            def _(v):
                v.memset(eps[:, :], EPS).then_inc(s_sc, 1)
                v.sem_inc(s_h, 2)
                v.sem_inc(s_add, 2)

                def add(b, s, k):
                    v.wait_ge(s_mm, b + 1)
                    v.wait_ge(s_x[s], k * 16 + 16)
                    for o in range(2):
                        n = bass.ds(b * CH, CH)
                        v.scalar_tensor_tensor(acc[:, o, n], ph[2 * s + o][:, 0:CH], vec[:, 0, o:o + 1],
                                               xT[:, s, o, :], ALU.add, ALU.add).then_inc(s_h, 1)
                        v.wait_ge(s_h, 2 * b + o + 3)
                        v.tensor_reduce(sums[:, o, bass.ds(b, 1)], acc[:, o, n], AX.X, ALU.add).then_inc(s_own, 1)

                v.wait_ge(s_w, 80)
                add(0, 0, 0)
                with v.Fori(0, (NCH - 1) // 2) as i:
                    add(2 * i + 1, 1, i)
                    add(2 * i + 2, 0, i + 1)
                v.wait_ge(s_own, 2 * NCH)
                own = Step(v, s_own, 2 * NCH)
                own(v.tensor_reduce(st[:, 1, :], sums[:, :, :], AX.X, ALU.add))
                v.scalar_tensor_tensor(st[:, 0, :], st[:, 1, :], -1.0 / N, vec[:, 3, :],
                                       ALU.mult, ALU.mult).then_inc(s_mean, 1)
                v.wait_ge(s_sq, 2 * NSQ)
                own(v.tensor_reduce(st[:, 1, :], squares[:, :, :], AX.X, ALU.add))
                v.tensor_scalar(st[:, 2, :], st[:, 1, :], 1.0 / N, None, ALU.mult).then_inc(s_sc, 1)
                v.wait_ge(s_std, 1)
                own(v.reciprocal(st[:, 3, :], st[:, 1, :]))
                own(v.tensor_tensor(st[:, 4, :], st[:, 3, :], vec[:, 1, :], ALU.mult))
                own(v.tensor_tensor(st[:, 5, :], st[:, 4, :], st[:, 0, :], ALU.mult))
                v.tensor_tensor(st[:, 5, :], st[:, 5, :], vec[:, 2, :], ALU.add).then_inc(s_sc, 1)
                with v.Fori(0, NBK // 2) as i:
                    for s in range(2):
                        b = 2 * i + s
                        v.wait_ge(s_t, b + 1)
                        v.wait_ge(s_r[s], i * 16 + 16)
                        v.tensor_tensor(row[:, s, :], row[:, s, :], pt[s][:, 0:D], ALU.add).then_inc(s_add, 1)

            @block.scalar
            def _(act):
                act.wait_ge(s_mean, 1)
                for o in range(2):
                    for q in range(NSQ):
                        if o + q:
                            act.wait_ge(s_sq, o * NSQ + q)
                        act.activation(junk[:, :], acc[:, o, q * SQ:q * SQ + SQ], ACT.Square, bias=st[:, 0, o:o + 1],
                                       accum_out=squares[:, o, q:q + 1]).then_inc(s_sq, 1)
                act.wait_ge(s_sc, 2)
                act.activation(st[:, 1, :], st[:, 2, :], ACT.Sqrt, bias=eps[:, 0:1]).then_inc(s_std, 1)
                act.wait_ge(s_sc, 3)

                def gelu(i, s):
                    b = 2 * i + s
                    if not isinstance(i, int):
                        act.wait_ge(s_t, b - 1)
                    for o in range(2):
                        t = act.activation(g[:, s, o, :], acc[:, o, bass.ds(b * P, P)], ACT.Gelu,
                                           bias=st[:, 5, o:o + 1], scale=st[:, 4, o:o + 1])
                    t.then_inc(s_g, 1)

                for s in range(2):
                    gelu(0, s)
                with act.Fori(1, NBK // 2) as i:
                    for s in range(2):
                        gelu(i, s)


def moe_top2(nc, c, dr, router_w, w1, b1, w2, b2):
    SBW, NSB = 256, NR // 256
    (s_w, s_c, s_x0, s_x1, s_own, s_bn, s_sd, s_ln, s_tp, s_xT, s_lg, s_ex, s_pr, s_cT, s_cS, s_m1, s_h, s_m2,
     s_y, s_yf, s_st0, s_st1, s_b0, s_go) = sems(
        nc, "top2", "weights", "consts", "rows0", "rows1", "dve", "stats", "std", "normed", "turned", "xT",
        "logits", "exp", "probs", "combT", "combS", "hidden_sums", "hidden", "expert_sums", "weighted",
        "started", "stored0", "stored1", "router", "go")
    s_x, s_st = (s_x0, s_x1), (s_st0, s_st1)
    with Scope(nc, "top2") as m:
        rw = m.sb("rw", [P, 2, 8])
        rw8 = m.sb("rw8", [8, D])
        W1 = m.sb("w1", [P, 8, 2, D])
        W2 = m.sb("w2", [P, 8, 2, D])
        B1 = m.sb("b1", [P, 8, 2])
        B2 = m.sb("b2", [8, D])
        eps = m.sb("eps", [P, 1])
        x = m.sb("x", [P, 2, 2, D])
        st = m.sb("st", [P, 2, 6])
        mv = m.sb("mv", [P, 2, 2])
        sd = m.sb("sd", [P, 2, 2])
        ln = m.sb("ln", [P, 2, 2, D])
        xT = m.sb("xT", [P, 2, 2, SBW])
        lg = m.sb("lg", [P, 2, 8])
        pr = m.sb("pr", [P, 2, 8])
        e1 = m.sb("e1", [P, 2, 8])
        k1 = m.sb("k1", [P, 2, 8])
        k2 = m.sb("k2", [P, 2, 8])
        p2 = m.sb("p2", [P, 2, 8])
        i8 = m.sb("i8", [P, 2, 8])
        sc = m.sb("sc", [P, 8, 2])
        comb = m.sb("comb", [P, 2, 2, 8])
        cT = m.sb("cT", [8, 2, 2, P])
        hT = m.sb("hT", [P, 2, 2, SBW])
        y = m.sb("y", [P, 2, 2, D])
        pT = m.ps("pT", [P, 512])
        pr_ = m.ps("pr_", [P, 512])
        ph = [m.ps(f"ph{i}", [P, 512]) for i in range(2)]
        py = [m.ps(f"py{i}", [P, 512]) for i in range(2)]
        pb = m.ps("pb", [P, 512])
        rows = lambda b: dr["x"][bass.ds(b * SBW, SBW), :].rearrange("(k p) d -> p k d", p=P)
        CV = 23

        def run(eng, front, experts):
            front(0, 0, 0)

            def both(b, s, *following):
                experts(b, s, range(0, 4))
                if following:
                    front(*following)
                experts(b, s, range(4, 8))

            with eng.Fori(0, NSB // 2 - 1) as i:
                both(2 * i, 0, 2 * i + 1, 1, i)
                both(2 * i + 1, 1, 2 * i + 2, 0, i + 1)
            both(NSB - 2, 0, NSB - 1, 1, NSB // 2 - 1)
            both(NSB - 1, 1)

        def wait(eng, sem, value):
            if not isinstance(value, int) or value > 0:
                eng.wait_ge(sem, value)

        with nc.Block() as block:

            @block.sync
            def _(sp):
                sp.dma_start(rw8[:, :], router_w).then_inc(s_w, 16)
                sp.dma_start(B1[:, :, :], b1.rearrange("e (c p) -> p e c", p=P),
                             allow_slow_non_contiguous=True).then_inc(s_w, 16)
                sp.dma_start(B2[:, :], b2).then_inc(s_w, 16)
                for e in range(8):
                    sp.dma_start(W1[:, e, :, :], w1[e].rearrange("(c p) n -> p c n", p=P)).then_inc(s_w, 16)
                    sp.dma_start(W2[:, e, :, :], w2[e].rearrange("(c p) n -> p c n", p=P)).then_inc(s_w, 16)
                for s in range(2):
                    sp.dma_start(x[:, s, :, :], rows(s)).then_inc(s_x[s], 16)
                    sp.sem_inc(s_st[s], 16)

                def store(b, s):
                    sp.wait_ge(s_y, b * 16 + 18)
                    sp.dma_start(rows(b), y[:, s, :, :]).then_inc(s_st[s], 16)

                with sp.Fori(0, NSB // 2 - 1) as i:
                    for s in range(2):
                        b = 2 * i + s
                        store(b, s)
                        sp.dma_start(x[:, s, :, :], rows(b + 2)).then_inc(s_x[s], 16)
                for s in range(2):
                    store(NSB - 2 + s, s)
                for s in range(2):
                    sp.wait_ge(s_st[s], NSB // 2 * 16 + 16)

            @block.vector
            def _(v):
                v.memset(eps[:, :], EPS).then_inc(s_c, 1)
                v.tensor_scalar(i8[:, 0, :], c.iota[:, 0:8], 8.0, None, ALU.subtract)
                v.tensor_scalar(i8[:, 1, :], c.iota[:, 0:8], 8.0, None, ALU.subtract).then_inc(s_c, 1)
                v.sem_inc(s_y, 2)
                v.wait_ge(s_b0, 1)
                v.tensor_copy(rw[:, :, :].rearrange("p c e -> p (c e)"), pr_[:, 0:16]).then_inc(s_c, 1)

                def front(b, s, u):
                    own = Step(v, s_own, b * CV)
                    for k in range(2):
                        if k == 0:
                            v.wait_ge(s_x[s], u * 16 + 16)
                        own(v.bn_stats(st[:, k, :], x[:, s, k, :]))
                        v.sem_inc(s_go, 1)
                        v.bn_aggr(mv[:, k, :], st[:, k, :]).then_inc(s_bn, 1)
                    v.wait_ge(s_sd, b + 1)
                    own(v.reciprocal(sd[:, :, 1], sd[:, :, 0]))
                    for k in range(2):
                        own(v.tensor_scalar(ln[:, s, k, :], x[:, s, k, :], mv[:, k, 0:1], sd[:, k, 1:2],
                                            ALU.subtract, ALU.mult))
                    v.sem_inc(s_ln, 1)
                    bc = lambda t: t.unsqueeze(2).to_broadcast([P, 2, 8])
                    v.wait_ge(s_lg, b + 1)
                    own(v.tensor_copy(lg[:, :, :].rearrange("p k e -> p (k e)"), pr_[:, 0:16]))
                    own(v.tensor_reduce(sc[:, 0, :], lg[:, :, :], AX.X, ALU.max))
                    v.tensor_tensor(lg[:, :, :], lg[:, :, :], bc(sc[:, 0, :]), ALU.subtract).then_inc(s_pr, 1)
                    v.wait_ge(s_ex, b + 1)
                    own(v.tensor_reduce(sc[:, 1, :], e1[:, :, :], AX.X, ALU.add))
                    own(v.reciprocal(sc[:, 2, :], sc[:, 1, :]))
                    own(v.tensor_tensor(pr[:, :, :], e1[:, :, :], bc(sc[:, 2, :]), ALU.mult))
                    own(v.tensor_reduce(sc[:, 3, :], pr[:, :, :], AX.X, ALU.max))
                    own(v.tensor_tensor(k1[:, :, :], pr[:, :, :], bc(sc[:, 3, :]), ALU.is_equal))
                    own(v.tensor_tensor(k2[:, :, :], k1[:, :, :], i8[:, :, :], ALU.mult))
                    own(v.tensor_reduce(sc[:, 4, :], k2[:, :, :], AX.X, ALU.min))
                    own(v.tensor_tensor(k1[:, :, :], i8[:, :, :], bc(sc[:, 4, :]), ALU.is_equal))
                    own(v.scalar_tensor_tensor(p2[:, :, :], k1[:, :, :], -4.0, pr[:, :, :], ALU.mult, ALU.add))
                    own(v.tensor_reduce(sc[:, 5, :], p2[:, :, :], AX.X, ALU.max))
                    own(v.tensor_tensor(p2[:, :, :], p2[:, :, :], bc(sc[:, 5, :]), ALU.is_equal))
                    own(v.tensor_tensor(p2[:, :, :], p2[:, :, :], i8[:, :, :], ALU.mult))
                    own(v.tensor_reduce(sc[:, 4, :], p2[:, :, :], AX.X, ALU.min))
                    own(v.tensor_tensor(k2[:, :, :], i8[:, :, :], bc(sc[:, 4, :]), ALU.is_equal))
                    own(v.tensor_tensor(k1[:, :, :], k1[:, :, :], k2[:, :, :], ALU.add))
                    v.tensor_tensor(sc[:, 6, :], sc[:, 3, :], sc[:, 5, :], ALU.add).then_inc(s_pr, 1)
                    v.wait_ge(s_pr, b * 5 + 2)
                    v.tensor_scalar(sc[:, 6, :], sc[:, 6, :], 1e-12, None, ALU.max).then_inc(s_pr, 1)
                    v.wait_ge(s_pr, b * 5 + 3)
                    v.reciprocal(sc[:, 7, :], sc[:, 6, :]).then_inc(s_pr, 1)
                    v.wait_ge(s_pr, b * 5 + 4)
                    own(v.tensor_tensor(k1[:, :, :], k1[:, :, :], bc(sc[:, 7, :]), ALU.mult))
                    v.tensor_tensor(comb[:, s, :, :], k1[:, :, :], pr[:, :, :], ALU.mult).then_inc(s_pr, 1)
                    v.wait_ge(s_pr, b * 5 + 5)
                    v.wait_ge(s_cT, 2 * b + 1)
                    v.tensor_copy(cT[:, s, :, :].rearrange("e k p -> e (k p)"), pr_[0:8, 256:512]).then_inc(s_cS, 1)
                    v.wait_ge(s_st[s], u * 16 + 16)
                    v.tensor_tensor(y[:, s, :, :], x[:, s, :, :], ln[:, s, :, :], ALU.add).then_inc(s_yf, 1)
                    v.wait_ge(s_yf, 2 * b + 1)
                    v.wait_ge(s_cT, 2 * b + 2)
                    v.tensor_tensor(y[:, s, :, :].rearrange("p k d -> p (k d)"),
                                    y[:, s, :, :].rearrange("p k d -> p (k d)"), pb[:, :], ALU.add).then_inc(s_yf, 1)
                    assert own.n == CV, own.n

                def experts(b, s, which):
                    for e in which:
                        for k in range(2):
                            v.wait_ge(s_m2, (b * 8 + e) * 2 + k + 5)
                            if e:
                                v.wait_ge(s_y, (b * 8 + e) * 2 + k + 1)
                            else:
                                v.wait_ge(s_yf, 2 * b + 2)
                            v.scalar_tensor_tensor(y[:, s, k, :], py[k][:, 0:D], comb[:, s, k, e:e + 1],
                                                   y[:, s, k, :], ALU.mult, ALU.add).then_inc(s_y, 1)

                run(v, front, experts)

            @block.scalar
            def _(act):
                act.wait_ge(s_c, 2)
                act.sem_inc(s_h, 2)
                act.sem_inc(s_m2, 4)
                act.wait_ge(s_w, 16 * 19)

                def front(b, s, u):
                    act.wait_ge(s_bn, 2 * b + 2)
                    act.activation(sd[:, :, 0], mv[:, :, 1], ACT.Sqrt, bias=eps[:, 0:1]).then_inc(s_sd, 1)
                    for k in range(2):
                        act.wait_ge(s_tp, 2 * b + k + 1)
                        act.copy(xT[:, s, :, k * P:k * P + P],
                                 pT[:, 0:D].rearrange("p (c n) -> p c n", c=2)).then_inc(s_xT, 1)
                    act.wait_ge(s_pr, b * 5 + 1)
                    act.activation(e1[:, :, :], lg[:, :, :], ACT.Exp).then_inc(s_ex, 1)

                def experts(b, s, which):
                    for e in which:
                        act.wait_ge(s_m1, b * 8 + e + 1)
                        act.wait_ge(s_m2, (b * 8 + e) * 2 + 2)
                        for f in range(2):
                            t = act.activation(hT[:, e % 2, f, :], ph[e % 2][:, f * SBW:f * SBW + SBW], ACT.Gelu,
                                               bias=B1[:, e, f:f + 1])
                        t.then_inc(s_h, 1)

                run(act, front, experts)

            @block.tensor
            def _(pe):
                pe.wait_ge(s_w, 16 * 19)
                for k in range(2):
                    t = pe.transpose(pr_[:, k * 8:k * 8 + 8], rw8[:, k * P:k * P + P], c.ident[0:8, 0:8])
                t.then_inc(s_b0, 1)
                pe.wait_ge(s_c, 3)

                def front(b, s, u):
                    pe.wait_ge(s_ln, b + 1)
                    for k in range(2):
                        wait(pe, s_xT, 2 * b + k)
                        for j in range(2):
                            t = pe.transpose(pT[:, j * P:j * P + P], ln[:, s, k, j * P:j * P + P], c.ident[:, :])
                        t.then_inc(s_tp, 1)
                    pe.wait_ge(s_xT, 2 * b + 2)
                    for k in range(2):
                        for j in range(2):
                            t = pe.matmul(pr_[:, k * 8:k * 8 + 8], xT[:, s, j, k * P:k * P + P], rw[:, j, :],
                                          start=(j == 0), stop=(j == 1))
                    t.then_inc(s_lg, 1)
                    pe.wait_ge(s_pr, b * 5 + 5)
                    for k in range(2):
                        t = pe.transpose(pr_[0:8, 256 + k * P:256 + k * P + P], comb[:, s, k, :], c.ident[:, :])
                    t.then_inc(s_cT, 1)
                    pe.wait_ge(s_cS, b + 1)
                    for k in range(2):
                        t = pe.matmul(pb[:, k * D:k * D + D], cT[:, s, k, :], B2[:, :], start=True, stop=True)
                    t.then_inc(s_cT, 1)

                def experts(b, s, which):
                    def first(e):
                        pe.wait_ge(s_h, b * 8 + e + 1)
                        for f in range(2):
                            for j in range(2):
                                t = pe.matmul(ph[e % 2][:, f * SBW:f * SBW + SBW], W1[:, e, j, f * P:f * P + P],
                                              xT[:, s, j, :], start=(j == 0), stop=(j == 1))
                        t.then_inc(s_m1, 1)

                    def second(e):
                        pe.wait_ge(s_h, b * 8 + e + 3)
                        for k in range(2):
                            pe.wait_ge(s_y, (b * 8 + e) * 2 + k + 1)
                            for j in range(2):
                                t = pe.matmul(py[k][:, 0:D], hT[:, e % 2, j, k * P:k * P + P], W2[:, e, j, :],
                                              start=(j == 0), stop=(j == 1))
                            t.then_inc(s_m2, 1)

                    for e in which:
                        if e % 4 == 0:
                            first(e)
                        if e % 4 < 3:
                            first(e + 1)
                        second(e)

                run(pe, front, experts)


def moe_switch(nc, c, dr, gate_b, w1, b1, w2, b2, out):
    NBK, FULL, EXP, FF = (N + P - 1) // P, N // P, 8, 1024
    CAP = -(-(5 * N) // (4 * EXP))
    ROWS = -(-CAP // 512) * 512
    SPE = ROWS // 512
    BIGI = float(1 << 20)
    (s_ld, s_c, s_own, s_ex, s_cnt, s_pl, s_zero, s_l0, s_l1, s_i, s_sc0, s_sc1, s_scx,
     s_w0, s_w1, s_r0, s_r1, s_t, s_tx, s_m1, s_h, s_m2, s_y, s_ys0, s_ys1,
     s_g0, s_g1, s_x0, s_x1, s_gi, s_o, s_st0, s_st1, s_nn, s_go) = sems(
        nc, "switch", "loaded", "consts", "dve", "exp", "counts", "pool", "zeroed", "rows0", "rows1", "index",
        "scattered0", "scattered1", "x",
        "weights0", "weights1", "buf0", "buf1", "turned", "copied", "hidden_sums", "hidden", "sums", "y",
        "ystored0", "ystored1", "gathered0", "gathered1", "x0", "x1", "gindex", "result", "stored0", "stored1", "nan", "go")
    s_l, s_sc, s_w, s_r, s_ys, s_g, s_x, s_st = ((s_l0, s_l1), (s_sc0, s_sc1), (s_w0, s_w1), (s_r0, s_r1),
                                                (s_ys0, s_ys1), (s_g0, s_g1), (s_x0, s_x1), (s_st0, s_st1))
    with Scope(nc, "switch") as top:
        sslot = top.sb("sslot", [P, NBK], I32)
        gslot = top.sb("gslot", [P, NBK], I32)
        wgt = top.sb("wgt", [P, NBK])
        flat = lambda t: t[:, :, :].rearrange("p b e -> p (b e)")
        with Scope(nc, "assign") as m:
            lg = m.sb("lg", [P, NBK, 8])
            gb = m.sb("gb", [P, 8])
            i8 = m.sb("i8", [P, 8])
            valid = m.sb("valid", [P, NBK])
            upto = m.sb("upto", [P, P])
            ones = m.sb("ones", [P, P])
            nil = m.sb("nil", [P, NBK])
            ex = m.sb("ex", [P, NBK, 8])
            oh = m.sb("oh", [P, NBK, 8])
            tt = m.sb("tt", [P, NBK, 8])
            tot = m.sb("tot", [P, 8, NBK])
            inc = m.sb("inc", [P, 8, NBK])
            a = m.sb("a", [P, 8, NBK])
            pw = [m.ps(f"pw{i}", [P, 512]) for i in range(2)]
            pt = [m.ps(f"pt{i}", [P, 512]) for i in range(2)]
            HB = NBK // 2
            assert NBK % 2 == 0
            with nc.Block() as block:

                @block.sync
                def _(sp):
                    sp.dma_start(lg[:, :, :], dr["logits"][0:NBK * P, :].rearrange(
                        "(b p) e -> p b e", p=P)).then_inc(s_ld, 16)
                    sp.dma_start(gb[:, :], gate_b.rearrange("(a e) -> a e", a=1).to_broadcast([P, 8])).then_inc(s_ld, 16)

                @block.gpsimd
                def _(pool):
                    pool.wait_ge(s_c, 1)
                    pool.affine_select(out=upto[:, :], in_=upto[:, :], compare_op=ALU.is_ge, fill=0.0, base=0,
                                       pattern=[[1, P]], channel_multiplier=-1)
                    pool.affine_select(out=valid[:, NBK - 1:NBK], in_=valid[:, NBK - 1:NBK], compare_op=ALU.is_ge,
                                       fill=0.0, base=N - FULL * P - 1, pattern=[[0, 1]],
                                       channel_multiplier=-1).then_inc(s_pl, 1)

                @block.scalar
                def _(act):
                    act.wait_ge(s_own, 4)
                    act.activation(ex[:, :, :], tt[:, :, :], ACT.Exp).then_inc(s_ex, 1)

                @block.tensor
                def _(pe):
                    pe.wait_ge(s_cnt, 1)
                    for i in range(2):
                        cols = oh[:, i * HB:i * HB + HB, :].rearrange("p b e -> p (b e)")
                        pe.matmul(pw[i][:, 0:HB * 8], upto[:, :], cols, start=True, stop=True)
                        t = pe.matmul(pt[i][:, 0:HB * 8], ones[:, :], cols, start=True, stop=True)
                    t.then_inc(s_cnt, 1)

                @block.vector
                def _(v):
                    bc = lambda t: t.unsqueeze(2).to_broadcast([P, NBK, 8])
                    row8 = lambda t: t[:, :].unsqueeze(1).to_broadcast([P, NBK, 8])
                    v.memset(upto[:, :], 1.0)
                    v.memset(ones[:, :], 1.0)
                    v.memset(nil[:, :], 0.0)
                    v.memset(valid[:, :], 1.0).then_inc(s_c, 1)
                    own = Step(v, s_own)
                    own(v.tensor_scalar(i8[:, :], c.iota[:, 0:8], 8.0, None, ALU.subtract))
                    v.wait_ge(s_ld, 32)
                    own(v.tensor_tensor(lg[:, :, :], lg[:, :, :], row8(gb), ALU.add))
                    own(v.tensor_reduce(a[:, 0, :], lg[:, :, :], AX.X, ALU.max))
                    own(v.tensor_tensor(tt[:, :, :], lg[:, :, :], bc(a[:, 0, :]), ALU.subtract))
                    v.wait_ge(s_ex, 1)
                    own(v.tensor_reduce(a[:, 1, :], ex[:, :, :], AX.X, ALU.add))
                    own(v.reciprocal(a[:, 2, :], a[:, 1, :]))
                    own(v.tensor_tensor(lg[:, :, :], ex[:, :, :], bc(a[:, 2, :]), ALU.mult))
                    own(v.tensor_reduce(a[:, 3, :], lg[:, :, :], AX.X, ALU.max))
                    own(v.tensor_tensor(tt[:, :, :], lg[:, :, :], bc(a[:, 3, :]), ALU.is_equal))
                    own(v.tensor_tensor(tt[:, :, :], tt[:, :, :], row8(i8), ALU.mult))
                    own(v.tensor_reduce(a[:, 4, :], tt[:, :, :], AX.X, ALU.min))
                    own(v.tensor_tensor(oh[:, :, :], row8(i8), bc(a[:, 4, :]), ALU.is_equal))
                    v.wait_ge(s_pl, 1)
                    v.tensor_tensor(oh[:, :, :], oh[:, :, :], bc(valid[:, :]), ALU.mult).then_inc(s_cnt, 1)
                    v.wait_ge(s_cnt, 2)
                    for i in range(2):
                        own(v.tensor_copy(tot[:, :, i * HB:i * HB + HB].rearrange("p e b -> p b e"),
                                          pt[i][:, 0:HB * 8].rearrange("p (b e) -> p b e", e=8)))
                    for e in range(8):
                        own(v.tensor_tensor_scan(inc[:, e, :], nil[:, :], tot[:, e, :], 0.0, ALU.add, ALU.add))
                    own(v.tensor_tensor(inc[:, :, :], inc[:, :, :], tot[:, :, :], ALU.subtract))
                    for i in range(2):
                        bl = slice(i * HB, i * HB + HB)
                        own(v.tensor_tensor(tt[:, bl, :], inc[:, :, bl].rearrange("p e b -> p b e"),
                                            pw[i][:, 0:HB * 8].rearrange("p (b e) -> p b e", e=8), ALU.add))
                    own(v.tensor_tensor(tt[:, :, :], tt[:, :, :], oh[:, :, :], ALU.mult))
                    own(v.tensor_reduce(a[:, 5, :], tt[:, :, :], AX.X, ALU.add))
                    own(v.tensor_scalar(a[:, 6, :], a[:, 5, :], float(CAP), None, ALU.is_le))
                    own(v.tensor_tensor(a[:, 6, :], a[:, 6, :], valid[:, :], ALU.mult))
                    own(v.tensor_tensor(wgt[:, :], a[:, 3, :], a[:, 6, :], ALU.mult))
                    own(v.tensor_scalar(a[:, 4, :], a[:, 4, :], float(ROWS), 8.0 * ROWS - 1.0, ALU.mult, ALU.add))
                    own(v.tensor_tensor(a[:, 0, :], a[:, 4, :], a[:, 5, :], ALU.add))
                    own(v.tensor_scalar(a[:, 6, :], a[:, 6, :], -BIGI, BIGI, ALU.mult, ALU.add))
                    own(v.tensor_tensor(a[:, 0, :], a[:, 0, :], a[:, 6, :], ALU.add))
                    own(v.tensor_copy(sslot[:, :], a[:, 0, :]))
                    own(v.tensor_scalar(a[:, 5, :], a[:, 5, :], 1.0, float(CAP), ALU.max, ALU.min))
                    own(v.tensor_tensor(a[:, 5, :], a[:, 5, :], a[:, 4, :], ALU.add))
                    own(v.tensor_copy(gslot[:, :], a[:, 5, :]))
                    v.sem_inc(s_i, 1)

        with Scope(nc, "scatter") as m:
            zero = m.sb("zero", [P, 4 * D])
            row = m.sb("row", [P, 2, D])
            slot = m.sb("slot", [P, 2, 2], I32)
            with nc.Block() as block:

                @block.vector
                def _(v):
                    v.memset(zero[:, :], 0.0).then_inc(s_zero, 1)
                    for s in range(2):
                        v.tensor_copy(slot[:, s, 0:1], sslot[:, s:s + 1]).then_inc(s_i, 1)
                    with v.Fori(1, NBK // 2) as i:
                        for s in range(2):
                            v.wait_ge(s_sc[s], i * 16)
                            v.tensor_copy(slot[:, s, 0:1], sslot[:, bass.ds(2 * i + s, 1)]).then_inc(s_i, 1)

                @block.scalar
                def _(act):
                    act.wait_ge(s_zero, 1)
                    with act.Fori(0, EXP * ROWS // 512) as i:
                        act.dma_start(dr["buf"][bass.ds(i * 512, 512), :].rearrange("(p r) d -> p (r d)", p=P),
                                      zero[:, :]).then_inc(s_zero, 16)

                @block.sync
                def _(sp):
                    for s in range(2):
                        sp.dma_start(row[:, s, :], dr["ln"][s * P:s * P + P, :]).then_inc(s_l[s], 16)
                    with sp.Fori(1, NBK // 2) as i:
                        for s in range(2):
                            sp.wait_ge(s_sc[s], i * 16)
                            sp.dma_start(row[:, s, :], dr["ln"][bass.ds((2 * i + s) * P, P), :]).then_inc(s_l[s], 16)

                @block.gpsimd
                def _(pool):
                    pool.wait_ge(s_zero, 1 + 16 * (EXP * ROWS // 512))
                    with pool.Fori(0, NBK // 2) as i:
                        for s in range(2):
                            pool.wait_ge(s_l[s], i * 16 + 16)
                            pool.wait_ge(s_i, 2 * i + s + 2)
                            pool.sem_inc(s_scx, 1)
                            pool.indirect_dma_start(dr["buf"], IndirectOffsetOnAxis(ap=slot[:, s, 0:1], axis=0),
                                                    row[:, s, :], None, bounds_check=EXP * ROWS - 1,
                                                    oob_is_err=False).then_inc(s_sc[s], 16)
                    for s in range(2):
                        pool.wait_ge(s_sc[s], NBK // 2 * 16)

        with Scope(nc, "experts") as m:
            W1 = m.sb("w1", [P, 2, 2, FF])
            W2 = m.sb("w2", [P, 2, 8, D])
            B1 = m.sb("b1", [P, 2, 8])
            B2 = m.sb("b2", [P, 2, D])
            row = m.sb("row", [P, 2, 4, D])
            xT = m.sb("xT", [P, 2, 2, 512])
            hT = m.sb("hT", [P, 2, 8, 512])
            y = m.sb("y", [P, 2, 4, D])
            pT = [m.ps(f"pT{i}", [P, 512]) for i in range(2)]
            ph = [m.ps(f"ph{i}", [P, 512]) for i in range(2)]
            py = [m.ps(f"py{i}", [P, 512]) for i in range(2)]
            assert SPE == 4
            NSUP = EXP * SPE
            rows = lambda t, n: dr[t][bass.ds(n * 512, 512), :].rearrange("(k p) d -> p k d", p=P)

            def weights(sp, e, s):
                ex_ = lambda a: a[bass.ds(e, 1)]
                sp.dma_start(W1[:, s, :, :], ex_(w1).rearrange("e (c p) n -> (e p) c n", p=P)).then_inc(s_w[s], 16)
                sp.dma_start(W2[:, s, :, :], ex_(w2).rearrange("e (c p) n -> (e p) c n", p=P)).then_inc(s_w[s], 16)
                sp.dma_start(B1[:, s, :], ex_(b1).rearrange("e (c p) -> (e p) c", p=P),
                             allow_slow_non_contiguous=True).then_inc(s_w[s], 16)
                sp.dma_start(B2[:, s, :], ex_(b2).to_broadcast([P, D])).then_inc(s_w[s], 16)

            with nc.Block() as block:

                @block.sync
                def _(sp):
                    sp.wait_ge(s_sc[0], NBK // 2 * 16)
                    sp.wait_ge(s_sc[1], NBK // 2 * 16)
                    for s in range(2):
                        weights(sp, s, s)
                        sp.dma_start(row[:, s, :, :], rows("buf", s)).then_inc(s_r[s], 16)
                        sp.sem_inc(s_ys[s], 16)

                    def pair(i, s, q, load):
                        n = (2 * i + s) * SPE + q
                        if load:
                            sp.wait_ge(s_t, n * 4 + 4)
                            sp.dma_start(row[:, q % 2, :, :], rows("buf", n + 2)).then_inc(s_r[q % 2], 16)
                        sp.wait_ge(s_y, n * 8 + 12)
                        sp.dma_start(rows("ybuf", n), y[:, q % 2, :, :]).then_inc(s_ys[q % 2], 16)

                    with sp.Fori(0, EXP // 2 - 1) as i:
                        for s in range(2):
                            for q in range(SPE):
                                pair(i, s, q, True)
                            weights(sp, 2 * i + s + 2, s)
                    for s in range(2):
                        for q in range(SPE):
                            pair(EXP // 2 - 1, s, q, s * SPE + q < 2 * SPE - 2)
                    for s in range(2):
                        sp.wait_ge(s_ys[s], NSUP // 2 * 16 + 16)

                def loop(eng, body):
                    with eng.Fori(0, EXP // 2) as i:
                        for s in range(2):
                            for q in range(SPE):
                                body(i, s, q, (2 * i + s) * SPE + q)

                @block.tensor
                def _(pe):
                    def body(i, s, q, n):
                        pe.wait_ge(s_r[q % 2], (2 * SPE * i + SPE * s + q - q % 2) * 8 + 16)
                        for k in range(4):
                            pe.wait_ge(s_tx, n * 4 + k + 1)
                            for j in range(2):
                                t = pe.transpose(pT[k % 2][:, j * P:j * P + P], row[:, q % 2, k, j * P:j * P + P],
                                                 c.ident[:, :])
                            t.then_inc(s_t, 1)
                        if q == 0:
                            pe.wait_ge(s_w[s], i * 64 + 64)
                        pe.wait_ge(s_tx, n * 4 + 6)
                        for f in range(8):
                            pe.wait_ge(s_h, n * 8 + f + 1)
                            for j in range(2):
                                t = pe.matmul(ph[f % 2][:, :], W1[:, s, j, f * P:f * P + P], xT[:, q % 2, j, :],
                                              start=(j == 0), stop=(j == 1))
                            t.then_inc(s_m1, 1)
                        for k in range(4):
                            pe.wait_ge(s_y, n * 8 + 2 * k + 2)
                            for f in range(8):
                                if k == 0:
                                    pe.wait_ge(s_h, n * 8 + f + 3)
                                t = pe.matmul(py[k % 2][:, 0:D], hT[:, q % 2, f, k * P:k * P + P], W2[:, s, f, :],
                                              start=(f == 0), stop=(f == 7))
                            t.then_inc(s_m2, 1)

                    loop(pe, body)

                @block.scalar
                def _(act):
                    act.sem_inc(s_tx, 2)
                    act.sem_inc(s_h, 2)

                    def body(i, s, q, n):
                        for k in range(4):
                            act.wait_ge(s_t, n * 4 + k + 1)
                            act.copy(xT[:, q % 2, :, k * P:k * P + P],
                                     pT[k % 2][:, 0:D].rearrange("p (c n) -> p c n", c=2)).then_inc(s_tx, 1)
                        if q == 0:
                            act.wait_ge(s_w[s], i * 64 + 64)
                        for f in range(8):
                            act.wait_ge(s_m1, n * 8 + f + 1)
                            act.activation(hT[:, q % 2, f, :], ph[f % 2][:, :], ACT.Relu,
                                           bias=B1[:, s, f:f + 1]).then_inc(s_h, 1)

                    loop(act, body)

                @block.vector
                def _(v):
                    v.sem_inc(s_y, 4)

                    def body(i, s, q, n):
                        v.wait_ge(s_ys[q % 2], (2 * SPE * i + SPE * s + q - q % 2) * 8 + 16)
                        for k in range(4):
                            v.wait_ge(s_m2, n * 4 + k + 1)
                            if k == 0 and q == 0:
                                v.wait_ge(s_w[s], i * 64 + 64)
                            v.tensor_tensor(y[:, q % 2, k, :], py[k % 2][:, 0:D], B2[:, s, :], ALU.add).then_inc(s_y, 2)

                    loop(v, body)

        with Scope(nc, "combine") as m:
            x = m.sb("x", [P, 2, D])
            yg = m.sb("yg", [P, 2, D])
            t_ = m.sb("t", [P, 2, D])
            bad = m.sb("bad", [P, 3, D], U32)
            lim = m.sb("lim", [P, 3, D])
            slot = m.sb("slot", [P, 2, 2], I32)
            with nc.Block() as block:

                @block.sync
                def _(sp):
                    def load(b, s):
                        sp.dma_start(x[:, s, :], dr["x"][bass.ds(b * P, P), :]).then_inc(s_x[s], 16)

                    def store(b, s, n=P):
                        sp.wait_ge(s_o, b + 1)
                        sp.dma_start(out[bass.ds(b * P, n), :], t_[0:n, s, :]).then_inc(s_st[s], 16)

                    for s in range(2):
                        sp.sem_inc(s_st[s], 16)
                        load(s, s)
                    with sp.Fori(0, NBK // 2 - 1) as i:
                        for s in range(2):
                            store(2 * i + s, s)
                            load(2 * i + s + 2, s)
                    store(NBK - 2, 0)
                    store(NBK - 1, 1, N - FULL * P)
                    for s in range(2):
                        sp.wait_ge(s_st[s], NBK // 2 * 16 + 16)

                @block.gpsimd
                def _(pool):
                    with pool.Fori(0, NBK // 2) as i:
                        for s in range(2):
                            b = 2 * i + s
                            pool.wait_ge(s_gi, b + 1)
                            pool.sem_inc(s_scx, 1)
                            pool.indirect_dma_start(yg[:, s, :], None, dr["ybuf"], IndirectOffsetOnAxis(
                                ap=slot[:, s, 0:1], axis=0)).then_inc(s_g[s], 16)

                @block.vector
                def _(v):
                    for j, value in enumerate((0.0, 1e4, -1e4)):
                        t = v.memset(lim[:, j, :], value)
                    t.then_inc(s_nn, 1)
                    v.wait_ge(s_nn, 1)
                    for s in range(2):
                        v.tensor_copy(slot[:, s, 0:1], gslot[:, s:s + 1]).then_inc(s_gi, 1)

                    def body(i, s, b, last=False):
                        own = Step(v, s_nn, b * 6 + 1)
                        v.wait_ge(s_g[s], i * 16 + 16)
                        v.wait_ge(s_st[s], i * 16 + 16)
                        own(v.tensor_scalar(t_[:, s, :], yg[:, s, :], wgt[:, bass.ds(b, 1)], None, ALU.mult))
                        if not last:
                            v.tensor_copy(slot[:, s, 0:1], gslot[:, bass.ds(b + 2, 1)]).then_inc(s_gi, 1)
                        v.tensor_tensor(bad[:, 0, :], t_[:, s, :], t_[:, s, :], ALU.not_equal)
                        v.tensor_scalar(bad[:, 1, :], t_[:, s, :], 3.4028235e38, None, ALU.is_gt)
                        own(v.tensor_scalar(bad[:, 2, :], t_[:, s, :], -3.4028235e38, None, ALU.is_lt))
                        for j in range(3):
                            v.sem_inc(s_go, 1)
                            own(v.copy_predicated(t_[:, s, :], bad[:, j, :], lim[:, j, :]))
                        v.wait_ge(s_x[s], i * 16 + 16)
                        own(v.tensor_tensor(t_[:, s, :], t_[:, s, :], x[:, s, :], ALU.add))
                        v.sem_inc(s_o, 1)

                    with v.Fori(0, NBK // 2 - 1) as i:
                        for s in range(2):
                            body(i, s, 2 * i + s)
                    for s in range(2):
                        body(NBK // 2 - 1, s, NBK - 2 + s, True)


def add_rows(nc, c, dr, acc):
    NBK = (N + P - 1) // P
    s_cp, s_t, s_r0, s_r1, s_add, s_st0, s_st1 = sems(
        nc, "rows", "copied", "turned", "rows0", "rows1", "added", "stored0", "stored1")
    s_r, s_st = (s_r0, s_r1), (s_st0, s_st1)
    with Scope(nc, "rows") as m:
        g = m.sb("g", [P, 2, 2, P])
        row = m.sb("row", [P, 2, D])
        pt = [m.ps(f"pt{i}", [P, 512]) for i in range(2)]
        with nc.Block() as block:

            @block.sync
            def _(sp):
                for s in range(2):
                    sp.dma_start(row[:, s, :], dr["x"][s * P:s * P + P, :]).then_inc(s_r[s], 16)
                with sp.Fori(0, NBK // 2 - 1) as i:
                    for s in range(2):
                        b = 2 * i + s
                        sp.wait_ge(s_add, b + 3)
                        sp.dma_start(dr["x"][bass.ds(b * P, P), :], row[:, s, :]).then_inc(s_st[s], 16)
                        sp.wait_ge(s_st[s], i * 16 + 16)
                        sp.dma_start(row[:, s, :], dr["x"][bass.ds((b + 2) * P, P), :]).then_inc(s_r[s], 16)
                for s in range(2):
                    sp.wait_ge(s_add, NBK + 1 + s)
                    sp.dma_start(dr["x"][(NBK - 2 + s) * P:(NBK - 1 + s) * P, :], row[:, s, :]).then_inc(s_st[s], 16)
                for s in range(2):
                    sp.wait_ge(s_st[s], NBK // 2 * 16)

            @block.scalar
            def _(act):
                act.sem_inc(s_t, 2)
                with act.Fori(0, NBK // 2) as i:
                    for s in range(2):
                        b = 2 * i + s
                        act.wait_ge(s_t, b + 1)
                        act.copy(g[:, s, :, :], acc[:, :, bass.ds(b * P, P)]).then_inc(s_cp, 1)

            @block.tensor
            def _(pe):
                with pe.Fori(0, NBK // 2) as i:
                    for s in range(2):
                        b = 2 * i + s
                        pe.wait_ge(s_cp, b + 1)
                        pe.wait_ge(s_add, b + 1)
                        for o in range(2):
                            t = pe.transpose(pt[s][:, o * P:o * P + P], g[:, s, o, :], c.ident[:, :])
                        t.then_inc(s_t, 1)

            @block.vector
            def _(v):
                v.sem_inc(s_add, 2)
                with v.Fori(0, NBK // 2) as i:
                    for s in range(2):
                        b = 2 * i + s
                        v.wait_ge(s_t, b + 3)
                        v.wait_ge(s_r[s], i * 16 + 16)
                        v.tensor_tensor(row[:, s, :], row[:, s, :], pt[s][:, 0:D], ALU.add).then_inc(s_add, 1)


def run_phase(nc, f, *args, **kw):
    before = set(nc.free_semaphores)
    f(nc, *args, **kw)
    used = sorted(before - set(nc.free_semaphores))
    nc.clear_and_free_semaphores(used)
    nc.all_engine_barrier()


def graph_program(nc, a, out):
    phase = lambda f, *args, **kw: run_phase(nc, f, *args, **kw)
    dram = lambda name, shape, dt=F32: nc.dram_tensor(name, shape, dt).ap()
    dr = dict(x=dram("xs", (NR, D)), src=dram("srcp", (1, NE), I32), dst=dram("dstp", (1, NE + 1), I32),
              dist=dram("distp", (1, NE)), mask=dram("mask", (NT, MW)), d0=dram("d0", (NT, 1), I32),
              srcT=dram("srcT", (P, NT + G), I32), relT=dram("relT", (P, NT + G)), distT=dram("distT", (P, NT)),
              q=dram("q", (NR, D)), kv=dram("kv", (NR, 2 * D)), xT=dram("xT", (P, 2, NR)),
              ft=dram("ft", (NR, 260)), ed=dram("ed", (NR, 4)), logits=dram("logits", (NR, 8)),
              ln=dram("ln", (NR, D)), buf=dram("buf", (8 * 2048, D)), ybuf=dram("ybuf", (8 * 2048, D)))
    NA = N + P + 12
    with Scope(nc, "all") as m:
        c = Constants(nc, m)
        phase(prepare_edges, c.ident, a["x"], a["src"], a["dst"], a["edge_attr3_1x1"], dr)
        phase(node_tables, c.ident, "qkv", dr["x"],
                    [(0, a["L0_gnn_WQ"]), (D, a["L0_gnn_WK"]), (2 * D, a["L0_gnn_WV"])], 3 * D,
                    [(dr["q"], 0, 0, D), (dr["kv"], 0, D, 2 * D)], xT_out=dr["xT"])
        with Scope(nc, "sum0") as s:
            acc = s.sb("acc", [P, 2, NA])
            phase(edge_phase, "att", c, dr, acc, 8, float(np.float32(1 / np.sqrt(np.float32(D // 8)))),
                       dr["kv"], dr["q"], None)
            phase(graph_norm, c, dr, acc, a["L0_gnn_W_out"], a["L0_gnn_b_out"], a["L0_gnn_gn_weight"],
                       a["L0_gnn_gn_bias"], a["L0_gnn_gn_mean_scale"])
        phase(moe_top2, c, dr, a["L0_ffn_router_w"], a["L0_ffn_w1"], a["L0_ffn_b1"], a["L0_ffn_w2"], a["L0_ffn_b2"])
        phase(node_tables, c.ident, "gat", dr["x"], [(0, a["L1_gnn_W"])], 264,
                    [(dr["ft"], 0, 0, 260), (dr["ed"], 0, 260, 4)],
                    attention=(a["L1_gnn_w_att_src"], a["L1_gnn_w_att_dst"]))
        with Scope(nc, "sum1") as s:
            acc = s.sb("acc", [P, 2, NA])
            phase(edge_phase, "gate", c, dr, acc, 4, 1.0, dr["ft"], dr["ed"], dr["distT"])
            phase(add_rows, c, dr, acc)
        phase(node_tables, c.ident, "gate_ln", dr["x"], [(0, a["L1_ffn_gate_w"])], 8,
                    [(dr["logits"], 0, 0, 8)], ln_out=dr["ln"])
        moe_switch(nc, c, dr, a["L1_ffn_gate_b"], a["L1_ffn_w1"], a["L1_ffn_b1"], a["L1_ffn_w2"],
                   a["L1_ffn_b2"], out)


_NAMES = ["x", "src", "dst", "edge_attr3_1x1", "L0_gnn_WQ", "L0_gnn_WK", "L0_gnn_WV", "L0_gnn_W_out", "L0_gnn_b_out",
          "L0_gnn_gn_weight", "L0_gnn_gn_bias", "L0_gnn_gn_mean_scale", "L0_ffn_router_w", "L0_ffn_w1", "L0_ffn_b1",
          "L0_ffn_w2", "L0_ffn_b2", "L1_gnn_W", "L1_gnn_w_att_src", "L1_gnn_w_att_dst", "L1_ffn_gate_w",
          "L1_ffn_gate_b", "L1_ffn_w1", "L1_ffn_b1", "L1_ffn_w2", "L1_ffn_b2"]


def kernel(**inputs):
    import numpy as _np
    import concourse.bacc as _bacc
    from concourse import mybir as _mybir
    from concourse.bass_utils import run_bass_kernel_spmd as _run

    nc = _bacc.Bacc("TRN2", target_bir_lowering=False, num_devices=1)
    arrays, aps = {}, {}
    for name in _NAMES:
        a = _np.ascontiguousarray(inputs[name])
        arrays[f"in_{name}_dram"] = a
        aps[name] = nc.dram_tensor(f"in_{name}_dram", a.shape, _mybir.dt.from_np(a.dtype), kind="ExternalInput").ap()
    out = nc.dram_tensor("out_0_dram", (N, D), F32, kind="ExternalOutput").ap()
    graph_program(nc, aps, out)
    r = _run(nc, [arrays], core_ids=[0])
    return r.results[0]["out_0_dram"]
```

```python
from contextlib import ExitStack

import numpy as np
import concourse.bass as bass
from concourse import mybir
from concourse.bass import IndirectOffsetOnAxis

ALU = mybir.AluOpType
ACT = mybir.ActivationFunctionType
AX = mybir.AxisListType
F32 = mybir.dt.float32
I32 = mybir.dt.int32
U32 = mybir.dt.uint32
BF16 = mybir.dt.bfloat16
SP_ENG, ACT_ENG, DVE_ENG = mybir.EngineType.SP, mybir.EngineType.Activation, mybir.EngineType.DVE

P = 128
N = 12500
D = 256
E = 212500
EPS = 1e-5
NB = 100
NR = NB * P
G = 16
NG = 105
NT = NG * G
NE = NT * P
TB = 120
MW = 132
BIG = 1e30
assert NT % TB == 0 and NE > E and NR >= N + P and E > (NT - 8) * P - 8 * P * G


class Step:

    def __init__(self, eng, sem, base=0):
        self.eng, self.sem, self.base, self.n = eng, sem, base, 0

    def __call__(self, ins):
        ins.then_inc(self.sem, 1)
        self.n += 1
        self.wait()

    def do(self, ins):
        ins.then_inc(self.sem, 1)
        self.n += 1

    def wait(self):
        self.eng.wait_ge(self.sem, self.base + self.n)


class Scope(ExitStack):

    def __init__(self, nc, tag):
        super().__init__()
        self.nc, self.tag = nc, tag

    def sb(self, name, shape, dt=F32):
        return self.enter_context(self.nc.sbuf_tensor(f"{self.tag}_{name}", shape, dt))

    def ps(self, name, shape, dt=F32):
        return self.enter_context(self.nc.psum_tensor(f"{self.tag}_{name}", shape, dt))


def sems(nc, tag, *names):
    return [nc.alloc_semaphore(name=f"{tag}_{n}") for n in names]



def prepare_edges(nc, ident, x, src, dst, dist, dr):
    s_fill, s_pad, s_nat, s_free, s_dve, s_turn, s_out, s_st = sems(
        nc, "prep", "filled", "padded", "loaded", "read", "dve", "turned", "copied", "stored")
    NP_ = NE - E
    with Scope(nc, "prep") as m:
        zero = m.sb("zero", [P, (NR - N) * D // 100])
        tail = m.sb("tail", [1, 3, NP_], I32)
        ftail = m.sb("ftail", [1, NP_])
        spare = m.sb("spare", [P, G], I32)
        nat = m.sb("nat", [P, 3, P], I32)
        natd = m.sb("natd", [P, P])
        f = m.sb("f", [P, 3, P])
        rel = m.sb("rel", [P, P])
        cont = m.sb("cont", [P, P])
        mask = m.sb("mask", [P, MW])
        tsrc = m.sb("tsrc", [P, P], I32)
        trel = m.sb("trel", [P, P])
        tdist = m.sb("tdist", [P, P])
        pt = m.ps("pt", [P, 3, P])
        with nc.Block() as block:

            @block.sync
            def _(sp):
                sp.dma_start(dr["x"][0:N, :], x).then_inc(s_pad, 16)
                sp.dma_start(dr["src"][0:1, 0:E], src.rearrange("(a e) -> a e", a=1)).then_inc(s_pad, 16)
                sp.dma_start(dr["dst"][0:1, 1:E + 1], dst.rearrange("(a e) -> a e", a=1)).then_inc(s_pad, 16)
                sp.dma_start(dr["dist"][0:1, 0:E], dist.rearrange("e a b -> (a b) e")).then_inc(s_pad, 16)
                sp.wait_ge(s_fill, 7)
                sp.dma_start(dr["x"][N:NR, :].rearrange("(p r) d -> p (r d)", p=100),
                             zero[0:100, :]).then_inc(s_pad, 16)
                sp.dma_start(dr["src"][0:1, E:NE], tail[:, 0, :]).then_inc(s_pad, 16)
                sp.dma_start(dr["dst"][0:1, E + 1:NE + 1], tail[:, 1, :]).then_inc(s_pad, 16)
                sp.dma_start(dr["dst"][0:1, 0:1], tail[:, 2, 0:1]).then_inc(s_pad, 16)
                sp.dma_start(dr["dist"][0:1, E:NE], ftail[:, :]).then_inc(s_pad, 16)
                sp.dma_start(dr["srcT"][:, NT:NT + G], spare[:, :]).then_inc(s_pad, 16)
                sp.dma_start(dr["relT"][:, NT:NT + G], zero[:, 0:G]).then_inc(s_pad, 16)
                sp.wait_ge(s_pad, 11 * 16)
                with sp.Fori(0, NT // TB) as b:
                    sp.wait_ge(s_free, b + 1)
                    e0 = b * (TB * P)
                    for i, (name, off) in enumerate((("src", 0), ("dst", 1), ("dst", 0))):
                        sp.dma_start(nat[0:TB, i, :], dr[name][0:1, bass.ds(e0 + off, TB * P)].rearrange(
                            "a (t e) -> (a t) e", e=P)).then_inc(s_nat, 16)
                    sp.dma_start(natd[0:TB, :], dr["dist"][0:1, bass.ds(e0, TB * P)].rearrange(
                        "a (t e) -> (a t) e", e=P)).then_inc(s_nat, 16)
                    sp.wait_ge(s_out, b + 1)
                    c = bass.ds(b * TB, TB)
                    sp.dma_start(dr["mask"][c, :], mask[0:TB, :]).then_inc(s_st, 16)
                    sp.dma_start(dr["d0"][c, :], nat[0:TB, 1, 0:1]).then_inc(s_st, 16)
                    sp.dma_start(dr["srcT"][:, c], tsrc[:, 0:TB]).then_inc(s_st, 16)
                    sp.dma_start(dr["relT"][:, c], trel[:, 0:TB]).then_inc(s_st, 16)
                    sp.dma_start(dr["distT"][:, c], tdist[:, 0:TB]).then_inc(s_st, 16)

            @block.vector
            def _(v):
                v.memset(zero[:, :], 0.0).then_inc(s_fill, 1)
                v.memset(tail[:, 0, :], 0).then_inc(s_fill, 1)
                v.memset(tail[:, 1, :], N).then_inc(s_fill, 1)
                v.memset(tail[:, 2, :], -1).then_inc(s_fill, 1)
                v.memset(ftail[:, :], 0.0).then_inc(s_fill, 1)
                v.memset(spare[:, :], 0).then_inc(s_fill, 1)
                v.memset(mask[:, :], 1.0).then_inc(s_fill, 1)
                v.wait_ge(s_fill, 7)
                v.sem_inc(s_free, 1)
                with v.Fori(0, NT // TB) as b:
                    own = Step(v, s_dve, b * 5)
                    v.wait_ge(s_nat, b * 64 + 64)
                    own(v.tensor_copy(f[0:TB, :, :], nat[0:TB, :, :]))
                    own(v.tensor_scalar(rel[0:TB, :], f[0:TB, 1, :], f[0:TB, 1, 0:1], None, ALU.subtract))
                    own(v.tensor_tensor(cont[0:TB, :], f[0:TB, 1, :], f[0:TB, 2, :], ALU.is_equal))
                    v.wait_ge(s_st, b * 80 + 16)
                    own(v.tensor_copy(mask[0:TB, 1:P], cont[0:TB, 1:P]))
                    v.tensor_copy(mask[0:TB, 129:130], cont[0:TB, 0:1])
                    own(v.scalar_tensor_tensor(mask[0:TB, 130:131], rel[0:TB, 127:128], 0.0, cont[0:TB, 0:1],
                                               ALU.is_equal, ALU.mult))
                    v.wait_ge(s_turn, b + 1)
                    v.tensor_copy(tsrc[:, 0:TB], pt[:, 0, 0:TB])
                    v.tensor_copy(trel[:, 0:TB], pt[:, 1, 0:TB])
                    v.tensor_copy(tdist[:, 0:TB], pt[:, 2, 0:TB]).then_inc(s_out, 1)
                    v.wait_ge(s_st, b * 80 + 96)
                    v.sem_inc(s_free, 1)

            @block.scalar
            def _(act):
                act.wait_ge(s_fill, 7)
                act.sem_inc(s_st, 16)

            @block.tensor
            def _(pe):
                with pe.Fori(0, NT // TB) as b:
                    pe.wait_ge(s_dve, b * 5 + 2)
                    pe.transpose(pt[:, 0, 0:TB], f[0:TB, 0, :], ident[0:TB, 0:TB])
                    pe.transpose(pt[:, 1, 0:TB], rel[0:TB, :], ident[0:TB, 0:TB])
                    pe.transpose(pt[:, 2, 0:TB], natd[0:TB, :], ident[0:TB, 0:TB]).then_inc(s_turn, 1)


def node_tables(nc, ident, tag, src_rows, weights, NC, outs, xT_out=None, attention=None, ln_out=None):
    (s_w, s_c, s_x0, s_x1, s_own, s_bn, s_sd, s_ln, s_tp, s_xt, s_mm, s_evd, s_eva, s_st0, s_st1, s_att, s_go) = sems(
        nc, tag, "weights", "consts", "rows0", "rows1", "dve", "stats", "std", "normed", "turned", "xT", "product",
        "copied_dve", "copied_act", "stored0", "stored1", "att", "go")
    s_x, s_st = (s_x0, s_x1), (s_st0, s_st1)
    nst = len(outs) + (xT_out is not None) + (ln_out is not None)
    NS, R2 = NB // 2, 2 * P
    cut = min(NC, 512)
    with Scope(nc, tag) as m:
        w = m.sb("w", [P, 2, NC])
        xin = m.sb("xin", [P, 2, 2, D])
        st = m.sb("st", [P, 2, 6])
        mv = m.sb("mv", [P, 2, 2, 2])
        sd = m.sb("sd", [P, 2, 2, 2])
        eps = m.sb("eps", [P, 1])
        xln = m.sb("xln", [P, 2, 2, D])
        xT = m.sb("xT", [P, 2, 2, R2])
        row = m.sb("row", [P, 2, 2, NC])
        att = m.sb("att", [P, 2, D])
        prod = m.sb("prod", [P, 2, D])
        pT = [m.ps(f"pT{i}", [P, 512]) for i in range(2)]
        pq = [m.ps(f"pq{i}", [P, 1024]) for i in range(2)]
        two = lambda ap, n: ap[bass.ds(n * R2, R2), :].rearrange("(k p) d -> p k d", p=P)

        def run(eng, step):
            step(0, 0, True)
            step(1, 1, True)
            with eng.Fori(0, NS // 2 - 2) as i:
                for j in range(2):
                    step(2 * i + (2 + j), j, True)
            step(NS - 2, 0, True)
            step(NS - 1, 1, False)

        def uses(n, s):
            return (n - s) * 8

        with nc.Block() as block:

            @block.sync
            def _(sp):
                for c0, ap in weights:
                    sp.dma_start(w[:, :, c0:c0 + ap.shape[1]], ap.rearrange("(c p) n -> p c n", p=P)).then_inc(s_w, 16)
                if attention:
                    for i in range(2):
                        sp.dma_start(att[:, i, :], attention[i].rearrange("a h o -> a (h o)").to_broadcast(
                            [P, D])).then_inc(s_w, 16)
                for s in range(2):
                    sp.dma_start(xin[:, s, :, :], two(src_rows, s)).then_inc(s_x[s], 16)

                def store(n, s):
                    sp.wait_ge(s_evd, 2 * n + 2)
                    if NC > 512:
                        sp.wait_ge(s_eva, 2 * n + 2)
                    for ap, o0, c0, width in outs:
                        sp.dma_start(two(ap, n)[:, :, o0:o0 + width], row[:, s, :, c0:c0 + width]).then_inc(s_st[s], 16)
                    if xT_out is not None:
                        sp.dma_start(xT_out[:, :, bass.ds(n * R2, R2)], xT[:, s, :, :]).then_inc(s_st[s], 16)
                    if ln_out is not None:
                        sp.dma_start(two(ln_out, n), xln[:, s, :, :]).then_inc(s_st[s], 16)

                def step(n, s, more):
                    if more and not (isinstance(n, int) and n + 2 >= NS):
                        sp.wait_ge(s_ln, n + 1)
                        sp.dma_start(xin[:, s, :, :], two(src_rows, n + 2)).then_inc(s_x[s], 16)
                    store(n, s)

                run(sp, step)
                for s in range(2):
                    sp.wait_ge(s_st[s], NS // 2 * nst * 16)

            @block.vector
            def _(v):
                v.memset(eps[:, :], EPS).then_inc(s_c, 1)
                if attention:
                    H = attention[0].shape[1]
                    v.wait_ge(s_w, 16 * (len(weights) + 2))
                    for a in range(2):
                        for c in range(2):
                            if a + c:
                                v.wait_ge(s_att, 2 * (2 * a + c))
                            v.tensor_tensor(prod[:, c, :], w[:, c, 0:D], att[:, a, :], ALU.mult).then_inc(s_att, 1)
                            v.wait_ge(s_att, 2 * (2 * a + c) + 1)
                            v.tensor_reduce(w[:, c, D + a * H:D + a * H + H],
                                            prod[:, c, :].rearrange("p (h o) -> p h o", h=H),
                                            AX.X, ALU.add).then_inc(s_att, 1)

                def stats(n, s):
                    v.wait_ge(s_x[s], uses(n, s) + 16)
                    for k in range(2):
                        v.bn_stats(st[:, k, :], xin[:, s, k, :]).then_inc(s_own, 1)
                    v.wait_ge(s_own, 3 * n + 2)
                    v.sem_inc(s_go, 1)
                    v.bn_aggr(mv[:, s, 0, :], st[:, 0, :])
                    v.bn_aggr(mv[:, s, 1, :], st[:, 1, :]).then_inc(s_bn, 1)

                def norm(n, s):
                    v.wait_ge(s_sd, n + 1)
                    v.reciprocal(sd[:, s, 1, :], sd[:, s, 0, :]).then_inc(s_own, 1)
                    if ln_out is not None and not (isinstance(n, int) and n < 2):
                        v.wait_ge(s_st[s], uses(n, s) * nst)
                    v.wait_ge(s_own, 3 * n + 3)
                    for k in range(2):
                        t = v.tensor_scalar(xln[:, s, k, :], xin[:, s, k, :], mv[:, s, k, 0:1], sd[:, s, 1, k:k + 1],
                                            ALU.subtract, ALU.mult)
                    t.then_inc(s_ln, 1)

                def copy(n, s, k):
                    v.wait_ge(s_mm, 2 * n + k + 1)
                    if k == 0 and not (isinstance(n, int) and n < 2):
                        v.wait_ge(s_st[s], uses(n, s) * nst)
                    v.tensor_copy(row[:, s, k, 0:cut], pq[k][:, 0:cut]).then_inc(s_evd, 1)

                stats(0, 0)
                norm(0, 0)

                def step(n, s, more):
                    if more:
                        stats(n + 1, 1 - s)
                    if not (isinstance(n, int) and n == 0):
                        copy(n - 1, 1 - s, 1)
                    if more:
                        norm(n + 1, 1 - s)
                    copy(n, s, 0)

                run(v, step)
                copy(NS - 1, 1, 1)

            @block.scalar
            def _(act):
                act.wait_ge(s_c, 1)

                def std(n, s):
                    act.wait_ge(s_bn, n + 1)
                    act.activation(sd[:, s, 0, :], mv[:, s, :, 1], ACT.Sqrt, bias=eps[:, 0:1]).then_inc(s_sd, 1)

                def turned(n, s):
                    act.wait_ge(s_tp, n + 1)
                    if not (isinstance(n, int) and n < 2):
                        act.wait_ge(s_mm, 2 * n - 2)
                        if xT_out is not None:
                            act.wait_ge(s_st[s], uses(n, s) * nst)
                    act.copy(xT[:, s, :, :].rearrange("p c (k r) -> p k c r", k=2),
                             pT[s][:, :].rearrange("p (k c r) -> p k c r", k=2, c=2)).then_inc(s_xt, 1)

                def copy(n, s, k):
                    if NC <= 512:
                        return
                    act.wait_ge(s_mm, 2 * n + k + 1)
                    if k == 0 and not (isinstance(n, int) and n < 2):
                        act.wait_ge(s_st[s], uses(n, s) * nst)
                    act.copy(row[:, s, k, cut:NC], pq[k][:, cut:NC]).then_inc(s_eva, 1)

                std(0, 0)
                turned(0, 0)

                def step(n, s, more):
                    if more:
                        std(n + 1, 1 - s)
                    if not (isinstance(n, int) and n == 0):
                        copy(n - 1, 1 - s, 1)
                    copy(n, s, 0)
                    if more:
                        turned(n + 1, 1 - s)

                run(act, step)
                copy(NS - 1, 1, 1)

            @block.tensor
            def _(pe):
                pe.wait_ge(s_w, 16 * (len(weights) + (2 if attention else 0)))
                if attention:
                    pe.wait_ge(s_att, 8)

                def turn(n, s):
                    pe.wait_ge(s_ln, n + 1)
                    for k in range(2):
                        for c in range(2):
                            t = pe.transpose(pT[s][:, (2 * k + c) * P:(2 * k + c) * P + P],
                                             xln[:, s, k, c * P:c * P + P], ident[:, :])
                    t.then_inc(s_tp, 1)

                def product(n, s, k):
                    if k == 0:
                        pe.wait_ge(s_xt, n + 1)
                    if not (isinstance(n, int) and n == 0):
                        pe.wait_ge(s_evd, 2 * n + k - 1)
                        if NC > 512:
                            pe.wait_ge(s_eva, 2 * n + k - 1)
                    for h0, h1 in [(0, cut)] + ([(cut, NC)] if NC > cut else []):
                        for c in range(2):
                            t = pe.matmul(pq[k][:, h0:h1], xT[:, s, c, k * P:k * P + P], w[:, c, h0:h1],
                                          start=(c == 0), stop=(c == 1))
                    t.then_inc(s_mm, 1)

                turn(0, 0)

                def step(n, s, more):
                    product(n, s, 0)
                    if more:
                        turn(n + 1, 1 - s)
                    product(n, s, 1)

                run(pe, step)


def split_rows(nc, dr, e, e3):
    s_l, s_o, s_st = sems(nc, "split", "loaded", "dve", "stored")
    R = NR // P
    with Scope(nc, "split") as m:
        x = m.sb("x", [P, R, 4])
        t = m.sb("t", [P, R, 3, 4], BF16)
        with nc.Block() as block:

            @block.sync
            def _(sp):
                sp.dma_start(x[:, :, :], e.rearrange("(p r) h -> p r h", p=P)).then_inc(s_l, 16)
                sp.wait_ge(s_o, 5)
                sp.dma_start(e3.rearrange("(p r) (c h) -> p r c h", p=P, c=3), t[:, :, :, :]).then_inc(s_st, 16)
                sp.wait_ge(s_st, 16)

            @block.vector
            def _(v):
                own = Step(v, s_o)
                v.wait_ge(s_l, 16)
                for k in range(3):
                    own(v.tensor_copy(t[:, :, k, :], x[:, :, :]))
                    if k < 2:
                        own(v.tensor_tensor(x[:, :, :], x[:, :, :], t[:, :, k, :], ALU.subtract))


def edge_phase(nc, tag, c, dr, acc, H, scale, rows_t, dst_t, dist_t):
    gat = dist_t is not None
    RW, DW = rows_t.shape[1], dst_t.shape[1]
    HALF = dst_t.dtype
    Dh, HT, VW = D // H, H * G, (RW if gat else D)
    GP, NP2 = G // 2, NG * (G // 2)
    RG, VR = 3, 3 if gat else 2
    UN = 3 if gat else 6
    LAG = 15
    AHOT = not gat
    R, Q = (8, 4) if gat else (4, 2)
    if gat:
        PE_AT = {(0, 1): 0, (1, 0): 1, (2, 0): 2, (4, 0): 3, (5, 0): 4, (6, 0): 5}
        ACT_AT = {(0, 1): 0, (1, 0): 1, (3, 0): 2, (4, 0): 3, (6, 0): 4}
        DVE_AT = {(0, 4): (0,), (0, 5): (1,), (0, 6): (2,), (1, 4): (3,), (1, 5): (4,), (1, 6): (5,),
                  (2, 3): (6,), (2, 4): (7,), (2, 5): (8,), (2, 6): (9,), (3, 6): (10,),
                  (4, 4): (11,), (4, 5): (12,), (4, 6): (13,), (5, 2): (14,), (5, 3): (15,), (5, 4): (16,),
                  (5, 5): (17,), (5, 6): (18,), (6, 6): (19,)}
    else:
        PE_AT = {(0, 1): 0, (1, 0): 1, (2, 0): 2, (4, 0): 3, (5, 0): 4, (6, 0): 5}
        ACT_AT = {(0, 1): 0, (1, 0): 1, (3, 0): 2, (4, 0): 3, (6, 0): 4}
        DVE_AT = {(0, 5): (0,), (0, 6): (2,), (1, 4): (3,), (1, 5): (4,), (1, 6): (5,),
                  (2, 3): (6,), (2, 4): (7,), (2, 5): (8,), (2, 6): (9,), (3, 6): (10,),
                  (4, 4): (11,), (4, 5): (12,), (4, 6): (13,), (5, 2): (14,), (5, 3): (15,), (5, 4): (16,),
                  (5, 5): (17,), (5, 6): (18,)}
    (s_d0, s_init, s_go) = sems(nc, tag, "firsts", "init", "go")
    s_fl = sems(nc, tag, *[f"lists{r}" for r in range(RG)])
    s_cl = sems(nc, tag, *[f"masks{r}" for r in range(VR)])
    s_g = sems(nc, tag, *[f"gathered{r}" for r in range(R)])
    s_q = sems(nc, tag, *[f"window{r}" for r in range(Q)])
    (s_S, s_turn, s_ST, s_qd, s_front, s_score, s_v, s_msg, s_agg, s_mul, s_add, s_cp, s_ca, s_cd, s_cn,
     s_pgo, s_abs, s_dst, s_clear) = sems(
        nc, tag, "onehot", "turned", "onehotT", "expanded", "front", "scores", "values", "messages",
        "summed", "rescaled", "added", "chain_pe", "chain_act", "chain_dve", "chain_own", "pe_go", "distance", "dst_score", "cleared")
    if gat:
        s_score = s_front
    CD, CN = (8, 13) if gat else (7, 12)
    NL = 2
    NC_ = 2 if gat else 1
    with Scope(nc, tag) as m:
        idx = m.sb("idx", [P, RG, G], I32)
        rel = m.sb("rel", [P, RG, G])
        mrow = m.sb("mrow", [G, VR, MW])
        dist = m.sb("dist", [P, VR, G]) if gat else None
        d0 = m.sb("d0", [1, NT], I32)
        S = m.sb("S", [P, RG, G, P])
        ST = m.sb("ST", [P, 2, 2 * P], HALF)
        vst = m.sb("vst", [P, VR, G, VW])
        kv = None if gat else m.sb("kv", [P, R, 2, RW])
        win = m.sb("win", [P, Q, 2, DW], HALF)
        edst = m.sb("edst", [P, 2 * H]) if gat else None
        prod = None if gat else m.sb("prod", [P, 2 * D])
        score = m.sb("score", [P, VR, H, G])
        msg = m.sb("msg", [P, 2, 2 * D])
        alpha = m.sb("alpha", [P, VR, H, G])
        fac = m.sb("fac", [P, VR, 2, G])
        X = m.sb("X", [HT, P])
        X0 = m.sb("X0", [HT, P]) if gat else X
        M = m.sb("M", [HT, 131])
        NBm = m.sb("NB", [HT, 129])
        F = m.sb("F", [HT, P])
        B = m.sb("B", [HT, P])
        Y = m.sb("Y", [HT, 129])
        EX = m.sb("EX", [HT, 129])
        AL = X
        Df = m.sb("Df", [HT, G])
        col = m.sb("col", [HT, 2])
        r3 = m.sb("r3", [1, 3, H, G])
        r2 = m.sb("r2", [1, 2, H, G])
        wn = m.sb("wn", [1, H, G + 1])
        Lx = m.sb("Lx", [1, H, G + 1])
        Rm = m.sb("Rm", [1, H, G + 1])
        wg = m.sb("wg", [1, H, G + 1])
        Ls = m.sb("Ls", [1, H, G + 1])
        Rs = m.sb("Rs", [1, H, G + 1])
        cn = m.sb("cn", [1, H, G])
        back_row = m.sb("brow", [1, H, G])
        pST = [m.ps(f"pST{i}", [P, 512]) for i in range(2)]
        pqd = [m.ps(f"pqd{i}", [P, 512]) for i in range(2)]
        pag = [m.ps(f"pag{i}", [P, 512]) for i in range(2)]
        cA = m.ps("cA", [P, 512])
        cB = m.ps("cB", [P, 512])
        flat = lambda t: t[:, :, :].rearrange("a h g -> a (h g)")

        def wait(eng, sem, value):
            if not isinstance(value, int) or value > 0:
                eng.wait_ge(sem, value)

        def near(g, gs, p, off):
            dg, q = (p + off) // GP, (p + off) % GP
            return g + dg, gs + dg, q, 0 <= gs + dg < NG

        def run(eng, step):
            assert (NG - 3) % UN == 0
            for g in range(2):
                step(g, g)
            with eng.Fori(0, (NG - 3) // UN) as it:
                for j in range(UN):
                    step(it * UN + (2 + j), 2 + UN + j)
            for g in range(NG - 1, NG + 2):
                step(g, g)

        def firsts(engine, tile, n=4):
            return nc.values_load_multi_w_load_instructions(
                d0[0:1, bass.ds(tile, n)], engines=[engine], min_val=0, max_val=N,
                skip_runtime_bounds_check_because="d0 is clamped to [0, N] when it has been loaded")[1]

        def use(g, gs, RG=RG):
            return gs // RG + 1 if isinstance(g, int) else (g - (gs % RG)) // RG + 1

        def arrived(g, p, R):
            return (g * (GP // R) + (p // R + 1)) * 32

        with nc.Block() as block:

            @block.sync
            def _(sp):
                sp.dma_start(d0[:, :], dr["d0"].rearrange("t a -> a t")).then_inc(s_d0, 16)

                def lists(g, k):
                    t = bass.ds(g * G, G)
                    sp.dma_start(idx[:, k, :], dr["srcT"][:, t]).then_inc(s_fl[k], 16)
                    sp.dma_start(rel[:, k, :], dr["relT"][:, t]).then_inc(s_fl[k], 16)

                lists(0, 0)
                sp.wait_ge(s_d0, 17)

                def step(g, gs):
                    if gs >= NG:
                        return
                    for p in range(GP):
                        if p % 2 == 0:
                            first = firsts(SP_ENG, g * G + 2 * p)
                        wait(sp, s_qd, g * GP + p - Q + 1)
                        for i in range(2):
                            sp.dma_start(win[:, p % Q, i, :],
                                         dst_t[bass.ds(first[2 * (p % 2) + i], P), :]).then_inc(s_q[p % Q], 16)
                        if p == 3:
                            k = gs % RG
                            wait(sp, s_front, g * GP)
                            lists(g + 1, (k + 1) % RG)
                            t = bass.ds(g * G, G)
                            k = gs % VR
                            sp.dma_start(mrow[:, k, :], dr["mask"][t, :]).then_inc(s_cl[k], 16)
                            if gat:
                                sp.dma_start(dist[:, k, :], dist_t[:, t]).then_inc(s_cl[k], 16)

                run(sp, step)
                sp.wait_ge(s_fl[NG % RG], 16 * NL * (NG // RG + 1))

            @block.gpsimd
            def _(pool):
                def step(g, gs):
                    if gs >= NG:
                        return
                    k = gs % RG
                    for p in range(GP):
                        T = g * GP + p
                        if p == 0:
                            pool.wait_ge(s_fl[k], use(g, gs) * (16 * NL))
                        if gat:
                            wait(pool, s_front, T - GP + 1)
                        else:
                            wait(pool, s_front, T - R + 1)
                            wait(pool, s_v, T - R + 1)
                        pool.sem_inc(s_go, 1)
                        for i in range(2):
                            row = vst[:, k, 2 * p + i, :] if gat else kv[:, p % R, i, :]
                            pool.indirect_dma_start(row, None, rows_t, IndirectOffsetOnAxis(
                                ap=idx[:, k, 2 * p + i:2 * p + i + 1], axis=0)).then_inc(s_g[p % R], 16)

                run(pool, step)

            @block.tensor
            def _(pe):
                pe.wait_ge(s_init, 11)

                def turn(g, gs, p):
                    k, T = gs % RG, g * GP + p
                    pe.wait_ge(s_S, T + 1)
                    for i in range(2):
                        t = pe.transpose(pST[p % 2][:, i * P:i * P + P], S[:, k, 2 * p + i, :], c.ident[:, :])
                    t.then_inc(s_turn, 1)

                def expand(g, gs, p):
                    T = g * GP + p
                    pe.wait_ge(s_ST, T + 1)
                    pe.wait_ge(s_q[p % Q], arrived(g, p, Q))
                    wait(pe, s_front, T - 1)
                    for i in range(2):
                        t = pe.matmul(pqd[p % 2][:, i * DW:i * DW + DW], ST[:, p % 2, i * P:i * P + P],
                                      win[:, p % Q, i, :], start=True, stop=True)
                    t.then_inc(s_qd, 1)

                def chain(n, h, hs):
                    b = hs % VR
                    if n == 0:
                        pe.wait_ge(s_score, h * GP + GP)
                        pe.wait_ge(s_cl[b], use(h, hs, VR) * (16 * NC_))
                        pe.sem_inc(s_pgo, 1)
                        pe.transpose(cA[0:HT, 0:P], score[:, b, :, :].rearrange("p h g -> p (h g)"), c.ident[:, :])
                        pe.matmul(cA[0:HT, P:P + 131], c.rep[:, 0:HT], mrow[:, b, 0:131],
                                  start=True, stop=True).then_inc(s_cp, 1)
                    elif n == 1:
                        pe.wait_ge(s_cd, h * CD + 2)
                        pe.sem_inc(s_pgo, 1)
                        pe.matmul(cB[0:1, 0:HT], F[:, 127:128], c.ident[0:HT, 0:HT], start=True, stop=True)
                        for j in range(2):
                            t = pe.matmul(cB[0:1, HT + j * HT:2 * HT + j * HT], M[:, 129 + j:130 + j],
                                          c.ident[0:HT, 0:HT], start=True, stop=True)
                        t.then_inc(s_cp, 1)
                    elif n in (2, 4):
                        pe.wait_ge(s_cd, h * CD + (3 if n == 2 else 6))
                        pe.sem_inc(s_pgo, 1)
                        pe.matmul(cB[0:HT, 400:401], flat(back_row), c.one[0:1, 0:1],
                                  start=True, stop=True).then_inc(s_cp, 1)
                    elif n == 3:
                        pe.wait_ge(s_cd, h * CD + 5)
                        pe.sem_inc(s_pgo, 1)
                        pe.matmul(cB[0:1, 0:HT], F[:, 127:128], c.ident[0:HT, 0:HT], start=True, stop=True)
                        pe.matmul(cB[0:1, HT:2 * HT], EX[:, 128:129], c.ident[0:HT, 0:HT],
                                  start=True, stop=True).then_inc(s_cp, 1)
                    else:
                        pe.wait_ge(s_cd, h * CD + 7)
                        pe.sem_inc(s_pgo, 1)
                        pe.transpose(cA[:, 0:HT], AL[:, :], c.ident[0:HT, 0:HT])
                        for j in range(2):
                            t = pe.matmul(cA[:, P + j * G:P + j * G + G], c.heads[H][:, j, :], Df[:, :],
                                          start=True, stop=True)
                        t.then_inc(s_cp, 1)

                def aggregate(g, gs, p):
                    pe.wait_ge(s_msg, g * GP + p + 1)
                    for i in range(2):
                        for j in range(2):
                            t = pe.matmul(pag[p % 2][:, i * D + j * P:i * D + j * P + P],
                                          msg[:, p % 2, i * D + j * P:i * D + j * P + P],
                                          S[:, gs % RG, 2 * p + i, :], start=True, stop=True)
                    t.then_inc(s_agg, 1)

                turn(0, 0, 0)
                turn(0, 0, 1)
                expand(0, 0, 0)

                def step(g, gs):
                    for p in range(GP):
                        chained = 0 < gs <= NG
                        if chained and (p, 0) in PE_AT:
                            chain(PE_AT[p, 0], g - 1, gs - 1)
                        for f, off in ((expand, 1), (turn, 2)):
                            fg, fs, fp, real = near(g, gs, p, off)
                            if real:
                                f(fg, fs, fp)
                        if chained and (p, 1) in PE_AT:
                            chain(PE_AT[p, 1], g - 1, gs - 1)
                        ug, us, up, real = near(g, gs, p, -LAG)
                        if real:
                            aggregate(ug, us, up)

                run(pe, step)

            @block.scalar
            def _(act):
                def onehot(g, gs, p):
                    k, T = gs % RG, g * GP + p
                    if p == 0:
                        act.wait_ge(s_fl[k], use(g, gs) * (16 * NL))
                    wait(act, s_agg, T - 3 - LAG)
                    for i in range(2):
                        act.activation(S[:, k, 2 * p + i, :], c.iota[:, :], ACT.Abs,
                                       bias=rel[:, k, 2 * p + i:2 * p + i + 1], scale=-1.0).then_inc(s_abs, 1)
                    act.wait_ge(s_abs, 2 * T + 2)
                    act.activation(S[:, k, 2 * p:2 * p + 2, :], S[:, k, 2 * p:2 * p + 2, :], ACT.Relu,
                                   bias=c.one[:, 0:1], scale=-1.0).then_inc(s_S, 1)

                def turned(g, p):
                    act.wait_ge(s_turn, g * GP + p + 1)
                    act.copy(ST[:, p % 2, :], pST[p % 2][:, 0:2 * P]).then_inc(s_ST, 1)

                def values(g, k, p):
                    act.wait_ge(s_g[p % R], arrived(g, p, R))
                    wait(act, s_msg, g * GP + p - VR * GP + 1)
                    act.copy(vst[:, k, 2 * p:2 * p + 2, :], kv[:, p % R, :, D:2 * D]).then_inc(s_v, 1)

                def chain(n, h, b):
                    if n == 0:
                        act.wait_ge(s_cp, h * 6 + 1)
                        act.activation(X0[:, :], cA[0:HT, 0:P], ACT.Copy, scale=scale).then_inc(s_ca, 1)
                    elif n == 1:
                        act.wait_ge(s_cp, h * 6 + 2)
                        act.copy(r3[:, :, :, :].rearrange("a c h g -> a (c h g)"), cB[0:1, 0:3 * HT]).then_inc(s_ca, 1)
                    elif n == 2:
                        act.wait_ge(s_cd, h * CD + 4)
                        act.activation(EX[:, :], Y[:, :], ACT.Exp).then_inc(s_ca, 1)
                    elif n == 3:
                        act.wait_ge(s_cp, h * 6 + 4)
                        act.copy(r2[:, :, :, :].rearrange("a c h g -> a (c h g)"), cB[0:1, 0:2 * HT]).then_inc(s_ca, 1)
                    else:
                        act.wait_ge(s_cp, h * 6 + 6)
                        if not gat:
                            act.copy(alpha[:, b, :, :].rearrange("p h g -> p (h g)"), cA[:, 0:HT])
                        act.copy(fac[:, b, :, :].rearrange("p c g -> p (c g)"),
                                 cA[:, P:P + 2 * G]).then_inc(s_ca, 1)

                for p in range(3 if AHOT else 0):
                    onehot(0, 0, p)
                for p in range(2):
                    turned(0, p)

                def step(g, gs):
                    for p in range(GP):
                        chained = 0 < gs <= NG
                        if chained and (p, 0) in ACT_AT:
                            chain(ACT_AT[p, 0], g - 1, (gs - 1) % VR)
                        fg, _, fp, real = near(g, gs, p, 2)
                        if real:
                            turned(fg, fp)
                        og, os_, op, ahead = near(g, gs, p, 3)
                        if ahead and AHOT:
                            onehot(og, os_, op)
                        if gs < NG and not gat:
                            values(g, gs % VR, p)
                        if chained and (p, 1) in ACT_AT:
                            chain(ACT_AT[p, 1], g - 1, (gs - 1) % VR)

                run(act, step)

            @block.vector
            def _(v):
                ini = Step(v, s_init)
                for t, value in ((wn, -BIG), (Rm, -BIG), (Lx, -BIG), (wg, 0.0), (Rs, 0.0), (Ls, 0.0)):
                    ini(v.memset(t[:, :, :], value))
                for t in (r3, r2):
                    ini(v.memset(t[:, :, :, :], 0.0))
                ini(v.memset(cn[:, :, :], 0.0))
                ini(v.memset(back_row[:, :, :], 0.0))
                ini(v.memset(col[:, :], 0.0))
                v.wait_ge(s_d0, 16)
                v.tensor_scalar(d0[:, :], d0[:, :], 0, N, ALU.max, ALU.min).then_inc(s_d0, 1)
                v.wait_ge(s_d0, 17)
                v.sem_inc(s_add, 2)

                def chain(n, h, b, own):
                    if n == 0:
                        v.wait_ge(s_ca, h * 5 + 1)
                        v.tensor_copy(M[:, :], cA[0:HT, P:P + 131]).then_inc(s_cd, 1)
                        own.do(v.tensor_scalar(NBm[:, :], cA[0:HT, P:P + 129], 1.0, BIG, ALU.subtract, ALU.mult))
                    elif n == 1:
                        if gat:
                            own.wait()
                            own.do(v.scalar_tensor_tensor(X[:, :], X0[:, :], 0.2, X0[:, :], ALU.mult, ALU.max))
                    elif n == 2:
                        own.wait()
                        v.tensor_tensor_scan(F[:, :], NBm[:, 0:P], X[:, :], -BIG, ALU.add, ALU.max).then_inc(s_cd, 1)
                    elif n == 3:
                        v.wait_ge(s_ca, h * 5 + 2)
                        v.tensor_copy(Lx[:, :, 0:1], Rm[:, :, G:G + 1])
                        v.tensor_scalar(wn[:, :, 1:G + 1], r3[:, 2, :, :], 1.0, BIG, ALU.subtract, ALU.mult)
                        v.tensor_scalar(cn[:, :, :], r3[:, 1, :, :], 1.0, BIG, ALU.subtract, ALU.mult)
                        own.do(v.tensor_copy(Lx[:, :, 1:G + 1], r3[:, 0, :, :]))
                    elif n == 4:
                        own.wait()
                        own.do(v.tensor_tensor_scan(flat(Rm), flat(wn), flat(Lx), -BIG, ALU.add, ALU.max))
                    elif n == 5:
                        own.wait()
                        v.tensor_tensor(back_row[:, :, :], Rm[:, :, 0:G], cn[:, :, :], ALU.add).then_inc(s_cd, 1)
                    elif n == 6:
                        v.wait_ge(s_cp, h * 6 + 3)
                        own.do(v.tensor_copy(col[:, 0:1], cB[0:HT, 400:401]))
                    elif n == 7:
                        own.wait()
                        own.do(v.tensor_tensor_scan(F[:, :], NBm[:, 0:P], X[:, :], col[:, 0:1], ALU.add, ALU.max))
                    elif n == 8:
                        own.wait()
                        own.do(v.tensor_tensor_scan(B[:, ::-1], NBm[:, 128:0:-1], F[:, ::-1], -BIG, ALU.add, ALU.max))
                    elif n == 9:
                        own.wait()
                        v.tensor_tensor(Y[:, 128:129], col[:, 0:1], B[:, 0:1], ALU.subtract)
                        v.tensor_tensor(Y[:, 0:P], X[:, :], B[:, :], ALU.subtract).then_inc(s_cd, 1)
                    elif n == 10:
                        v.wait_ge(s_ca, h * 5 + 3)
                        v.tensor_tensor_scan(F[:, :], M[:, 0:P], EX[:, 0:P], 0.0, ALU.mult, ALU.add).then_inc(s_cd, 1)
                    elif n == 11:
                        v.wait_ge(s_ca, h * 5 + 4)
                        v.tensor_copy(Ls[:, :, 0:1], Rs[:, :, G:G + 1])
                        v.tensor_tensor(wg[:, :, 1:G + 1], r3[:, 2, :, :], r2[:, 1, :, :], ALU.mult)
                        own.do(v.tensor_copy(Ls[:, :, 1:G + 1], r2[:, 0, :, :]))
                    elif n == 12:
                        own.wait()
                        own.do(v.tensor_tensor_scan(flat(Rs), flat(wg), flat(Ls), 0.0, ALU.mult, ALU.add))
                    elif n == 13:
                        own.wait()
                        v.tensor_tensor(back_row[:, :, :], Rs[:, :, 0:G], r2[:, 1, :, :], ALU.mult).then_inc(s_cd, 1)
                    elif n == 14:
                        v.wait_ge(s_cp, h * 6 + 5)
                        own.do(v.tensor_copy(col[:, 1:2], cB[0:HT, 400:401]))
                    elif n == 15:
                        own.wait()
                        own.do(v.tensor_tensor_scan(F[:, :], M[:, 0:P], EX[:, 0:P], col[:, 1:2], ALU.mult, ALU.add))
                    elif n == 16:
                        own.wait()
                        own.do(v.tensor_tensor_scan(B[:, ::-1], M[:, 128:0:-1], F[:, ::-1], 0.0, ALU.mult, ALU.max))
                    elif n == 17:
                        own.wait()
                        own.do(v.reciprocal(Y[:, 0:P], B[:, :]))
                    elif n == 18:
                        own.wait()
                        v.tensor_scalar(Df[:, :], c.same[0:HT, :], col[:, 1:2], Y[:, 0:1], ALU.mult, ALU.mult)
                        v.tensor_tensor(AL[:, :], EX[:, 0:P], Y[:, 0:P], ALU.mult).then_inc(s_cd, 1)
                    elif gat:
                        v.wait_ge(s_ca, h * 5 + 5)
                        v.tensor_tensor(alpha[:, b, :, :], cA[:, 0:HT].rearrange("p (h g) -> p h g", h=H),
                                        dist[:, b, :].unsqueeze(1).to_broadcast([P, H, G]), ALU.mult).then_inc(s_cd, 1)

                def onehot(g, gs, p):
                    k = gs % RG
                    if p == 0:
                        v.wait_ge(s_fl[k], use(g, gs) * (16 * NL))
                    v.tensor_tensor(S[:, k, 2 * p:2 * p + 2, :], c.iota[:, :].unsqueeze(1).to_broadcast([P, 2, P]),
                                    rel[:, k, 2 * p:2 * p + 2].unsqueeze(2).to_broadcast([P, 2, P]),
                                    ALU.is_equal).then_inc(s_S, 1)

                def destination(g, p):
                    T = g * GP + p
                    wait(v, s_front, T)
                    v.wait_ge(s_qd, T + 1)
                    v.tensor_reduce(edst[:, :].rearrange("p (i h) -> p i h", i=2),
                                    pqd[p % 2][:, 0:2 * DW].rearrange("p (i c h) -> p i h c", i=2, c=3),
                                    AX.X, ALU.add).then_inc(s_dst, 1)

                def products(g, k, p):
                    T = g * GP + p
                    v.wait_ge(s_g[p % R], arrived(g, p, R))
                    if gat:
                        v.wait_ge(s_dst, T + 1)
                        v.tensor_tensor(score[:, k, :, 2 * p:2 * p + 2].rearrange("p h i -> p i h"),
                                        vst[:, k, 2 * p:2 * p + 2, D:D + H],
                                        edst[:, :].rearrange("p (i h) -> p i h", i=2),
                                        ALU.add).then_inc(s_front, 1)
                    else:
                        wait(v, s_score, T)
                        v.wait_ge(s_qd, T + 1)
                        v.tensor_tensor(prod[:, :].rearrange("p (i d) -> p i d", i=2), kv[:, p % R, :, 0:D],
                                        pqd[p % 2][:, :].rearrange("p (i d) -> p i d", i=2),
                                        ALU.mult).then_inc(s_front, 1)

                def reduce(g, k, p):
                    v.wait_ge(s_front, g * GP + p + 1)
                    v.tensor_reduce(score[:, k, :, 2 * p:2 * p + 2].rearrange("p h i -> p i h"),
                                    prod[:, :].rearrange("p (i h o) -> p i h o", i=2, h=H),
                                    AX.X, ALU.add).then_inc(s_score, 1)

                def message(g, gs, p):
                    if p == 0:
                        if gat:
                            v.wait_ge(s_cd, g * CD + CD)
                        else:
                            v.wait_ge(s_ca, g * 5 + 5)
                    v.tensor_tensor(msg[:, p % 2, :].rearrange("p (i h o) -> p i h o", i=2, h=H),
                                    vst[:, gs % VR, 2 * p:2 * p + 2, 0:D].rearrange("p i (h o) -> p i h o", h=H),
                                    alpha[:, gs % VR, :, 2 * p:2 * p + 2].rearrange("p h i -> p i h").unsqueeze(
                                        3).to_broadcast([P, 2, H, Dh]), ALU.mult).then_inc(s_msg, 1)

                first = [None]

                def rescale(g, b, p, i, fresh):
                    V, t = g * GP + p, 2 * p + i
                    if fresh or (p % 2 == 0 and i == 0):
                        first[0] = firsts(DVE_ENG, 2 * V - 2 * (p % 2))
                    n0 = first[0][2 * (p % 2) + i]
                    v.wait_ge(s_add, 2 * V + 2 + i)
                    v.tensor_tensor(acc[:, :, bass.ds(n0, 1)], acc[:, :, bass.ds(n0, 1)],
                                    fac[:, b, :, t:t + 1], ALU.mult).then_inc(s_mul, 1)

                def add(g, b, p, i):
                    V = g * GP + p
                    n0 = first[0][2 * (p % 2) + i]
                    if i == 0:
                        v.wait_ge(s_agg, V + 1)
                    v.wait_ge(s_mul, 2 * V + 1 + i)
                    n = bass.ds(n0, P)
                    v.tensor_tensor(acc[:, :, n], acc[:, :, n],
                                    pag[p % 2][:, i * D:i * D + D].rearrange("p (j r) -> p j r", j=2),
                                    ALU.add).then_inc(s_add, 1)

                for p in range(0 if AHOT else 3):
                    onehot(0, 0, p)

                CH = -(-acc.shape[2] // LAG)

                def step(g, gs):
                    own = Step(v, s_cn, (g - 1) * CN)
                    for p in range(GP):
                        if isinstance(g, int) and g * GP + p < LAG:
                            t = g * GP + p
                            v.memset(acc[:, :, t * CH:min(t * CH + CH, acc.shape[2])], 0.0).then_inc(s_clear, 1)
                        elif isinstance(g, int) and g * GP + p == LAG:
                            v.wait_ge(s_clear, LAG)
                        k, front, chained = gs % VR, gs < NG, 0 < gs <= NG
                        vg, vs, vp, adds = near(g, gs, p, -LAG - 1)
                        vk = vs % VR
                        ug, us, up, sends = near(g, gs, p, -LAG)
                        def work(slot):
                            if chained:
                                for n in DVE_AT.get((p, slot), ()):
                                    chain(n, g - 1, (gs - 1) % VR, own)

                        og, ok, op, ahead = near(g, gs, p, 3)
                        if gat and sends:
                            message(ug, us, up)
                        if front and not gat:
                            products(g, k, p)
                        work(0)
                        if adds:
                            rescale(vg, vk, vp, 0, p == 0)
                        work(1)
                        if front and gat:
                            destination(g, p)
                        if sends and not gat:
                            message(ug, us, up)
                        work(2)
                        if adds:
                            add(vg, vk, vp, 0)
                        if ahead and not AHOT:
                            onehot(og, ok, op)
                        work(3)
                        if adds:
                            rescale(vg, vk, vp, 1, False)
                        work(4)
                        if front:
                            products(g, k, p) if gat else reduce(g, k, p)
                        work(5)
                        if adds:
                            add(vg, vk, vp, 1)
                        work(6)

                run(v, step)


class Constants:

    def __init__(self, nc, m):
        s_c, s_p, s_o = sems(nc, "const", "dve", "pool", "own")
        self.ident = m.sb("ident", [P, P])
        self.iota = m.sb("iota", [P, P])
        self.one = m.sb("one", [P, 2])
        self.rep = m.sb("rep", [G, 8 * G])
        self.same = m.sb("same", [P, G])
        self.heads = {H: m.sb(f"heads{H}", [H * G, 2, P]) for H in (8, 4)}
        ints = m.sb("ints", [P, P], I32)
        with nc.Block() as block:

            @block.vector
            def _(v):
                own = Step(v, s_o)
                v.memset(self.one[:, :], 1.0)
                v.memset(self.ident[:, :], 1.0)
                for H in (8, 4):
                    v.memset(self.heads[H][:, :, :], 1.0)
                v.engine_nop().then_inc(s_c, 1)
                v.wait_ge(s_p, 6)
                v.tensor_copy(self.iota[:, :], ints[:, :])
                for h in range(8):
                    v.tensor_copy(self.rep[:, h * G:h * G + G], self.ident[0:G, 0:G])
                own(v.tensor_reduce(self.same[:, :], self.ident[:, :].rearrange("p (h t) -> p t h", t=G),
                                    AX.X, ALU.add))

            @block.gpsimd
            def _(pool):
                pool.wait_ge(s_c, 1)
                own = Step(pool, s_p)
                own(pool.affine_select(out=self.ident[:, :], in_=self.ident[:, :], compare_op=ALU.is_equal,
                                       fill=0.0, base=0, pattern=[[-1, P]], channel_multiplier=1))
                own(pool.iota(ints[:, :], [[1, P]], base=0, channel_multiplier=0))
                for H in (8, 4):
                    HH, Dh = H // 2, D // H
                    t = self.heads[H][:, :, :].rearrange("p j (a o) -> p j a o", a=HH)
                    own(pool.affine_select(out=t, in_=t, compare_op=ALU.is_ge, fill=0.0, base=0,
                                           pattern=[[-G * HH, 2], [-G, HH], [0, Dh]], channel_multiplier=1))
                    own(pool.affine_select(out=t, in_=t, compare_op=ALU.is_ge, fill=0.0, base=G - 1,
                                           pattern=[[G * HH, 2], [G, HH], [0, Dh]], channel_multiplier=-1))


def add_rows(nc, c, dr, acc, gelu=None):
    NBK, K = (N + P - 1) // P, 7
    NGR = NBK // K
    assert NBK % K == 0 and NGR % 2 == 0
    s_cp, s_t, s_r0, s_r1, s_add, s_st0, s_st1 = sems(
        nc, "rows" if gelu is None else "gelu_rows", "copied", "turned", "rows0", "rows1", "added", "stored0", "stored1")
    s_r, s_st = (s_r0, s_r1), (s_st0, s_st1)
    with Scope(nc, "rows" if gelu is None else "gelu_rows") as m:
        f = m.sb("f", [P, K, 2, P])
        row = m.sb("row", [P, 2, K, D])
        pt = [m.ps(f"pt{k}", [P, 512]) for k in range(K)]
        group = lambda g: dr["x"][bass.ds(g * (K * P), K * P), :].rearrange("(k p) d -> p k d", p=P)
        with nc.Block() as block:

            @block.sync
            def _(sp):
                def load(g, s):
                    sp.dma_start(row[:, s, :, :], group(g)).then_inc(s_r[s], 16)

                def store(g, s):
                    sp.wait_ge(s_add, g * K + 2 * K)
                    sp.dma_start(group(g), row[:, s, :, :]).then_inc(s_st[s], 16)

                for s in range(2):
                    load(s, s)
                with sp.Fori(0, NGR // 2 - 1) as i:
                    for s in range(2):
                        store(2 * i + s, s)
                        sp.wait_ge(s_st[s], i * 16 + 16)
                        load(2 * i + s + 2, s)
                for s in range(2):
                    store(NGR - 2 + s, s)
                for s in range(2):
                    sp.wait_ge(s_st[s], NGR // 2 * 16)

            @block.scalar
            def _(act):
                act.sem_inc(s_t, K)
                with act.Fori(0, NGR) as g:
                    for k in range(K):
                        b = g * K + k
                        act.wait_ge(s_t, b + 1)
                        if gelu is None:
                            t = act.copy(f[:, k, :, :], acc[:, :, bass.ds(b * P, P)])
                        else:
                            for o in range(2):
                                t = act.activation(f[:, k, o, :], acc[:, o, bass.ds(b * P, P)], ACT.Gelu,
                                                   bias=gelu[1][:, o:o + 1], scale=gelu[0][:, o:o + 1])
                        t.then_inc(s_cp, 1)

            @block.tensor
            def _(pe):
                with pe.Fori(0, NGR) as g:
                    for k in range(K):
                        b = g * K + k
                        pe.wait_ge(s_cp, b + 1)
                        pe.wait_ge(s_add, b + 1)
                        for o in range(2):
                            t = pe.transpose(pt[k][:, o * P:o * P + P], f[:, k, o, :], c.ident[:, :])
                        t.then_inc(s_t, 1)

            @block.vector
            def _(v):
                v.sem_inc(s_add, K)
                with v.Fori(0, NGR // 2) as i:
                    for s in range(2):
                        v.wait_ge(s_r[s], i * 16 + 16)
                        for k in range(K):
                            b = (2 * i + s) * K + k
                            v.wait_ge(s_t, b + K + 1)
                            v.tensor_tensor(row[:, s, k, :], row[:, s, k, :], pt[k][:, 0:D], ALU.add).then_inc(s_add, 1)


def graph_norm(nc, c, dr, acc, w_out, b_out, gw, gb, gms):
    CH, SQ = 500, 2500
    NCH, NSQ = N // CH, N // SQ
    (s_w, s_x0, s_x1, s_mm, s_h, s_own, s_mean, s_sq, s_std, s_sc) = sems(
        nc, "gn", "weights", "xT0", "xT1", "product", "h", "dve", "mean", "squares", "std", "scale")
    s_x = (s_x0, s_x1)
    with Scope(nc, "gn") as m:
        wo = m.sb("wo", [P, 2, D])
        vec = m.sb("vec", [P, 4, 2])
        xT = m.sb("xT", [P, 2, 2, CH])
        sums = m.sb("sums", [P, 2, NCH])
        squares = m.sb("squares", [P, 2, NSQ])
        junk = m.sb("junk", [P, SQ])
        st = m.sb("st", [P, 6, 2])
        eps = m.sb("eps", [P, 1])
        product = ExitStack()
        ph = [product.enter_context(nc.psum_tensor(f"gn_ph{i}", [P, 512], F32)) for i in range(4)]
        with nc.Block() as block:

            @block.sync
            def _(sp):
                sp.dma_start(wo[:, :, :], w_out.rearrange("(c p) n -> p c n", p=P)).then_inc(s_w, 16)
                for j, a in enumerate((b_out, gw, gb, gms)):
                    sp.dma_start(vec[:, j, :], a.rearrange("(c p) -> p c", p=P),
                                 allow_slow_non_contiguous=True).then_inc(s_w, 16)
                for s in range(2):
                    sp.dma_start(xT[:, s, :, :], dr["xT"][:, :, s * CH:s * CH + CH]).then_inc(s_x[s], 16)
                with sp.Fori(0, (NCH - 3) // 2) as i:
                    for s in range(2):
                        b = 2 * i + s
                        sp.wait_ge(s_h, 2 * b + 4)
                        sp.dma_start(xT[:, s, :, :], dr["xT"][:, :, bass.ds((b + 2) * CH, CH)]).then_inc(s_x[s], 16)
                sp.wait_ge(s_h, 2 * NCH - 2)
                sp.dma_start(xT[:, 0, :, :], dr["xT"][:, :, (NCH - 1) * CH:NCH * CH]).then_inc(s_x[0], 16)

            @block.tensor
            def _(pe):
                pe.wait_ge(s_w, 80)

                def project(b, s):
                    if not isinstance(b, int):
                        pe.wait_ge(s_h, 2 * b)
                    for o in range(2):
                        for k in range(2):
                            t = pe.matmul(ph[2 * s + o][:, 0:CH], wo[:, k, o * P:o * P + P],
                                          acc[:, k, bass.ds(b * CH, CH)], start=(k == 0), stop=(k == 1))
                    t.then_inc(s_mm, 1)

                project(0, 0)
                with pe.Fori(0, (NCH - 1) // 2) as i:
                    project(2 * i + 1, 1)
                    project(2 * i + 2, 0)

            @block.vector
            def _(v):
                v.memset(eps[:, :], EPS).then_inc(s_sc, 1)
                v.sem_inc(s_h, 2)

                def add(b, s, k):
                    v.wait_ge(s_mm, b + 1)
                    v.wait_ge(s_x[s], k * 16 + 16)
                    for o in range(2):
                        n = bass.ds(b * CH, CH)
                        v.scalar_tensor_tensor(acc[:, o, n], ph[2 * s + o][:, 0:CH], vec[:, 0, o:o + 1],
                                               xT[:, s, o, :], ALU.add, ALU.add).then_inc(s_h, 1)
                        v.wait_ge(s_h, 2 * b + o + 3)
                        v.tensor_reduce(sums[:, o, bass.ds(b, 1)], acc[:, o, n], AX.X, ALU.add).then_inc(s_own, 1)

                v.wait_ge(s_w, 80)
                add(0, 0, 0)
                with v.Fori(0, (NCH - 1) // 2) as i:
                    add(2 * i + 1, 1, i)
                    add(2 * i + 2, 0, i + 1)
                v.wait_ge(s_own, 2 * NCH)
                own = Step(v, s_own, 2 * NCH)
                own(v.tensor_reduce(st[:, 1, :], sums[:, :, :], AX.X, ALU.add))
                v.scalar_tensor_tensor(st[:, 0, :], st[:, 1, :], -1.0 / N, vec[:, 3, :],
                                       ALU.mult, ALU.mult).then_inc(s_mean, 1)
                v.wait_ge(s_sq, 2 * NSQ)
                own(v.tensor_reduce(st[:, 1, :], squares[:, :, :], AX.X, ALU.add))
                v.tensor_scalar(st[:, 2, :], st[:, 1, :], 1.0 / N, None, ALU.mult).then_inc(s_sc, 1)
                v.wait_ge(s_std, 1)
                own(v.reciprocal(st[:, 3, :], st[:, 1, :]))
                own(v.tensor_tensor(st[:, 4, :], st[:, 3, :], vec[:, 1, :], ALU.mult))
                own(v.tensor_tensor(st[:, 5, :], st[:, 4, :], st[:, 0, :], ALU.mult))
                v.tensor_tensor(st[:, 5, :], st[:, 5, :], vec[:, 2, :], ALU.add).then_inc(s_sc, 1)

            @block.scalar
            def _(act):
                act.wait_ge(s_mean, 1)
                for o in range(2):
                    for q in range(NSQ):
                        if o + q:
                            act.wait_ge(s_sq, o * NSQ + q)
                        act.activation(junk[:, :], acc[:, o, q * SQ:q * SQ + SQ], ACT.Square, bias=st[:, 0, o:o + 1],
                                       accum_out=squares[:, o, q:q + 1]).then_inc(s_sq, 1)
                act.wait_ge(s_sc, 2)
                act.activation(st[:, 1, :], st[:, 2, :], ACT.Sqrt, bias=eps[:, 0:1]).then_inc(s_std, 1)

        product.close()
        add_rows(nc, c, dr, acc, gelu=(st[:, 4, :], st[:, 5, :]))


def moe_top2(nc, c, dr, router_w, w1, b1, w2, b2):
    SBW, NSB = 256, NR // 256
    (s_w, s_c, s_x0, s_x1, s_own, s_bn, s_sd, s_ln, s_tp, s_xT, s_lg, s_ex, s_pr, s_cT, s_cS, s_m1, s_h, s_m2,
     s_y, s_yf, s_st0, s_st1, s_b0, s_go) = sems(
        nc, "top2", "weights", "consts", "rows0", "rows1", "dve", "stats", "std", "normed", "turned", "xT",
        "logits", "exp", "probs", "combT", "combS", "hidden_sums", "hidden", "expert_sums", "weighted",
        "started", "stored0", "stored1", "router", "go")
    s_x, s_st = (s_x0, s_x1), (s_st0, s_st1)
    with Scope(nc, "top2") as m:
        rw = m.sb("rw", [P, 2, 8])
        rw8 = m.sb("rw8", [8, D])
        W1 = m.sb("w1", [P, 8, 2, D])
        W2 = m.sb("w2", [P, 8, 2, D])
        B1 = m.sb("b1", [P, 8, 2])
        B2 = m.sb("b2", [8, D])
        eps = m.sb("eps", [P, 1])
        x = m.sb("x", [P, 2, 2, D])
        st = m.sb("st", [P, 2, 6])
        mv = m.sb("mv", [P, 2, 2])
        sd = m.sb("sd", [P, 2, 2])
        ln = m.sb("ln", [P, 2, 2, D])
        xT = m.sb("xT", [P, 2, 2, SBW])
        lg = m.sb("lg", [P, 2, 8])
        pr = m.sb("pr", [P, 2, 8])
        e1 = m.sb("e1", [P, 2, 8])
        k1 = m.sb("k1", [P, 2, 8])
        k2 = m.sb("k2", [P, 2, 8])
        p2 = m.sb("p2", [P, 2, 8])
        i8 = m.sb("i8", [P, 2, 8])
        sc = m.sb("sc", [P, 8, 2])
        comb = m.sb("comb", [P, 2, 2, 8])
        cT = m.sb("cT", [8, 2, 2, P])
        hT = m.sb("hT", [P, 2, 2, SBW])
        y = m.sb("y", [P, 2, 2, D])
        pT = m.ps("pT", [P, 512])
        pr_ = m.ps("pr_", [P, 512])
        ph = [m.ps(f"ph{i}", [P, 512]) for i in range(2)]
        py = [m.ps(f"py{i}", [P, 512]) for i in range(2)]
        pb = m.ps("pb", [P, 512])
        rows = lambda b: dr["x"][bass.ds(b * SBW, SBW), :].rearrange("(k p) d -> p k d", p=P)
        CV = 23

        def run(eng, expert, front, ahead):
            def step(b, s, more):
                own = Step(eng, s_own, (b + 1) * CV)
                for e in range(8):
                    expert(b, s, e, more)
                    if more:
                        for stage in ahead.get(e, ()):
                            front(b + 1, 1 - s, stage, own)

            own = Step(eng, s_own, 0)
            for e in range(8):
                for stage in ahead.get(e, ()):
                    front(0, 0, stage, own)
            expert(-1, 1, 7, True)
            with eng.Fori(0, NSB // 2 - 1) as i:
                for s in range(2):
                    step(2 * i + s, s, True)
            step(NSB - 2, 0, True)
            step(NSB - 1, 1, False)

        def uses(b, s):
            return (b - s) * 8

        def wait(eng, sem, value):
            if not isinstance(value, int) or value > 0:
                eng.wait_ge(sem, value)

        with nc.Block() as block:

            @block.sync
            def _(sp):
                sp.dma_start(rw8[:, :], router_w).then_inc(s_w, 16)
                sp.dma_start(B1[:, :, :], b1.rearrange("e (c p) -> p e c", p=P),
                             allow_slow_non_contiguous=True).then_inc(s_w, 16)
                sp.dma_start(B2[:, :], b2).then_inc(s_w, 16)
                for e in range(8):
                    sp.dma_start(W1[:, e, :, :], w1[e].rearrange("(c p) n -> p c n", p=P)).then_inc(s_w, 16)
                    sp.dma_start(W2[:, e, :, :], w2[e].rearrange("(c p) n -> p c n", p=P)).then_inc(s_w, 16)
                for s in range(2):
                    sp.dma_start(x[:, s, :, :], rows(s)).then_inc(s_x[s], 16)
                    sp.sem_inc(s_st[s], 16)

                def store(b, s):
                    sp.wait_ge(s_y, b * 16 + 18)
                    sp.dma_start(rows(b), y[:, s, :, :]).then_inc(s_st[s], 16)

                with sp.Fori(0, NSB // 2 - 1) as i:
                    for s in range(2):
                        b = 2 * i + s
                        store(b, s)
                        sp.dma_start(x[:, s, :, :], rows(b + 2)).then_inc(s_x[s], 16)
                for s in range(2):
                    store(NSB - 2 + s, s)
                for s in range(2):
                    sp.wait_ge(s_st[s], NSB // 2 * 16 + 16)

            @block.vector
            def _(v):
                v.memset(eps[:, :], EPS).then_inc(s_c, 1)
                v.tensor_scalar(i8[:, 0, :], c.iota[:, 0:8], 8.0, None, ALU.subtract)
                v.tensor_scalar(i8[:, 1, :], c.iota[:, 0:8], 8.0, None, ALU.subtract).then_inc(s_c, 1)
                v.sem_inc(s_y, 2)
                v.wait_ge(s_b0, 1)
                v.tensor_copy(rw[:, :, :].rearrange("p c e -> p (c e)"), pr_[:, 0:16]).then_inc(s_c, 1)

                def front(b, s, stage, own):
                    if stage == 0:
                        statistics(b, s, own)
                    elif stage == 1:
                        normalise(b, s, own)
                    elif stage == 2:
                        logits(b, s, own)
                    elif stage == 3:
                        best_two(b, s, own)
                    elif stage == 4:
                        start(b, s, own)
                    else:
                        biases(b, s, own)
                        assert own.n == CV, own.n

                bc = lambda t: t.unsqueeze(2).to_broadcast([P, 2, 8])

                def statistics(b, s, own):
                    for k in range(2):
                        if k == 0:
                            v.wait_ge(s_x[s], uses(b, s) + 16)
                        own(v.bn_stats(st[:, k, :], x[:, s, k, :]))
                        v.sem_inc(s_go, 1)
                        v.bn_aggr(mv[:, k, :], st[:, k, :]).then_inc(s_bn, 1)

                def normalise(b, s, own):
                    v.wait_ge(s_sd, b + 1)
                    own(v.reciprocal(sd[:, :, 1], sd[:, :, 0]))
                    for k in range(2):
                        own(v.tensor_scalar(ln[:, s, k, :], x[:, s, k, :], mv[:, k, 0:1], sd[:, k, 1:2],
                                            ALU.subtract, ALU.mult))
                    v.sem_inc(s_ln, 1)

                def logits(b, s, own):
                    v.wait_ge(s_lg, b + 1)
                    own(v.tensor_copy(lg[:, :, :].rearrange("p k e -> p (k e)"), pr_[:, 0:16]))
                    own(v.tensor_reduce(sc[:, 0, :], lg[:, :, :], AX.X, ALU.max))
                    v.tensor_tensor(lg[:, :, :], lg[:, :, :], bc(sc[:, 0, :]), ALU.subtract).then_inc(s_pr, 1)

                def best_two(b, s, own):
                    v.wait_ge(s_ex, b + 1)
                    own(v.tensor_reduce(sc[:, 1, :], e1[:, :, :], AX.X, ALU.add))
                    own(v.reciprocal(sc[:, 2, :], sc[:, 1, :]))
                    own(v.tensor_tensor(pr[:, :, :], e1[:, :, :], bc(sc[:, 2, :]), ALU.mult))
                    own(v.tensor_reduce(sc[:, 3, :], pr[:, :, :], AX.X, ALU.max))
                    own(v.tensor_tensor(k1[:, :, :], pr[:, :, :], bc(sc[:, 3, :]), ALU.is_equal))
                    own(v.tensor_tensor(k2[:, :, :], k1[:, :, :], i8[:, :, :], ALU.mult))
                    own(v.tensor_reduce(sc[:, 4, :], k2[:, :, :], AX.X, ALU.min))
                    own(v.tensor_tensor(k1[:, :, :], i8[:, :, :], bc(sc[:, 4, :]), ALU.is_equal))
                    own(v.scalar_tensor_tensor(p2[:, :, :], k1[:, :, :], -4.0, pr[:, :, :], ALU.mult, ALU.add))
                    own(v.tensor_reduce(sc[:, 5, :], p2[:, :, :], AX.X, ALU.max))
                    own(v.tensor_tensor(p2[:, :, :], p2[:, :, :], bc(sc[:, 5, :]), ALU.is_equal))
                    own(v.tensor_tensor(p2[:, :, :], p2[:, :, :], i8[:, :, :], ALU.mult))
                    own(v.tensor_reduce(sc[:, 4, :], p2[:, :, :], AX.X, ALU.min))
                    own(v.tensor_tensor(k2[:, :, :], i8[:, :, :], bc(sc[:, 4, :]), ALU.is_equal))
                    own(v.tensor_tensor(k1[:, :, :], k1[:, :, :], k2[:, :, :], ALU.add))
                    v.tensor_tensor(sc[:, 6, :], sc[:, 3, :], sc[:, 5, :], ALU.add).then_inc(s_pr, 1)
                    v.wait_ge(s_pr, b * 5 + 2)
                    v.tensor_scalar(sc[:, 6, :], sc[:, 6, :], 1e-12, None, ALU.max).then_inc(s_pr, 1)
                    v.wait_ge(s_pr, b * 5 + 3)
                    v.reciprocal(sc[:, 7, :], sc[:, 6, :]).then_inc(s_pr, 1)
                    v.wait_ge(s_pr, b * 5 + 4)
                    own(v.tensor_tensor(k1[:, :, :], k1[:, :, :], bc(sc[:, 7, :]), ALU.mult))
                    v.tensor_tensor(comb[:, s, :, :], k1[:, :, :], pr[:, :, :], ALU.mult).then_inc(s_pr, 1)
                    v.wait_ge(s_pr, b * 5 + 5)

                def start(b, s, own):
                    v.wait_ge(s_cT, 2 * b + 1)
                    v.tensor_copy(cT[:, s, :, :].rearrange("e k p -> e (k p)"), pr_[0:8, 256:512]).then_inc(s_cS, 1)
                    v.wait_ge(s_st[s], uses(b, s) + 16)
                    v.tensor_tensor(y[:, s, :, :], x[:, s, :, :], ln[:, s, :, :], ALU.add).then_inc(s_yf, 1)

                def biases(b, s, own):
                    v.wait_ge(s_yf, 2 * b + 1)
                    v.wait_ge(s_cT, 2 * b + 2)
                    v.tensor_tensor(y[:, s, :, :].rearrange("p k d -> p (k d)"),
                                    y[:, s, :, :].rearrange("p k d -> p (k d)"), pb[:, :], ALU.add).then_inc(s_yf, 1)

                def expert(b, s, e, more):
                    if isinstance(b, int) and b < 0:
                        return
                    for k in range(2):
                        v.wait_ge(s_m2, (b * 8 + e) * 2 + k + 5)
                        if e:
                            v.wait_ge(s_y, (b * 8 + e) * 2 + k + 1)
                        else:
                            v.wait_ge(s_yf, 2 * b + 2)
                        v.scalar_tensor_tensor(y[:, s, k, :], py[k][:, 0:D], comb[:, s, k, e:e + 1],
                                               y[:, s, k, :], ALU.mult, ALU.add).then_inc(s_y, 1)

                run(v, expert, front, {0: (0,), 1: (1,), 3: (2,), 4: (3,), 6: (4,), 7: (5,)})

            @block.scalar
            def _(act):
                act.wait_ge(s_c, 2)
                act.sem_inc(s_h, 2)
                act.sem_inc(s_m2, 4)
                act.wait_ge(s_w, 16 * 19)

                def front(b, s, stage, own):
                    if stage == 0:
                        act.wait_ge(s_bn, 2 * b + 2)
                        act.activation(sd[:, :, 0], mv[:, :, 1], ACT.Sqrt, bias=eps[:, 0:1]).then_inc(s_sd, 1)
                    elif stage == 1:
                        act.wait_ge(s_tp, b + 1)
                        act.copy(xT[:, s, :, :].rearrange("p c (k r) -> p k c r", k=2),
                                 pT[:, :].rearrange("p (k c r) -> p k c r", k=2, c=2)).then_inc(s_xT, 1)
                    else:
                        act.wait_ge(s_pr, b * 5 + 1)
                        act.activation(e1[:, :, :], lg[:, :, :], ACT.Exp).then_inc(s_ex, 1)

                def expert(b, s, e, more):
                    if e == 7 and not more:
                        return
                    n, f = b * 8 + e + 1, (e + 1) % 8
                    act.wait_ge(s_m1, n + 1)
                    act.wait_ge(s_m2, n * 2 + 2)
                    for c_ in range(2):
                        t = act.activation(hT[:, f % 2, c_, :], ph[f % 2][:, c_ * SBW:c_ * SBW + SBW], ACT.Gelu,
                                           bias=B1[:, f, c_:c_ + 1])
                    t.then_inc(s_h, 1)

                run(act, expert, front, {0: (0,), 2: (1,), 3: (2,)})

            @block.tensor
            def _(pe):
                pe.wait_ge(s_w, 16 * 19)
                for k in range(2):
                    t = pe.transpose(pr_[:, k * 8:k * 8 + 8], rw8[:, k * P:k * P + P], c.ident[0:8, 0:8])
                t.then_inc(s_b0, 1)
                pe.wait_ge(s_c, 3)

                def front(b, s, stage, own):
                    if stage == 0:
                        pe.wait_ge(s_ln, b + 1)
                        wait(pe, s_xT, b)
                        for k in range(2):
                            for j in range(2):
                                t = pe.transpose(pT[:, (2 * k + j) * P:(2 * k + j) * P + P],
                                                 ln[:, s, k, j * P:j * P + P], c.ident[:, :])
                        t.then_inc(s_tp, 1)
                    elif stage == 1:
                        pe.wait_ge(s_xT, b + 1)
                        for k in range(2):
                            for j in range(2):
                                t = pe.matmul(pr_[:, k * 8:k * 8 + 8], xT[:, s, j, k * P:k * P + P], rw[:, j, :],
                                              start=(j == 0), stop=(j == 1))
                        t.then_inc(s_lg, 1)
                    elif stage == 2:
                        pe.wait_ge(s_pr, b * 5 + 5)
                        for k in range(2):
                            t = pe.transpose(pr_[0:8, 256 + k * P:256 + k * P + P], comb[:, s, k, :], c.ident[:, :])
                        t.then_inc(s_cT, 1)
                    else:
                        pe.wait_ge(s_cS, b + 1)
                        for k in range(2):
                            t = pe.matmul(pb[:, k * D:k * D + D], cT[:, s, k, :], B2[:, :], start=True, stop=True)
                        t.then_inc(s_cT, 1)

                def expert(b, s, e, more):
                    if e < 7 or more:
                        n, f, fs = b * 8 + e + 1, (e + 1) % 8, s if e < 7 else 1 - s
                        pe.wait_ge(s_h, n + 1)
                        for o in range(2):
                            for j in range(2):
                                t = pe.matmul(ph[f % 2][:, o * SBW:o * SBW + SBW], W1[:, f, j, o * P:o * P + P],
                                              xT[:, fs, j, :], start=(j == 0), stop=(j == 1))
                        t.then_inc(s_m1, 1)
                    if isinstance(b, int) and b < 0:
                        return
                    pe.wait_ge(s_h, b * 8 + e + 3)
                    for k in range(2):
                        pe.wait_ge(s_y, (b * 8 + e) * 2 + k + 1)
                        for j in range(2):
                            t = pe.matmul(py[k][:, 0:D], hT[:, e % 2, j, k * P:k * P + P], W2[:, e, j, :],
                                          start=(j == 0), stop=(j == 1))
                        t.then_inc(s_m2, 1)

                run(pe, expert, front, {2: (0,), 3: (1,), 6: (2,), 7: (3,)})


def moe_switch(nc, c, dr, gate_b, w1, b1, w2, b2, out):
    NBK, FULL, EXP, FF = (N + P - 1) // P, N // P, 8, 1024
    CAP = -(-(5 * N) // (4 * EXP))
    ROWS = -(-CAP // 512) * 512
    SPE = ROWS // 512
    BIGI = float(1 << 20)
    K = 7
    assert NBK % K == 0
    (s_ld, s_c, s_own, s_ex, s_cnt, s_pl, s_zero, s_i, s_pool_go,
     s_w0, s_w1, s_r0, s_r1, s_t, s_tx, s_m1, s_h, s_m2, s_y, s_ys0, s_ys1, s_gi, s_o, s_nn, s_go) = sems(
        nc, "switch", "loaded", "consts", "dve", "exp", "counts", "pool", "zeroed", "index", "pool_go",
        "weights0", "weights1", "buf0", "buf1", "turned", "copied", "hidden_sums", "hidden", "sums", "y",
        "ystored0", "ystored1", "gindex", "result", "nan", "go")
    s_w, s_r, s_ys = (s_w0, s_w1), (s_r0, s_r1), (s_ys0, s_ys1)
    s_l, s_sc, s_g, s_x, s_st = (sems(nc, "switch", *[f"{what}{s}" for s in range(K)])
                                 for what in ("rows", "scattered", "gathered", "x", "stored"))
    with Scope(nc, "switch") as top:
        sslot = top.sb("sslot", [P, NBK], I32)
        gslot = top.sb("gslot", [P, NBK], I32)
        wgt = top.sb("wgt", [P, NBK])
        zero = top.sb("zero", [P, 4 * D])
        flat = lambda t: t[:, :, :].rearrange("p b e -> p (b e)")
        with Scope(nc, "assign") as m:
            lg = m.sb("lg", [P, NBK, 8])
            gb = m.sb("gb", [P, 8])
            i8 = m.sb("i8", [P, 8])
            valid = m.sb("valid", [P, NBK])
            upto = m.sb("upto", [P, P])
            ones = m.sb("ones", [P, P])
            nil = m.sb("nil", [P, NBK])
            ex = m.sb("ex", [P, NBK, 8])
            oh = m.sb("oh", [P, NBK, 8])
            tt = m.sb("tt", [P, NBK, 8])
            tot = m.sb("tot", [P, 8, NBK])
            inc = m.sb("inc", [P, 8, NBK])
            a = m.sb("a", [P, 8, NBK])
            pw = [m.ps(f"pw{i}", [P, 512]) for i in range(2)]
            pt = [m.ps(f"pt{i}", [P, 512]) for i in range(2)]
            HB = NBK // 2
            assert NBK % 2 == 0
            with nc.Block() as block:

                @block.sync
                def _(sp):
                    sp.dma_start(lg[:, :, :], dr["logits"][0:NBK * P, :].rearrange(
                        "(b p) e -> p b e", p=P)).then_inc(s_ld, 16)
                    sp.dma_start(gb[:, :], gate_b.rearrange("(a e) -> a e", a=1).to_broadcast([P, 8])).then_inc(s_ld, 16)

                @block.gpsimd
                def _(pool):
                    pool.wait_ge(s_c, 1)
                    pool.affine_select(out=upto[:, :], in_=upto[:, :], compare_op=ALU.is_ge, fill=0.0, base=0,
                                       pattern=[[1, P]], channel_multiplier=-1)
                    pool.affine_select(out=valid[:, NBK - 1:NBK], in_=valid[:, NBK - 1:NBK], compare_op=ALU.is_ge,
                                       fill=0.0, base=N - FULL * P - 1, pattern=[[0, 1]],
                                       channel_multiplier=-1).then_inc(s_pl, 1)

                @block.scalar
                def _(act):
                    act.wait_ge(s_zero, 1)
                    with act.Fori(0, EXP * ROWS // 512) as i:
                        act.dma_start(dr["buf"][bass.ds(i * 512, 512), :].rearrange("(p r) d -> p (r d)", p=P),
                                      zero[:, :]).then_inc(s_zero, 16)
                    act.wait_ge(s_own, 4)
                    act.activation(ex[:, :, :], tt[:, :, :], ACT.Exp).then_inc(s_ex, 1)

                @block.tensor
                def _(pe):
                    pe.wait_ge(s_cnt, 1)
                    for i in range(2):
                        cols = oh[:, i * HB:i * HB + HB, :].rearrange("p b e -> p (b e)")
                        pe.matmul(pw[i][:, 0:HB * 8], upto[:, :], cols, start=True, stop=True)
                        t = pe.matmul(pt[i][:, 0:HB * 8], ones[:, :], cols, start=True, stop=True)
                    t.then_inc(s_cnt, 1)

                @block.vector
                def _(v):
                    bc = lambda t: t.unsqueeze(2).to_broadcast([P, NBK, 8])
                    row8 = lambda t: t[:, :].unsqueeze(1).to_broadcast([P, NBK, 8])
                    v.memset(zero[:, :], 0.0).then_inc(s_zero, 1)
                    v.memset(upto[:, :], 1.0)
                    v.memset(ones[:, :], 1.0)
                    v.memset(nil[:, :], 0.0)
                    v.memset(valid[:, :], 1.0).then_inc(s_c, 1)
                    own = Step(v, s_own)
                    own(v.tensor_scalar(i8[:, :], c.iota[:, 0:8], 8.0, None, ALU.subtract))
                    v.wait_ge(s_ld, 32)
                    own(v.tensor_tensor(lg[:, :, :], lg[:, :, :], row8(gb), ALU.add))
                    own(v.tensor_reduce(a[:, 0, :], lg[:, :, :], AX.X, ALU.max))
                    own(v.tensor_tensor(tt[:, :, :], lg[:, :, :], bc(a[:, 0, :]), ALU.subtract))
                    v.wait_ge(s_ex, 1)
                    own(v.tensor_reduce(a[:, 1, :], ex[:, :, :], AX.X, ALU.add))
                    own(v.reciprocal(a[:, 2, :], a[:, 1, :]))
                    own(v.tensor_tensor(lg[:, :, :], ex[:, :, :], bc(a[:, 2, :]), ALU.mult))
                    own(v.tensor_reduce(a[:, 3, :], lg[:, :, :], AX.X, ALU.max))
                    own(v.tensor_tensor(tt[:, :, :], lg[:, :, :], bc(a[:, 3, :]), ALU.is_equal))
                    own(v.tensor_tensor(tt[:, :, :], tt[:, :, :], row8(i8), ALU.mult))
                    own(v.tensor_reduce(a[:, 4, :], tt[:, :, :], AX.X, ALU.min))
                    own(v.tensor_tensor(oh[:, :, :], row8(i8), bc(a[:, 4, :]), ALU.is_equal))
                    v.wait_ge(s_pl, 1)
                    v.tensor_tensor(oh[:, :, :], oh[:, :, :], bc(valid[:, :]), ALU.mult).then_inc(s_cnt, 1)
                    v.wait_ge(s_cnt, 2)
                    for i in range(2):
                        own(v.tensor_copy(tot[:, :, i * HB:i * HB + HB].rearrange("p e b -> p b e"),
                                          pt[i][:, 0:HB * 8].rearrange("p (b e) -> p b e", e=8)))
                    for e in range(8):
                        own(v.tensor_tensor_scan(inc[:, e, :], nil[:, :], tot[:, e, :], 0.0, ALU.add, ALU.add))
                    own(v.tensor_tensor(inc[:, :, :], inc[:, :, :], tot[:, :, :], ALU.subtract))
                    for i in range(2):
                        bl = slice(i * HB, i * HB + HB)
                        own(v.tensor_tensor(tt[:, bl, :], inc[:, :, bl].rearrange("p e b -> p b e"),
                                            pw[i][:, 0:HB * 8].rearrange("p (b e) -> p b e", e=8), ALU.add))
                    own(v.tensor_tensor(tt[:, :, :], tt[:, :, :], oh[:, :, :], ALU.mult))
                    own(v.tensor_reduce(a[:, 5, :], tt[:, :, :], AX.X, ALU.add))
                    own(v.tensor_scalar(a[:, 6, :], a[:, 5, :], float(CAP), None, ALU.is_le))
                    own(v.tensor_tensor(a[:, 6, :], a[:, 6, :], valid[:, :], ALU.mult))
                    own(v.tensor_tensor(wgt[:, :], a[:, 3, :], a[:, 6, :], ALU.mult))
                    own(v.tensor_scalar(a[:, 4, :], a[:, 4, :], float(ROWS), 8.0 * ROWS - 1.0, ALU.mult, ALU.add))
                    own(v.tensor_tensor(a[:, 0, :], a[:, 4, :], a[:, 5, :], ALU.add))
                    own(v.tensor_scalar(a[:, 6, :], a[:, 6, :], -BIGI, BIGI, ALU.mult, ALU.add))
                    own(v.tensor_tensor(a[:, 0, :], a[:, 0, :], a[:, 6, :], ALU.add))
                    own(v.tensor_copy(sslot[:, :], a[:, 0, :]))
                    own(v.tensor_scalar(a[:, 5, :], a[:, 5, :], 1.0, float(CAP), ALU.max, ALU.min))
                    own(v.tensor_tensor(a[:, 5, :], a[:, 5, :], a[:, 4, :], ALU.add))
                    own(v.tensor_copy(gslot[:, :], a[:, 5, :]))
                    v.sem_inc(s_i, 1)

        with Scope(nc, "scatter") as m:
            row = m.sb("row", [P, K, D])
            slot = m.sb("slot", [P, K, 2], I32)
            with nc.Block() as block:

                @block.vector
                def _(v):
                    for s in range(K):
                        v.tensor_copy(slot[:, s, 0:1], sslot[:, s:s + 1]).then_inc(s_i, 1)
                    with v.Fori(1, NBK // K) as i:
                        for s in range(K):
                            v.wait_ge(s_sc[s], i * 16)
                            v.tensor_copy(slot[:, s, 0:1], sslot[:, bass.ds(K * i + s, 1)]).then_inc(s_i, 1)

                @block.sync
                def _(sp):
                    for s in range(K):
                        sp.dma_start(row[:, s, :], dr["ln"][s * P:s * P + P, :]).then_inc(s_l[s], 16)
                    with sp.Fori(1, NBK // K) as i:
                        for s in range(K):
                            sp.wait_ge(s_sc[s], i * 16)
                            sp.dma_start(row[:, s, :], dr["ln"][bass.ds((K * i + s) * P, P), :]).then_inc(s_l[s], 16)

                @block.gpsimd
                def _(pool):
                    pool.wait_ge(s_zero, 1 + 16 * (EXP * ROWS // 512))
                    with pool.Fori(0, NBK // K) as i:
                        for s in range(K):
                            pool.wait_ge(s_l[s], i * 16 + 16)
                            pool.wait_ge(s_i, K * i + s + 2)
                            pool.sem_inc(s_pool_go, 1)
                            pool.indirect_dma_start(dr["buf"], IndirectOffsetOnAxis(ap=slot[:, s, 0:1], axis=0),
                                                    row[:, s, :], None, bounds_check=EXP * ROWS - 1,
                                                    oob_is_err=False).then_inc(s_sc[s], 16)
                    for s in range(K):
                        pool.wait_ge(s_sc[s], NBK // K * 16)

        with Scope(nc, "experts") as m:
            W1 = m.sb("w1", [P, 2, 2, FF])
            W2 = m.sb("w2", [P, 2, 8, D])
            B1 = m.sb("b1", [P, 2, 8])
            B2 = m.sb("b2", [P, 2, D])
            row = m.sb("row", [P, 2, 4, D])
            xT = m.sb("xT", [P, 2, 2, 512])
            hT = m.sb("hT", [P, 2, 8, 512])
            y = m.sb("y", [P, 2, 4, D])
            pT = [m.ps(f"pT{i}", [P, 512]) for i in range(2)]
            ph = [m.ps(f"ph{i}", [P, 512]) for i in range(2)]
            py = [m.ps(f"py{i}", [P, 512]) for i in range(2)]
            assert SPE == 4
            NSUP = EXP * SPE
            rows = lambda t, n: dr[t][bass.ds(n * 512, 512), :].rearrange("(k p) d -> p k d", p=P)

            def weights(sp, e, s):
                ex_ = lambda a: a[bass.ds(e, 1)]
                sp.dma_start(W1[:, s, :, :], ex_(w1).rearrange("e (c p) n -> (e p) c n", p=P)).then_inc(s_w[s], 16)
                sp.dma_start(W2[:, s, :, :], ex_(w2).rearrange("e (c p) n -> (e p) c n", p=P)).then_inc(s_w[s], 16)
                sp.dma_start(B1[:, s, :], ex_(b1).rearrange("e (c p) -> (e p) c", p=P),
                             allow_slow_non_contiguous=True).then_inc(s_w[s], 16)
                sp.dma_start(B2[:, s, :], ex_(b2).to_broadcast([P, D])).then_inc(s_w[s], 16)

            with nc.Block() as block:

                @block.sync
                def _(sp):
                    for s in range(K):
                        sp.wait_ge(s_sc[s], NBK // K * 16)
                    for s in range(2):
                        weights(sp, s, s)
                        sp.dma_start(row[:, s, :, :], rows("buf", s)).then_inc(s_r[s], 16)
                        sp.sem_inc(s_ys[s], 16)

                    def pair(i, s, q, load):
                        n = (2 * i + s) * SPE + q
                        if load:
                            sp.wait_ge(s_t, n * 4 + 4)
                            sp.dma_start(row[:, q % 2, :, :], rows("buf", n + 2)).then_inc(s_r[q % 2], 16)
                        sp.wait_ge(s_y, n * 8 + 12)
                        sp.dma_start(rows("ybuf", n), y[:, q % 2, :, :]).then_inc(s_ys[q % 2], 16)

                    with sp.Fori(0, EXP // 2 - 1) as i:
                        for s in range(2):
                            for q in range(SPE):
                                pair(i, s, q, True)
                            weights(sp, 2 * i + s + 2, s)
                    for s in range(2):
                        for q in range(SPE):
                            pair(EXP // 2 - 1, s, q, s * SPE + q < 2 * SPE - 2)
                    for s in range(2):
                        sp.wait_ge(s_ys[s], NSUP // 2 * 16 + 16)

                def loop(eng, body):
                    with eng.Fori(0, EXP // 2) as i:
                        for s in range(2):
                            for q in range(SPE):
                                body(i, s, q, (2 * i + s) * SPE + q)

                @block.tensor
                def _(pe):
                    def body(i, s, q, n):
                        pe.wait_ge(s_r[q % 2], (2 * SPE * i + SPE * s + q - q % 2) * 8 + 16)
                        for k in range(4):
                            pe.wait_ge(s_tx, n * 4 + k + 1)
                            for j in range(2):
                                t = pe.transpose(pT[k % 2][:, j * P:j * P + P], row[:, q % 2, k, j * P:j * P + P],
                                                 c.ident[:, :])
                            t.then_inc(s_t, 1)
                        if q == 0:
                            pe.wait_ge(s_w[s], i * 64 + 64)
                        pe.wait_ge(s_tx, n * 4 + 6)
                        for f in range(8):
                            pe.wait_ge(s_h, n * 8 + f + 1)
                            for j in range(2):
                                t = pe.matmul(ph[f % 2][:, :], W1[:, s, j, f * P:f * P + P], xT[:, q % 2, j, :],
                                              start=(j == 0), stop=(j == 1))
                            t.then_inc(s_m1, 1)
                        for k in range(4):
                            pe.wait_ge(s_y, n * 8 + 2 * k + 2)
                            for f in range(8):
                                if k == 0:
                                    pe.wait_ge(s_h, n * 8 + f + 3)
                                t = pe.matmul(py[k % 2][:, 0:D], hT[:, q % 2, f, k * P:k * P + P], W2[:, s, f, :],
                                              start=(f == 0), stop=(f == 7))
                            t.then_inc(s_m2, 1)

                    loop(pe, body)

                @block.scalar
                def _(act):
                    act.sem_inc(s_tx, 2)
                    act.sem_inc(s_h, 2)

                    def body(i, s, q, n):
                        for k in range(4):
                            act.wait_ge(s_t, n * 4 + k + 1)
                            act.copy(xT[:, q % 2, :, k * P:k * P + P],
                                     pT[k % 2][:, 0:D].rearrange("p (c n) -> p c n", c=2)).then_inc(s_tx, 1)
                        if q == 0:
                            act.wait_ge(s_w[s], i * 64 + 64)
                        for f in range(8):
                            act.wait_ge(s_m1, n * 8 + f + 1)
                            act.activation(hT[:, q % 2, f, :], ph[f % 2][:, :], ACT.Relu,
                                           bias=B1[:, s, f:f + 1]).then_inc(s_h, 1)

                    loop(act, body)

                @block.vector
                def _(v):
                    v.sem_inc(s_y, 4)

                    def body(i, s, q, n):
                        v.wait_ge(s_ys[q % 2], (2 * SPE * i + SPE * s + q - q % 2) * 8 + 16)
                        for k in range(4):
                            v.wait_ge(s_m2, n * 4 + k + 1)
                            if k == 0 and q == 0:
                                v.wait_ge(s_w[s], i * 64 + 64)
                            v.tensor_tensor(y[:, q % 2, k, :], py[k % 2][:, 0:D], B2[:, s, :], ALU.add).then_inc(s_y, 2)

                    loop(v, body)

        with Scope(nc, "combine") as m:
            x = m.sb("x", [P, 2, K, D])
            yg = m.sb("yg", [P, 2, K, D])
            t_ = m.sb("t", [P, 2, K, D])
            bad = m.sb("bad", [P, 3, K * D], U32)
            lim = m.sb("lim", [P, 3, K * D])
            slot = m.sb("slot", [P, 2, K, 2], I32)
            NGR, GR = NBK // K, K * P
            group = lambda ap, g: ap[bass.ds(g * GR, GR), :].rearrange("(k p) d -> p k d", p=P)
            assert NGR % 2 == 0
            with nc.Block() as block:

                @block.sync
                def _(sp):
                    def load(g, s):
                        sp.dma_start(x[:, s, :, :], group(dr["x"], g)).then_inc(s_x[s], 16)

                    for s in range(2):
                        sp.sem_inc(s_st[s], 16)
                        load(s, s)
                    with sp.Fori(0, NGR // 2 - 1) as i:
                        for s in range(2):
                            g = 2 * i + s
                            sp.wait_ge(s_o, g + 1)
                            sp.dma_start(group(out, g), t_[:, s, :, :]).then_inc(s_st[s], 16)
                            load(g + 2, s)
                    sp.wait_ge(s_o, NGR - 1)
                    sp.dma_start(group(out, NGR - 2), t_[:, 0, :, :]).then_inc(s_st[0], 16)
                    sp.wait_ge(s_o, NGR)
                    r0, whole = (NGR - 1) * GR, FULL % K
                    sp.dma_start(out[r0:r0 + whole * P, :].rearrange("(k p) d -> p k d", p=P),
                                 t_[:, 1, 0:whole, :]).then_inc(s_st[1], 16)
                    sp.dma_start(out[FULL * P:N, :], t_[0:N - FULL * P, 1, whole, :]).then_inc(s_st[1], 16)
                    sp.wait_ge(s_st[0], NGR // 2 * 16 + 16)
                    sp.wait_ge(s_st[1], NGR // 2 * 16 + 32)

                @block.gpsimd
                def _(pool):
                    with pool.Fori(0, NGR // 2) as i:
                        for s in range(2):
                            pool.wait_ge(s_gi, 2 * i + s + 1)
                            pool.sem_inc(s_pool_go, 1)
                            for k in range(K):
                                pool.indirect_dma_start(yg[:, s, k, :], None, dr["ybuf"], IndirectOffsetOnAxis(
                                    ap=slot[:, s, k, 0:1], axis=0)).then_inc(s_g[s], 16)

                @block.vector
                def _(v):
                    for j, value in enumerate((0.0, 1e4, -1e4)):
                        t = v.memset(lim[:, j, :], value)
                    t.then_inc(s_nn, 1)
                    v.wait_ge(s_nn, 1)
                    for s in range(2):
                        v.tensor_copy(slot[:, s, :, 0], gslot[:, s * K:s * K + K]).then_inc(s_gi, 1)

                    def body(i, s, g, last=False):
                        own = Step(v, s_nn, g * 6 + 1)
                        t = t_[:, s, :, :].rearrange("p k d -> p (k d)")
                        v.wait_ge(s_g[s], i * (16 * K) + 16 * K)
                        v.wait_ge(s_st[s], i * 16 + 16)
                        own(v.tensor_tensor(t_[:, s, :, :], yg[:, s, :, :], wgt[:, bass.ds(g * K, K)].unsqueeze(
                            2).to_broadcast([P, K, D]), ALU.mult))
                        if not last:
                            v.tensor_copy(slot[:, s, :, 0], gslot[:, bass.ds(g * K + 2 * K, K)]).then_inc(s_gi, 1)
                        v.tensor_tensor(bad[:, 0, :], t, t, ALU.not_equal)
                        v.tensor_scalar(bad[:, 1, :], t, 3.4028235e38, None, ALU.is_gt)
                        own(v.tensor_scalar(bad[:, 2, :], t, -3.4028235e38, None, ALU.is_lt))
                        for j in range(3):
                            v.sem_inc(s_go, 1)
                            own(v.copy_predicated(t, bad[:, j, :], lim[:, j, :]))
                        v.wait_ge(s_x[s], i * 16 + 16)
                        own(v.tensor_tensor(t_[:, s, :, :], t_[:, s, :, :], x[:, s, :, :], ALU.add))
                        v.sem_inc(s_o, 1)

                    with v.Fori(0, NGR // 2 - 1) as i:
                        for s in range(2):
                            body(i, s, 2 * i + s)
                    for s in range(2):
                        body(NGR // 2 - 1, s, NGR - 2 + s, True)


def run_phase(nc, f, *args, **kw):
    before = set(nc.free_semaphores)
    f(nc, *args, **kw)
    used = sorted(before - set(nc.free_semaphores))
    nc.clear_and_free_semaphores(used)
    nc.all_engine_barrier()


def graph_program(nc, a, out):
    phase = lambda f, *args, **kw: run_phase(nc, f, *args, **kw)
    dram = lambda name, shape, dt=F32: nc.dram_tensor(name, shape, dt).ap()
    dr = dict(x=dram("xs", (NR, D)), src=dram("srcp", (1, NE), I32), dst=dram("dstp", (1, NE + 1), I32),
              dist=dram("distp", (1, NE)), mask=dram("mask", (NT, MW)), d0=dram("d0", (NT, 1), I32),
              srcT=dram("srcT", (P, NT + G), I32), relT=dram("relT", (P, NT + G)), distT=dram("distT", (P, NT)),
              q=dram("q", (NR, D)), kv=dram("kv", (NR, 2 * D)), xT=dram("xT", (P, 2, NR)),
              ft=dram("ft", (NR, 260)), ed=dram("ed", (NR, 4)), ed3=dram("ed3", (NR, 12), BF16), logits=dram("logits", (NR, 8)),
              ln=dram("ln", (NR, D)), buf=dram("buf", (8 * 2048, D)), ybuf=dram("ybuf", (8 * 2048, D)))
    NA = N + P + 12
    with Scope(nc, "all") as m:
        c = Constants(nc, m)
        phase(prepare_edges, c.ident, a["x"], a["src"], a["dst"], a["edge_attr3_1x1"], dr)
        phase(node_tables, c.ident, "qkv", dr["x"],
                    [(0, a["L0_gnn_WQ"]), (D, a["L0_gnn_WK"]), (2 * D, a["L0_gnn_WV"])], 3 * D,
                    [(dr["q"], 0, 0, D), (dr["kv"], 0, D, 2 * D)], xT_out=dr["xT"])
        with Scope(nc, "sum0") as s:
            acc = s.sb("acc", [P, 2, NA])
            phase(edge_phase, "att", c, dr, acc, 8, float(np.float32(1 / np.sqrt(np.float32(D // 8)))),
                       dr["kv"], dr["q"], None)
            phase(graph_norm, c, dr, acc, a["L0_gnn_W_out"], a["L0_gnn_b_out"], a["L0_gnn_gn_weight"],
                       a["L0_gnn_gn_bias"], a["L0_gnn_gn_mean_scale"])
        phase(moe_top2, c, dr, a["L0_ffn_router_w"], a["L0_ffn_w1"], a["L0_ffn_b1"], a["L0_ffn_w2"], a["L0_ffn_b2"])
        phase(node_tables, c.ident, "gat", dr["x"], [(0, a["L1_gnn_W"])], 264,
                    [(dr["ft"], 0, 0, 260), (dr["ed"], 0, 260, 4)],
                    attention=(a["L1_gnn_w_att_src"], a["L1_gnn_w_att_dst"]))
        phase(split_rows, dr, dr["ed"], dr["ed3"])
        with Scope(nc, "sum1") as s:
            acc = s.sb("acc", [P, 2, NA])
            phase(edge_phase, "gat_att", c, dr, acc, 4, 1.0, dr["ft"], dr["ed3"], dr["distT"])
            phase(add_rows, c, dr, acc)
        phase(node_tables, c.ident, "gate_ln", dr["x"], [(0, a["L1_ffn_gate_w"])], 8,
                    [(dr["logits"], 0, 0, 8)], ln_out=dr["ln"])
        moe_switch(nc, c, dr, a["L1_ffn_gate_b"], a["L1_ffn_w1"], a["L1_ffn_b1"], a["L1_ffn_w2"],
                   a["L1_ffn_b2"], out)


_NAMES = ["x", "src", "dst", "edge_attr3_1x1", "L0_gnn_WQ", "L0_gnn_WK", "L0_gnn_WV", "L0_gnn_W_out", "L0_gnn_b_out",
          "L0_gnn_gn_weight", "L0_gnn_gn_bias", "L0_gnn_gn_mean_scale", "L0_ffn_router_w", "L0_ffn_w1", "L0_ffn_b1",
          "L0_ffn_w2", "L0_ffn_b2", "L1_gnn_W", "L1_gnn_w_att_src", "L1_gnn_w_att_dst", "L1_ffn_gate_w",
          "L1_ffn_gate_b", "L1_ffn_w1", "L1_ffn_b1", "L1_ffn_w2", "L1_ffn_b2"]


def kernel(**inputs):
    import numpy as _np
    import concourse.bacc as _bacc
    from concourse import mybir as _mybir
    from concourse.bass_utils import run_bass_kernel_spmd as _run

    nc = _bacc.Bacc("TRN2", target_bir_lowering=False, num_devices=1)
    arrays, aps = {}, {}
    for name in _NAMES:
        a = _np.ascontiguousarray(inputs[name])
        arrays[f"in_{name}_dram"] = a
        aps[name] = nc.dram_tensor(f"in_{name}_dram", a.shape, _mybir.dt.from_np(a.dtype), kind="ExternalInput").ap()
    out = nc.dram_tensor("out_0_dram", (N, D), F32, kind="ExternalOutput").ap()
    graph_program(nc, aps, out)
    r = _run(nc, [arrays], core_ids=[0])
    return r.results[0]["out_0_dram"]
```
